# Optimizing a Trainium2 kernel written in Bass

```python
import numpy as np
import jax
import jax.numpy as jnp

def _softmax(x, axis=-1):
    return jax.nn.softmax(x, axis=axis)

def _gelu(x):
    return jax.nn.gelu(x, approximate=True)

def _silu(x):
    return jax.nn.silu(x)

def _sigmoid(x):
    return jax.nn.sigmoid(x)

def _layernorm(x, axis=-1, eps=1e-05):
    m = jnp.mean(x, axis=axis, keepdims=True)
    v = jnp.var(x, axis=axis, keepdims=True)
    return (x - m) / jnp.sqrt(v + eps)

def _scatter_add(tgt, idx, src, axis=0):
    return tgt.at[idx].add(src)

def _segment_sum(src, seg, n):
    return jax.ops.segment_sum(src, seg, n)
kernel_name = 'mk_gnn_resnorm_d2_gnn_r64_2d49c6'

def setup_inputs(seed: int=0):
    np.random.seed(seed)
    _w = jnp.asarray

    def _rec_inputs():
        import jax
        import jax.numpy as jnp
        _gk = jax.random.key(seed)
        x = -0.000202 + 1 * jax.random.normal(jax.random.fold_in(_gk, 1), (50000, 128), jnp.float32)
        src = jax.random.randint(jax.random.fold_in(_gk, 2), (12500,), 0, 50000, jnp.int32)
        dst = jax.random.randint(jax.random.fold_in(_gk, 3), (12500,), 0, 50000, jnp.int32)
        _o = jnp.argsort(dst, stable=True)
        src = src[_o]
        dst = dst[_o]
        edge_attr_2 = -0.000414295 + 0.999828 * jax.random.normal(jax.random.fold_in(_gk, 11), (12500, 2), jnp.float32)
        edge_type_4 = jax.random.randint(jax.random.fold_in(_gk, 13), (12500,), 0, 4, jnp.int32)
        return (x, src, dst, edge_attr_2, edge_type_4)
    x, src, dst, edge_attr_2, edge_type_4 = _rec_inputs()

    def _L0_gnn_setup():
        import jax, jax.numpy as jnp
        import numpy as np
        N = 50000
        E = 12500
        IN = 128
        OUT = 128
        R = 4
        H = 8
        D = OUT // H
        NEG_SLOPE = 0.2

        def _hgnn_forward(node_inp, edge_index, edge_type, W_rel, att_src_rel, att_dst_rel, bias_rel, W_self, W_cross, att_src_lang, att_dst_lang, bias_lang):
            src, dst = (edge_index[0], edge_index[1])

            def rel_gat(W, a_s, a_d, b, mask):
                x = (node_inp @ W).reshape(N, H, D)
                es = jnp.einsum('nhd,hd->nh', x, a_s)
                ed = jnp.einsum('nhd,hd->nh', x, a_d)
                logit = jax.nn.leaky_relu(es[src] + ed[dst], NEG_SLOPE)
                logit = jnp.where(mask[:, None], logit, -1e+30)
                mx = jax.ops.segment_max(logit, dst, num_segments=N)
                mx = jnp.maximum(mx, -1e+30)
                p = jnp.exp(logit - mx[dst]) * mask[:, None]
                den = jax.ops.segment_sum(p, dst, num_segments=N)
                alpha = p / jnp.where(den > 0, den, 1.0)[dst]
                msg = alpha[..., None] * x[src]
                out = jax.ops.segment_sum(msg, dst, num_segments=N)
                tmask = jax.ops.segment_sum(mask.astype(jnp.float32), dst, num_segments=N) > 0
                return (out.reshape(N, OUT) + b, tmask)
            rel_masks = edge_type[None, :] == jnp.arange(R)[:, None]
            rel_out, tmask = jax.vmap(rel_gat)(W_rel, att_src_rel, att_dst_rel, bias_rel, rel_masks)
            h = jax.nn.gelu(rel_out, approximate=False) @ W_cross
            S = node_inp @ W_self
            ent = jnp.concatenate([S[None], h], axis=0).reshape(R + 1, N, H, D)
            valid = jnp.concatenate([jnp.ones((1, N), bool), tmask], axis=0)
            ls = jnp.einsum('knhd,hd->knh', ent, att_src_lang)
            ld = jnp.einsum('nhd,hd->nh', ent[0], att_dst_lang)
            logit = jax.nn.leaky_relu(ls + ld[None], NEG_SLOPE)
            logit = jnp.where(valid[..., None], logit, -jnp.inf)
            alpha = jax.nn.softmax(logit, axis=0)
            out = jnp.einsum('knh,knhd->nhd', alpha, ent).reshape(N, OUT)
            return out + bias_lang
        key = jax.random.key(seed)
        ks = jax.random.split(key, 12)
        s = 0.05
        return {'node_inp': jax.random.normal(ks[0], (N, IN), dtype=jnp.float32), 'edge_index': jax.random.randint(ks[1], (2, E), 0, N), 'edge_type': jax.random.randint(ks[2], (E,), 0, R), 'W_rel': jax.random.normal(ks[3], (R, IN, OUT), dtype=jnp.float32) * s, 'att_src_rel': jax.random.normal(ks[4], (R, H, D), dtype=jnp.float32) * s, 'att_dst_rel': jax.random.normal(ks[5], (R, H, D), dtype=jnp.float32) * s, 'bias_rel': jax.random.normal(ks[6], (R, OUT), dtype=jnp.float32) * s, 'W_self': jax.random.normal(ks[7], (IN, OUT), dtype=jnp.float32) * s, 'W_cross': jax.random.normal(ks[8], (OUT, OUT), dtype=jnp.float32) * s, 'att_src_lang': jax.random.normal(ks[9], (H, D), dtype=jnp.float32) * s, 'att_dst_lang': jax.random.normal(ks[10], (H, D), dtype=jnp.float32) * s, 'bias_lang': jax.random.normal(ks[11], (OUT,), dtype=jnp.float32) * s}
    _L0_gnn_all = _L0_gnn_setup()
    _L0_gnn_in = {k: v for k, v in _L0_gnn_all.items() if k in ('W_rel', 'att_src_rel', 'att_dst_rel', 'bias_rel', 'W_self', 'W_cross', 'att_src_lang', 'att_dst_lang', 'bias_lang')}
    del _L0_gnn_all

    def _L1_gnn_setup():
        import jax, jax.numpy as jnp
        import numpy as np
        N_NODES = 50000
        N_EDGES = 12500
        IN_DIM = 128
        OUT_DIM = 128
        EDGE_DIM = 2
        LN_EPS = 1e-05
        key = jax.random.key(seed)
        ks = jax.random.split(key, 8)
        s = lambda fan_in: 1.0 / np.sqrt(fan_in)
        x = jax.random.normal(ks[0], (N_NODES, IN_DIM), dtype=jnp.float32)
        edge_attr = jax.random.normal(ks[1], (N_EDGES, EDGE_DIM), dtype=jnp.float32)
        mW1 = jax.random.normal(ks[2], (2 * IN_DIM + EDGE_DIM, OUT_DIM), dtype=jnp.float32) * s(2 * IN_DIM + EDGE_DIM)
        mb1 = jnp.zeros((OUT_DIM,), jnp.float32)
        mW2 = jax.random.normal(ks[3], (OUT_DIM, OUT_DIM), dtype=jnp.float32) * s(OUT_DIM)
        mb2 = jnp.zeros((OUT_DIM,), jnp.float32)
        uW1 = jax.random.normal(ks[4], (IN_DIM + OUT_DIM, OUT_DIM), dtype=jnp.float32) * s(IN_DIM + OUT_DIM)
        ub1 = jnp.zeros((OUT_DIM,), jnp.float32)
        uW2 = jax.random.normal(ks[5], (OUT_DIM, OUT_DIM), dtype=jnp.float32) * s(OUT_DIM)
        ub2 = jnp.zeros((OUT_DIM,), jnp.float32)
        gamma = jnp.ones((OUT_DIM,), jnp.float32)
        beta = jnp.zeros((OUT_DIM,), jnp.float32)
        edge_index = jax.random.randint(ks[6], (2, N_EDGES), 0, N_NODES, dtype=jnp.int64 if jax.config.jax_enable_x64 else jnp.int32)
        return {'x': x, 'edge_attr': edge_attr, 'mW1': mW1, 'mb1': mb1, 'mW2': mW2, 'mb2': mb2, 'uW1': uW1, 'ub1': ub1, 'uW2': uW2, 'ub2': ub2, 'gamma': gamma, 'beta': beta, 'edge_index': edge_index}
    _L1_gnn_all = _L1_gnn_setup()
    _L1_gnn_in = {k: v for k, v in _L1_gnn_all.items() if k in ('mW1', 'mb1', 'mW2', 'mb2', 'uW1', 'ub1', 'uW2', 'ub2', 'gamma', 'beta')}
    del _L1_gnn_all
    return {'x': x, 'src': src, 'dst': dst, 'edge_attr_2': edge_attr_2, 'edge_type_4': edge_type_4, 'L0_gnn_W_rel': _L0_gnn_in['W_rel'], 'L0_gnn_att_src_rel': _L0_gnn_in['att_src_rel'], 'L0_gnn_att_dst_rel': _L0_gnn_in['att_dst_rel'], 'L0_gnn_bias_rel': _L0_gnn_in['bias_rel'], 'L0_gnn_W_self': _L0_gnn_in['W_self'], 'L0_gnn_W_cross': _L0_gnn_in['W_cross'], 'L0_gnn_att_src_lang': _L0_gnn_in['att_src_lang'], 'L0_gnn_att_dst_lang': _L0_gnn_in['att_dst_lang'], 'L0_gnn_bias_lang': _L0_gnn_in['bias_lang'], 'L1_gnn_mW1': _L1_gnn_in['mW1'], 'L1_gnn_mb1': _L1_gnn_in['mb1'], 'L1_gnn_mW2': _L1_gnn_in['mW2'], 'L1_gnn_mb2': _L1_gnn_in['mb2'], 'L1_gnn_uW1': _L1_gnn_in['uW1'], 'L1_gnn_ub1': _L1_gnn_in['ub1'], 'L1_gnn_uW2': _L1_gnn_in['uW2'], 'L1_gnn_ub2': _L1_gnn_in['ub2'], 'L1_gnn_gamma': _L1_gnn_in['gamma'], 'L1_gnn_beta': _L1_gnn_in['beta']}

def reference(x, src, dst, edge_attr_2, edge_type_4, L0_gnn_W_rel, L0_gnn_att_src_rel, L0_gnn_att_dst_rel, L0_gnn_bias_rel, L0_gnn_W_self, L0_gnn_W_cross, L0_gnn_att_src_lang, L0_gnn_att_dst_lang, L0_gnn_bias_lang, L1_gnn_mW1, L1_gnn_mb1, L1_gnn_mW2, L1_gnn_mb2, L1_gnn_uW1, L1_gnn_ub1, L1_gnn_uW2, L1_gnn_ub2, L1_gnn_gamma, L1_gnn_beta):
    import jax
    import jax.numpy as jnp

    def _L0_gnn_ref(node_inp, edge_index, edge_type, W_rel, att_src_rel, att_dst_rel, bias_rel, W_self, W_cross, att_src_lang, att_dst_lang, bias_lang):
        import jax, jax.numpy as jnp
        import numpy as np
        N = 50000
        E = 12500
        IN = 128
        OUT = 128
        R = 4
        H = 8
        D = OUT // H
        NEG_SLOPE = 0.2

        def _hgnn_forward(node_inp, edge_index, edge_type, W_rel, att_src_rel, att_dst_rel, bias_rel, W_self, W_cross, att_src_lang, att_dst_lang, bias_lang):
            src, dst = (edge_index[0], edge_index[1])

            def rel_gat(W, a_s, a_d, b, mask):
                x = (node_inp @ W).reshape(N, H, D)
                es = jnp.einsum('nhd,hd->nh', x, a_s)
                ed = jnp.einsum('nhd,hd->nh', x, a_d)
                logit = jax.nn.leaky_relu(es[src] + ed[dst], NEG_SLOPE)
                logit = jnp.where(mask[:, None], logit, -1e+30)
                mx = jax.ops.segment_max(logit, dst, num_segments=N)
                mx = jnp.maximum(mx, -1e+30)
                p = jnp.exp(logit - mx[dst]) * mask[:, None]
                den = jax.ops.segment_sum(p, dst, num_segments=N)
                alpha = p / jnp.where(den > 0, den, 1.0)[dst]
                msg = alpha[..., None] * x[src]
                out = jax.ops.segment_sum(msg, dst, num_segments=N)
                tmask = jax.ops.segment_sum(mask.astype(jnp.float32), dst, num_segments=N) > 0
                return (out.reshape(N, OUT) + b, tmask)
            rel_masks = edge_type[None, :] == jnp.arange(R)[:, None]
            rel_out, tmask = jax.vmap(rel_gat)(W_rel, att_src_rel, att_dst_rel, bias_rel, rel_masks)
            h = jax.nn.gelu(rel_out, approximate=False) @ W_cross
            S = node_inp @ W_self
            ent = jnp.concatenate([S[None], h], axis=0).reshape(R + 1, N, H, D)
            valid = jnp.concatenate([jnp.ones((1, N), bool), tmask], axis=0)
            ls = jnp.einsum('knhd,hd->knh', ent, att_src_lang)
            ld = jnp.einsum('nhd,hd->nh', ent[0], att_dst_lang)
            logit = jax.nn.leaky_relu(ls + ld[None], NEG_SLOPE)
            logit = jnp.where(valid[..., None], logit, -jnp.inf)
            alpha = jax.nn.softmax(logit, axis=0)
            out = jnp.einsum('knh,knhd->nhd', alpha, ent).reshape(N, OUT)
            return out + bias_lang
        return _hgnn_forward(node_inp, edge_index, edge_type, W_rel, att_src_rel, att_dst_rel, bias_rel, W_self, W_cross, att_src_lang, att_dst_lang, bias_lang)

    def _L1_gnn_ref(x, edge_attr, mW1, mb1, mW2, mb2, uW1, ub1, uW2, ub2, gamma, beta, edge_index):
        import jax, jax.numpy as jnp
        import numpy as np
        N_NODES = 50000
        N_EDGES = 12500
        IN_DIM = 128
        OUT_DIM = 128
        EDGE_DIM = 2
        LN_EPS = 1e-05
        num_nodes = x.shape[0]
        src, dst = (edge_index[0], edge_index[1])
        msg_in = jnp.concatenate([x[src], x[dst], edge_attr], axis=-1)
        msgs = jnp.maximum(msg_in @ mW1 + mb1, 0.0) @ mW2 + mb2
        agg = jax.ops.segment_sum(msgs, dst, num_segments=num_nodes)
        cnt = jax.ops.segment_sum(jnp.ones((dst.shape[0],), x.dtype), dst, num_segments=num_nodes)
        agg = agg / jnp.clip(cnt, 1.0)[:, None]
        upd_in = jnp.concatenate([x, agg], axis=-1)
        upd = jnp.maximum(upd_in @ uW1 + ub1, 0.0) @ uW2 + ub2
        upd = upd + x
        mu = jnp.mean(upd, axis=-1, keepdims=True)
        var = jnp.mean(jnp.square(upd - mu), axis=-1, keepdims=True)
        return (upd - mu) * jax.lax.rsqrt(var + LN_EPS) * gamma + beta
    edge_index = jnp.stack([src, dst])
    x = _layernorm(x + _L0_gnn_ref(x, edge_index, edge_type_4, L0_gnn_W_rel, L0_gnn_att_src_rel, L0_gnn_att_dst_rel, L0_gnn_bias_rel, L0_gnn_W_self, L0_gnn_W_cross, L0_gnn_att_src_lang, L0_gnn_att_dst_lang, L0_gnn_bias_lang), axis=-1)
    x = _layernorm(x + _L1_gnn_ref(x, edge_attr_2, L1_gnn_mW1, L1_gnn_mb1, L1_gnn_mW2, L1_gnn_mb2, L1_gnn_uW1, L1_gnn_ub1, L1_gnn_uW2, L1_gnn_ub2, L1_gnn_gamma, L1_gnn_beta, edge_index), axis=-1)
    return x

_drawn_inputs = setup_inputs


def setup_inputs(seed=0):
    import zlib

    import numpy as np

    out = dict(_drawn_inputs(seed))
    spreads = {'L1_gnn_mb1': (0.0, 0.8),
     'L1_gnn_mb2': (0.0, 0.8),
     'L1_gnn_ub1': (0.0, 0.1),
     'L1_gnn_ub2': (0.0, 0.1),
     'L1_gnn_gamma': (1.0, 0.2),
     'L1_gnn_beta': (0.0, 0.1)}
    factors = {'edge_attr_2': 8.0,
     'L0_gnn_att_src_rel': 64.0,
     'L0_gnn_att_dst_rel': 64.0,
     'L0_gnn_bias_rel': 8.0,
     'L0_gnn_att_src_lang': 8.0,
     'L0_gnn_att_dst_lang': 27.088}
    for name, (base, spread) in spreads.items():
        noise = np.random.default_rng([zlib.crc32(name.encode()), seed]).standard_normal(out[name].shape)
        drawn = base * np.exp(spread * noise) if base else spread * noise
        out[name] = jnp.asarray(drawn.astype(out[name].dtype))
    for name, factor in factors.items():
        out[name] = (out[name] * factor).astype(out[name].dtype)
    return out
```

```python
from contextlib import ExitStack
from collections import namedtuple

import concourse.bass as bass
from concourse import mybir

P = 128
QUAD = 4
F32 = mybir.dt.float32
BF16 = mybir.dt.bfloat16
I32 = mybir.dt.int32
ALU = mybir.AluOpType
ACT = mybir.ActivationFunctionType
AX_X = mybir.AxisListType.X
LN_EPS = 1e-5
SLOPE = 0.2
NEG = -1e30

Group = namedtuple("Group", "n turn slot real")


def need(eng, sem, value):
    if not isinstance(value, int) or value > 0:
        eng.wait_ge(sem, value)


def behind(turn, k, unroll, offset, total, first=0):
    t, slot = turn + (k - offset) // unroll, (k - offset) % unroll
    n = unroll * t + slot + first
    real = 0 <= n < total if isinstance(n, int) else True
    return Group(n, t, slot, real)


def split(v):
    return v.rearrange("p (j f) -> p j f", j=QUAD)


def build(nc, x, src, dst, edge_attr, edge_type, W_rel, a_src_rel, a_dst_rel, b_rel, W_self, W_cross,
          a_src_lang, a_dst_lang, b_lang, mW1, mb1, mW2, mb2, uW1, ub1, uW2, ub2, gamma, beta, out):
    N, F = x.shape
    E = src.shape[0]
    R, H, D = a_src_rel.shape
    RH = R * H
    K5 = R + 1
    EB = F + H
    GROUP = QUAD * P
    SUPER = 2 * GROUP
    SUPERS = -(-N // SUPER)
    GROUPS = 2 * SUPERS
    TAIL = N - SUPER
    SKIP = ((SUPERS - 1) * SUPER - TAIL) // 8
    BLOCKS = P // RH
    BT = -(-E // (P * BLOCKS))
    TILES = BLOCKS * BT
    EP = TILES * P
    EG = TILES // QUAD
    BE = BT * P
    FULL = E // P
    REST = E - FULL * P
    assert F == P and H * D == F and RH * BLOCKS == P and TILES % QUAD == 0 and TILES <= P
    assert SUPERS == 2 * (EG - 1) + 1 and N < 2 ** 24 and ((SUPERS - 1) * SUPER - TAIL) % 8 == 0

    x1_dram = nc.dram_tensor("x1_rows", (N, F), F32, kind="Internal").ap()
    same_dram = nc.dram_tensor("same_run", (EP,), F32, kind="Internal").ap()
    last_dram = nc.dram_tensor("last_of_run", (EP,), F32, kind="Internal").ap()
    attr_dram = nc.dram_tensor("attr_t", (2, EP), F32, kind="Internal").ap()
    rcnt_dram = nc.dram_tensor("inverse_count", (BLOCKS, BE), F32, kind="Internal").ap()

    whole = ExitStack()
    with whole:
        def sb(name, shape, dt=F32, ctx=whole):
            return ctx.enter_context(nc.sbuf_tensor(name, shape, dt))

        def sem(name):
            return whole.enter_context(nc.semaphore(name))

        bank = [whole.enter_context(nc.psum_tensor(f"bank{i}", [P, 512], F32)) for i in range(8)]

        ident = sb("ident", [P, P])
        w_self_id = sb("w_self_id", [P, F])
        w_node = sb("w_node", [P, 2 * EB])
        w_rel = sb("w_rel", [P, R * F])
        w_log_s = sb("w_log_s", [P, RH])
        w_log_d = sb("w_log_d", [P, RH])
        w_cross = sb("w_cross", [P, EB])
        w_m1s = sb("w_m1s", [P, F])
        w_m1d = sb("w_m1d", [P, F])
        w_m1a = sb("w_m1a", [2, F])
        w_u1x = sb("w_u1x", [P, F])
        w_u1m = sb("w_u1m", [P, F])
        w_u2 = sb("w_u2", [P, F])
        rel_bias = sb("rel_bias", [P, R])
        m1_bias = sb("m1_bias", [P, 1])
        u1_bias = sb("u1_bias", [P, 1])
        u1m_bias = sb("u1m_bias", [P, 1])
        gamma_b = sb("gamma_b", [P, F])
        beta_b = sb("beta_b", [P, F])
        eps_col = sb("eps_col", [P, 1])
        ones_b = sb("ones_b", [P, P], BF16)
        lang3 = sb("lang3", [P, F], BF16)
        u2b3 = sb("u2b3", [P, F], BF16)
        idx_src = sb("idx_src", [P, TILES], I32)
        idx_dst = sb("idx_dst", [P, TILES], I32)
        idx_put = sb("idx_put", [P, TILES], I32)
        off_rel = sb("off_rel", [P, TILES * R])
        logit = sb("logit", [P, TILES * RH])
        absent = sb("absent", [P, TILES * R])
        edges_only = whole.enter_context(ExitStack())
        src_t = sb("src_t", [P, EP], F32, edges_only)
        dst_t = sb("dst_t", [P, EP], F32, edges_only)

        with ExitStack() as ctx:
            w_self = sb("w_self", [P, F], F32, ctx)
            w_m2 = sb("w_m2", [P, F], F32, ctx)
            w_m2t = sb("w_m2t", [P, F], F32, ctx)
            w_u1b = sb("w_u1b", [P, F], F32, ctx)
            mb2_col = sb("mb2_col", [P, 1], F32, ctx)
            a_s = sb("a_s", [P, R * F], F32, ctx)
            a_d = sb("a_d", [P, R * F], F32, ctx)
            al_s = sb("al_s", [P, F], F32, ctx)
            al_d = sb("al_d", [P, F], F32, ctx)
            bias2 = sb("bias2", [P, 2, F], F32, ctx)
            part = sb("part", [P, 3, 2, F], BF16, ctx)
            left = sb("left", [P, 2, 2, F], F32, ctx)
            prod = sb("prod", [P, 5, R * F], F32, ctx)
            rows_i = sb("rows_i", [P, 5, P], I32, ctx)
            rows = sb("rows", [P, 5, P], F32, ctx)
            flags = sb("flags", [P, 4, P], F32, ctx)
            attr = sb("attr", [P, 2 * P], F32, ctx)
            attr2 = sb("attr2", [P, 2, P], F32, ctx)
            type_e = sb("type_e", [P, TILES], F32, ctx)
            s_weights = sem("s_weights")
            s_ident0 = sem("s_ident0")
            s_ident = sem("s_ident")
            s_pads = sem("s_pads")
            s_rows = sem("s_rows")
            s_const = sem("s_const")
            s_split = sem("s_split")
            s_prod = sem("s_prod")
            s_rowsf = sem("s_rowsf")
            s_flags = sem("s_flags")
            s_scratch = sem("s_scratch")
            s_tabs = sem("s_tabs")
            s_taken = sem("s_taken")
            s_type = sem("s_type")
            s_m2t = sem("s_m2t")
            s_m2ts = sem("s_m2ts")
            s_fold = sem("s_fold")
            s_done = sem("s_done")

            def row_of(v):
                return v.unsqueeze(0)

            loads = [
                (w_self[:, :], W_self), (w_rel[:, :].rearrange("i (r o) -> i r o", r=R), W_rel.rearrange("r i o -> i r o")),
                (w_cross[:, 0:F], W_cross), (w_m1s[:, :], mW1[0:F, :]), (w_m1d[:, :], mW1[F:2 * F, :]),
                (w_m1a[:, :], mW1[2 * F:2 * F + 2, :]), (w_m2[:, :], mW2), (w_u1x[:, :], uW1[0:F, :]),
                (w_u1b[:, :], uW1[F:2 * F, :]), (w_u2[:, :], uW2),
                (m1_bias[:, :], mb1.unsqueeze(1)), (u1_bias[:, :], ub1.unsqueeze(1)), (mb2_col[:, :], mb2.unsqueeze(1)),
                (gamma_b[:, :], row_of(gamma).broadcast_to([P, F])), (beta_b[:, :], row_of(beta).broadcast_to([P, F])),
                (al_s[:, :], row_of(a_src_lang.rearrange("h d -> (h d)")).broadcast_to([P, F])),
                (al_d[:, :], row_of(a_dst_lang.rearrange("h d -> (h d)")).broadcast_to([P, F])),
                (a_s[:, :], row_of(a_src_rel.rearrange("r h d -> (r h d)")).broadcast_to([P, R * F])),
                (a_d[:, :], row_of(a_dst_rel.rearrange("r h d -> (r h d)")).broadcast_to([P, R * F])),
                (bias2[:, 0, :], row_of(b_lang).broadcast_to([P, F])), (bias2[:, 1, :], row_of(ub2).broadcast_to([P, F])),
            ] + [(rel_bias[:, r:r + 1], b_rel[r, :].unsqueeze(1)) for r in range(R)]

            def tiled(v, start, count):
                return v[start:start + count * P].rearrange("(t p) -> t p", p=P)

            n_loads = 0
            with nc.Block() as block:
                @block.sync
                def _(sp):
                    for dest, source in loads:
                        sp.dma_start(dest, source).then_inc(s_weights, 16)

                @block.scalar
                def _(act):
                    act.wait_ge(s_pads, 6)
                    for kind, v in ((0, src), (1, edge_type), (2, dst)):
                        act.dma_start(rows_i[0:FULL, kind, :], tiled(v, 0, FULL)).then_inc(s_rows, 16)
                        act.dma_start(rows_i[FULL:FULL + 1, kind, 0:REST], row_of(v[FULL * P:E])).then_inc(s_rows, 16)
                    act.dma_start(rows_i[0:1, 3, 1:P], row_of(dst[0:P - 1])).then_inc(s_rows, 16)
                    act.dma_start(rows_i[1:FULL, 3, :], tiled(dst, P - 1, FULL - 1)).then_inc(s_rows, 16)
                    act.dma_start(rows_i[FULL:FULL + 1, 3, 0:REST + 1], row_of(dst[FULL * P - 1:E])).then_inc(s_rows, 16)
                    act.dma_start(rows_i[0:FULL, 4, :], tiled(dst, 1, FULL)).then_inc(s_rows, 16)
                    act.dma_start(rows_i[FULL:FULL + 1, 4, 0:REST - 1], row_of(dst[FULL * P + 1:E])).then_inc(s_rows, 16)
                    act.dma_start(attr[0:FULL, :], edge_attr[0:FULL * P, :].rearrange("(t p) c -> t (p c)", p=P)).then_inc(s_rows, 16)
                    act.dma_start(attr[FULL:FULL + 1, 0:2 * REST],
                                  row_of(edge_attr[FULL * P:E, :].rearrange("p c -> (p c)"))).then_inc(s_rows, 16)

                @block.gpsimd
                def _(pool):
                    for kind, value in ((0, 0), (1, 0), (2, N), (3, N), (4, N + 1)):
                        pool.memset(rows_i[:, kind, :], value).then_inc(s_pads, 1)
                    pool.memset(attr[:, :], 0.0).then_inc(s_pads, 1)
                    pool.memset(ident[:, :], 0.0).then_inc(s_ident0, 1)
                    pool.wait_ge(s_ident0, 1)
                    pool.affine_select(out=ident[:, :], in_=ident[:, :], compare_op=ALU.not_equal, fill=1.0, base=0,
                                       pattern=[[-1, P]], channel_multiplier=1).then_inc(s_ident, 1)
                    pool.memset(ones_b[:, :], 1.0).then_inc(s_const, 1)
                    pool.memset(eps_col[:, :], LN_EPS).then_inc(s_const, 1)
                    pool.memset(lang3[:, :], 0.0).then_inc(s_const, 1)
                    pool.memset(u2b3[:, :], 0.0).then_inc(s_const, 1)

            ROW_LOADS = 13
            with nc.Block() as block:
                @block.vector
                def _(dve):
                    dve.wait_ge(s_rows, 16 * ROW_LOADS)
                    dve.tensor_copy(rows[:, :, :], rows_i[:, :, :]).then_inc(s_rowsf, 1)
                    dve.tensor_copy(attr2[:, :, :], attr[:, :].rearrange("t (p c) -> t c p", c=2)).then_inc(s_rowsf, 1)
                    dve.wait_ge(s_rowsf, 2)
                    dve.tensor_tensor(flags[:, 0, :], rows[:, 2, :], rows[:, 3, :], ALU.is_equal).then_inc(s_flags, 1)
                    dve.tensor_tensor(flags[:, 1, :], rows[:, 2, :], rows[:, 4, :], ALU.not_equal).then_inc(s_flags, 1)
                    dve.tensor_scalar(flags[:, 2, :], rows[:, 2, :], float(N - 1), None, ALU.min).then_inc(s_flags, 1)
                    dve.wait_ge(s_flags, 3)
                    dve.scalar_tensor_tensor(flags[:, 3, :], rows[:, 2, :], float(N), flags[:, 1, :],
                                             ALU.subtract, ALU.mult).then_inc(s_flags, 1)
                    dve.wait_ge(s_flags, 4)
                    dve.tensor_scalar(flags[:, 3, :], flags[:, 3, :], float(N), None, ALU.add).then_inc(s_flags, 1)
                    dve.wait_ge(s_weights, 16 * len(loads))
                    dve.tensor_copy(part[:, 0], bias2[:, :, :]).then_inc(s_split, 1)
                    dve.wait_ge(s_split, 1)
                    dve.tensor_tensor(left[:, 0], bias2[:, :, :], part[:, 0], ALU.subtract).then_inc(s_split, 1)
                    dve.wait_ge(s_split, 2)
                    dve.tensor_copy(part[:, 1], left[:, 0]).then_inc(s_split, 1)
                    dve.wait_ge(s_split, 3)
                    dve.tensor_tensor(left[:, 1], left[:, 0], part[:, 1], ALU.subtract).then_inc(s_split, 1)
                    dve.wait_ge(s_split, 4)
                    dve.tensor_copy(part[:, 2], left[:, 1]).then_inc(s_split, 1)
                    dve.wait_ge(s_split, 5)
                    dve.wait_ge(s_const, 4)
                    for k in range(3):
                        for b, dest in ((0, lang3), (1, u2b3)):
                            dve.tensor_copy(dest[32 * k:32 * k + 1, :], part[32 * k:32 * k + 1, k, b, :]).then_inc(s_done, 1)
                    dve.wait_ge(s_ident, 1)
                    pairs = [(w_rel[:, :], a_s[:, :], w_log_s[:, :], R * F), (w_rel[:, :], a_d[:, :], w_log_d[:, :], R * F),
                             (w_cross[:, 0:F], al_s[:, :], w_cross[:, F:EB], F),
                             (w_self[:, :], al_s[:, :], w_node[:, F:EB], F),
                             (w_self[:, :], al_d[:, :], w_node[:, EB + F:2 * EB], F)]
                    for n, (w, a, _, size) in enumerate(pairs):
                        dve.tensor_tensor(prod[:, n, 0:size], w, a, ALU.mult).then_inc(s_prod, 1)
                    for n, (_, _, dest, size) in enumerate(pairs):
                        dve.wait_ge(s_prod, n + 1)
                        dve.tensor_reduce(dest, prod[:, n, 0:size].rearrange("p (h d) -> p h d", d=D), AX_X, ALU.add).then_inc(s_done, 1)
                    dve.tensor_copy(w_node[:, 0:F], w_self[:, :]).then_inc(s_done, 1)
                    dve.tensor_copy(w_node[:, EB:EB + F], ident[:, :]).then_inc(s_done, 1)
                    dve.tensor_tensor(w_self_id[:, :], w_self[:, :], ident[:, :], ALU.add).then_inc(s_done, 1)
                    dve.wait_ge(s_tabs, 4)
                    for k, dest in ((0, idx_src), (1, idx_dst), (2, idx_put), (3, type_e)):
                        dve.tensor_copy(dest[:, :], bank[0][:, k * P:k * P + TILES]).then_inc(s_type, 1)
                    dve.wait_ge(s_type, 4)
                    for r in range(R):
                        dve.tensor_scalar(off_rel[:, r::R], type_e[:, :], float(r), NEG, ALU.not_equal, ALU.mult).then_inc(s_done, 1)
                    dve.wait_ge(s_m2t, 1)
                    dve.tensor_copy(w_m2t[:, :], bank[1][:, 0:F]).then_inc(s_m2ts, 1)
                    dve.wait_ge(s_fold, 2)
                    dve.tensor_copy(w_u1m[:, :], bank[2][:, 0:F]).then_inc(s_done, 1)
                    dve.tensor_tensor(u1m_bias[:, :], bank[3][:, 0:1], u1_bias[:, :], ALU.add).then_inc(s_done, 1)

                @block.tensor
                def _(pe):
                    pe.wait_ge(s_ident, 1)
                    pe.wait_ge(s_flags, 5)
                    for k, table in enumerate((rows[:, 0, :], flags[:, 2, :], flags[:, 3, :], rows[:, 1, :])):
                        pe.transpose(bank[0][:, k * P:(k + 1) * P], table, ident[:, :]).then_inc(s_tabs, 1)
                    pe.wait_ge(s_weights, 16 * len(loads))
                    pe.transpose(bank[1][:, 0:F], w_m2[:, :], ident[:, :]).then_inc(s_m2t, 1)
                    pe.wait_ge(s_m2ts, 1)
                    pe.matmul(bank[2][:, 0:F], w_m2t[:, :], w_u1b[:, :], start=True, stop=True).then_inc(s_fold, 1)
                    pe.matmul(bank[3][:, 0:1], w_u1b[:, :], mb2_col[:, :], start=True, stop=True).then_inc(s_fold, 1)

                @block.sync
                def _(sp):
                    sp.wait_ge(s_flags, 2)
                    sp.dma_start(same_dram.rearrange("(t p) -> t p", p=P), flags[0:TILES, 0, :]).then_inc(s_scratch, 16)
                    sp.dma_start(last_dram.rearrange("(t p) -> t p", p=P), flags[0:TILES, 1, :]).then_inc(s_scratch, 16)
                    for c in range(2):
                        sp.dma_start(attr_dram[c].rearrange("(t p) -> t p", p=P), attr2[0:TILES, c, :]).then_inc(s_scratch, 16)
                    sp.wait_ge(s_scratch, 64)

        S = {k: sem(f"tail_{k}") for k in (
                "v", "st2", "hv2", "sp2", "mv2", "hv3", "sp3", "sd2", "rs2", "w", "xb", "y", "st3", "mv3", "sd3", "rs3", "nm3", "out")}

        def tail_buffers(tag, ctx):
            return {
                "v": sb(f"{tag}_v", [P, 2, QUAD, F], F32, ctx), "w": sb(f"{tag}_w", [P, 2, QUAD, F], F32, ctx),
                "xb": sb(f"{tag}_xb", [P, 2, QUAD, F], F32, ctx), "st2": sb(f"{tag}_st2", [P, QUAD, 6], F32, ctx),
                "st3": sb(f"{tag}_st3", [P, QUAD, 6], F32, ctx), "mid": sb(f"{tag}_mid", [P, 2, QUAD, 4], F32, ctx), "mv2": sb(f"{tag}_mv2", [P, 2, QUAD, 2], F32, ctx),
                "mv3": sb(f"{tag}_mv3", [P, 2, QUAD, 2], F32, ctx), "sd": sb(f"{tag}_sd", [P, 2, QUAD], F32, ctx),
                "rs2": sb(f"{tag}_rs2", [P, QUAD], F32, ctx), "rs3": sb(f"{tag}_rs3", [P, 2, QUAD], F32, ctx),
                "nm3": sb(f"{tag}_nm3", [P, 2, QUAD], F32, ctx)}

        def stats(dve, rows_in, st, done):
            for j in range(QUAD):
                ins = dve.bn_stats(st[:, j, :], rows_in[:, j, :])
            ins.then_inc(done, 1)

        def means(dve, n, st, mid, mv, halves, spread, done):
            dve.tensor_tensor(mid[:, :, 0:2], st[:, :, 1:3], st[:, :, 4:6], ALU.add).then_inc(halves, 1)
            dve.tensor_tensor(mid[:, :, 2], st[:, :, 1], st[:, :, 4], ALU.subtract).then_inc(halves, 1)
            dve.wait_ge(halves, 2 * n + 2)
            dve.scalar_tensor_tensor(mid[:, :, 3], mid[:, :, 2], F / 4.0, mid[:, :, 2], ALU.mult, ALU.mult).then_inc(spread, 1)
            dve.tensor_scalar(mv[:, :, 0], mid[:, :, 0], 0.5, None, ALU.mult).then_inc(done, 1)
            dve.wait_ge(spread, n + 1)
            dve.tensor_tensor(mv[:, :, 1], mid[:, :, 3], mid[:, :, 1], ALU.add).then_inc(done, 1)

        def tail_vector_add(dve, g, S, B, pV, c_V, count, x1_rows):
            dve.wait_ge(c_V, count)
            dve.tensor_tensor(B["v"][:, g.slot % 2], split(pV[:, :]), x1_rows, ALU.add).then_inc(S["v"], 1)

        def tail_vector_stats2(dve, g, S, B):
            dve.wait_ge(S["v"], g.n + 1)
            stats(dve, B["v"][:, g.slot % 2], B["st2"], S["st2"])

        def tail_vector_means2(dve, g, S, B):
            need(dve, S["sd2"], g.n - 1)
            dve.wait_ge(S["st2"], g.n + 1)
            means(dve, g.n, B["st2"], B["mid"][:, 0], B["mv2"][:, g.slot % 2], S["hv2"], S["sp2"], S["mv2"])

        def tail_vector_scale(dve, g, S, B):
            b = g.slot % 2
            dve.wait_ge(S["mv2"], 2 * g.n + 2)
            for j in range(QUAD):
                ins = dve.scalar_tensor_tensor(B["w"][:, b, j, :], B["v"][:, b, j, :], B["mv2"][:, b, j, 0:1],
                                               gamma_b[:, :], ALU.subtract, ALU.mult)
            ins.then_inc(S["w"], 1)
            dve.wait_ge(S["sd2"], g.n + 1)
            dve.reciprocal(B["rs2"][:, :], B["sd"][:, 0, :]).then_inc(S["rs2"], 1)

        def tail_vector_rs3(dve, g, S, B):
            b = g.slot % 2
            need(dve, S["out"], g.n - 1)
            dve.wait_ge(S["sd3"], g.n + 1)
            dve.reciprocal(B["rs3"][:, b, :], B["sd"][:, 1, :]).then_inc(S["rs3"], 1)
            dve.wait_ge(S["rs3"], g.n + 1)
            dve.scalar_tensor_tensor(B["nm3"][:, b, :], B["mv3"][:, b, :, 0], -1.0, B["rs3"][:, b, :],
                                     ALU.mult, ALU.mult).then_inc(S["nm3"], 1)

        def tail_vector_y(dve, g, S, B):
            b = g.slot % 2
            dve.wait_ge(S["rs2"], g.n + 1)
            dve.wait_ge(S["w"], g.n + 1)
            dve.wait_ge(S["xb"], g.n + 1)
            for j in range(QUAD):
                ins = dve.scalar_tensor_tensor(B["w"][:, b, j, :], B["w"][:, b, j, :], B["rs2"][:, j:j + 1],
                                               B["xb"][:, b, j, :], ALU.mult, ALU.add)
            ins.then_inc(S["y"], 1)

        def tail_vector_stats3(dve, g, S, B):
            b = g.slot % 2
            dve.wait_ge(S["y"], g.n + 1)
            stats(dve, B["w"][:, b], B["st3"], S["st3"])
            dve.wait_ge(S["st3"], g.n + 1)
            means(dve, g.n, B["st3"], B["mid"][:, 1], B["mv3"][:, b], S["hv3"], S["sp3"], S["mv3"])

        def tail_pool(pool, g, S, B, x1_done, x1_rows):
            need(pool, S["y"], g.n - 1)
            pool.wait_ge(x1_done, x1_rows[0])
            pool.tensor_tensor(B["xb"][:, g.slot % 2], x1_rows[1], beta_b[:, :].unsqueeze(1).broadcast_to([P, QUAD, F]),
                               ALU.add).then_inc(S["xb"], 1)

        def root(act, g, S, B, k):
            need(act, S[f"rs{k}"], g.n)
            act.wait_ge(S[f"mv{k}"], 2 * g.n + 2)
            act.activation(B["sd"][:, k - 2, :], B[f"mv{k}"][:, g.slot % 2, :, 1], ACT.Sqrt,
                           bias=eps_col[:, 0:1], scale=1.0 / F).then_inc(S[f"sd{k}"], 1)

        def tail_scalar_out(act, g, S, B, out_rows):
            b = g.slot % 2
            act.wait_ge(S["nm3"], g.n + 1)
            for j in range(QUAD):
                ins = act.activation(out_rows[:, j, :], B["w"][:, b, j, :], ACT.Identity,
                                     bias=B["nm3"][:, b, j:j + 1], scale=B["rs3"][:, b, j:j + 1])
            ins.then_inc(S["out"], 1)

        with ExitStack() as ctx:
            x_in = sb("x_in", [P, 2, 8 * F], F32, ctx)
            x_t = sb("x_t", [P, 2, GROUP], F32, ctx)
            z = sb("z", [P, 2, QUAD, F], F32, ctx)
            x1 = sb("x1", [P, 2, 8, F], F32, ctx)
            x1_t = sb("x1_t", [P, 2, GROUP], F32, ctx)
            hid_t = sb("hid_t", [P, 2, GROUP], F32, ctx)
            o_out = sb("o_out", [P, 2, 8, F], F32, ctx)
            st1 = sb("st1", [P, QUAD, 6], F32, ctx)
            mv1 = sb("mv1", [P, 2, QUAD, 2], F32, ctx)
            mid1 = sb("mid1", [P, QUAD, 4], F32, ctx)
            sd1 = sb("sd1", [P, QUAD], F32, ctx)
            rs1 = sb("rs1", [P, QUAD], F32, ctx)
            B = tail_buffers("n", ctx)
            e_rows = sb("e_rows", [P, 2 * QUAD, F], F32, ctx)
            e_idx = sb("e_idx", [P, 2 * QUAD], I32, ctx)
            e_t = sb("e_t", [P, 2, GROUP], F32, ctx)
            l_low = sb("l_low", [P, QUAD * RH], F32, ctx)
            l_leaky = sb("l_leaky", [P, QUAD * RH], F32, ctx)
            pT, pS, pX, pU, pV, pEs, pEd, pL = bank

            s_x = [sem(f"s_x{i}") for i in range(2)]
            s_x1 = [sem(f"s_x1out{i}") for i in range(2)]
            s_out = [sem(f"s_out{i}") for i in range(2)]
            c_T, c_xt, c_S, c_z = sem("c_T"), sem("c_xt"), sem("c_S"), sem("c_z")
            c_st1, c_mv1, c_sd1, c_rs1, c_x1 = sem("c_st1"), sem("c_mv1"), sem("c_sd1"), sem("c_rs1"), sem("c_x1")
            c_X, c_x1t, c_U, c_hid, c_V = sem("c_X"), sem("c_x1t"), sem("c_U"), sem("c_hid"), sem("c_V")
            c_hv1, c_sp1 = sem("c_hv1"), sem("c_sp1")
            e_ix, e_got, e_T, e_ts, e_kept, e_L, e_low, e_lk, e_log = (
                sem("e_ix"), sem("e_got"), sem("e_T"), sem("e_ts"), sem("e_kept"), sem("e_L"), sem("e_low"),
                sem("e_lk"), sem("e_log"))

            def rows_of(buf, g):
                return buf[:, g.slot // 2, 4 * (g.slot % 2):4 * (g.slot % 2) + 4, :]

            def steps(eng, step):
                for turn in (0, 1):
                    for k in range(4):
                        step(turn, k)
                with eng.Fori(2, EG - 1) as turn:
                    for k in range(4):
                        step(turn, k)
                for turn in (EG - 1, EG):
                    for k in range(4):
                        step(turn, k)

            def at(turn, k, offset):
                return behind(turn, k, 4, offset, GROUPS)

            def has_edges(turn):
                return not isinstance(turn, int) or turn < EG

            with nc.Block() as block:
                @block.sync
                def _(sp):
                    def view(dram, turn, q):
                        s = 2 * turn + q
                        base = TAIL if isinstance(s, int) and s == SUPERS - 1 else s * SUPER
                        return dram[bass.ds(base, SUPER), :].rearrange("(p j) f -> p (j f)", p=P)

                    def load(turn, q):
                        if isinstance(turn, int) and 2 * turn + q >= SUPERS:
                            return
                        need(sp, c_T, 4 * turn + 2 * q - 2)
                        sp.dma_start(x_in[:, q, :], view(x, turn, q)).then_inc(s_x[q], 16)

                    def store(turn, q, buf, dram, ready, done):
                        if isinstance(turn, int) and 2 * turn + q >= SUPERS:
                            return
                        sp.wait_ge(ready, 4 * turn + 2 * q + 2)
                        flat = buf[:, q].rearrange("p j f -> p (j f)")
                        to = view(dram, turn, q)
                        if isinstance(turn, int) and 2 * turn + q == SUPERS - 1:
                            for lo, hi in ((SKIP, 32), (32, P)):
                                sp.dma_start(to[lo:hi, :], flat[lo:hi, :]).then_inc(done[q], 16)
                        else:
                            sp.dma_start(to, flat).then_inc(done[q], 16)

                    def turn_of(turn):
                        for q in range(2):
                            load(turn + 1, q)
                            if not isinstance(turn, int) or turn >= 1:
                                store(turn - 1, q, o_out, out, S["out"], s_out)
                            store(turn, q, x1, x1_dram, c_x1, s_x1)
                    load(0, 0)
                    load(0, 1)
                    turn_of(0)
                    with sp.Fori(1, EG - 2) as turn:
                        turn_of(turn)
                    for turn in range(EG - 2, EG + 1):
                        turn_of(turn)
                    for q in range(2):
                        count = 16 * (EG - 1) + (32 if q == 0 else 0)
                        sp.wait_ge(s_x1[q], count)
                        sp.wait_ge(s_out[q], count)

                @block.gpsimd
                def _(pool):
                    def gather(turn, half):
                        for j in range(4 * half, 4 * half + 4):
                            pool.indirect_dma_start(e_rows[:, j, :], None, x[:, :],
                                                    bass.IndirectOffsetOnAxis(ap=e_idx[:, j:j + 1], axis=0)).then_inc(e_got, 16)

                    def step(turn, k):
                        if has_edges(turn) and k == 0:
                            need(pool, e_T, turn)
                            pool.tensor_copy(e_idx[:, 0:4], idx_src[:, bass.ds(turn * QUAD, QUAD)]).then_inc(e_ix, 1)
                            pool.tensor_copy(e_idx[:, 4:8], idx_dst[:, bass.ds(turn * QUAD, QUAD)]).then_inc(e_ix, 1)
                            pool.wait_ge(e_ix, 2 * turn + 2)
                        g = at(turn, k, 3)
                        if g.real:
                            tail_pool(pool, g, S, B, c_x1, (g.n + 1, rows_of(x1, g)))
                        if has_edges(turn) and k < 2:
                            gather(turn, k)
                    steps(pool, step)

                @block.tensor
                def _(pe):
                    def step(turn, k):
                        g = at(turn, k, 0)
                        if g.real:
                            pe.wait_ge(s_x[g.slot // 2], 16 * (g.turn + 1))
                            need(pe, c_xt, g.n)
                            for j in range(QUAD):
                                r = 4 * (g.slot % 2) + j
                                ins = pe.transpose(pT[:, j * P:(j + 1) * P], x_in[:, g.slot // 2, r * F:(r + 1) * F], ident[:, :])
                            ins.then_inc(c_T, 1)
                        g = at(turn, k, 1)
                        if g.real:
                            pe.wait_ge(c_xt, g.n + 1)
                            need(pe, c_z, g.n)
                            pe.matmul(pS[:, :], ones_b[:, :], lang3[:, :].unsqueeze(1).broadcast_to([P, QUAD, F]),
                                      start=True, stop=False)
                            for j in range(QUAD):
                                ins = pe.matmul(pS[:, j * F:(j + 1) * F], x_t[:, g.slot % 2, j * P:(j + 1) * P],
                                                w_self_id[:, :], start=False, stop=(j == QUAD - 1))
                            ins.then_inc(c_S, 1)
                        g = at(turn, k, 2)
                        if g.real:
                            pe.wait_ge(c_x1, g.n + 1)
                            need(pe, c_x1t, g.n)
                            for j in range(QUAD):
                                ins = pe.transpose(pX[:, j * P:(j + 1) * P], rows_of(x1, g)[:, j, :], ident[:, :])
                            ins.then_inc(c_X, 1)
                        g = at(turn, k, 3)
                        if g.real:
                            pe.wait_ge(c_x1t, g.n + 1)
                            need(pe, c_hid, g.n)
                            pe.matmul(pU[:, :], w_u1x[:, :], x1_t[:, g.slot % 2, :], start=True, stop=True).then_inc(c_U, 1)
                        g = at(turn, k, 4)
                        if g.real:
                            pe.wait_ge(c_hid, g.n + 1)
                            need(pe, S["v"], g.n)
                            pe.matmul(pV[:, :], ones_b[:, :], u2b3[:, :].unsqueeze(1).broadcast_to([P, QUAD, F]),
                                      start=True, stop=False)
                            for j in range(QUAD):
                                ins = pe.matmul(pV[:, j * F:(j + 1) * F], hid_t[:, g.slot % 2, j * P:(j + 1) * P],
                                                w_u2[:, :], start=False, stop=(j == QUAD - 1))
                            ins.then_inc(c_V, 1)
                        if has_edges(turn) and k == 2:
                            pe.wait_ge(e_got, 128 * (turn + 1))
                            need(pe, e_ts, 2 * turn)
                            need(pe, e_kept, 2 * turn)
                            for j in range(2 * QUAD):
                                to = (pEs, pEd)[j // QUAD]
                                ins = pe.transpose(to[:, (j % QUAD) * P:(j % QUAD + 1) * P], e_rows[:, j, :], ident[:, :])
                            ins.then_inc(e_T, 1)
                        if has_edges(turn) and k == 3:
                            pe.wait_ge(e_ts, 2 * turn + 2)
                            need(pe, e_low, turn)
                            need(pe, e_lk, turn)
                            for j in range(QUAD):
                                pe.matmul(pL[:, j * RH:(j + 1) * RH], e_t[:, 0, j * P:(j + 1) * P], w_log_s[:, :],
                                          start=True, stop=False)
                                ins = pe.matmul(pL[:, j * RH:(j + 1) * RH], e_t[:, 1, j * P:(j + 1) * P], w_log_d[:, :],
                                                start=False, stop=True)
                            ins.then_inc(e_L, 1)
                    steps(pe, step)

                @block.scalar
                def _(act):
                    def step(turn, k):
                        g = at(turn, k, 5)
                        if g.real:
                            root(act, g, S, B, 3)
                        g = at(turn, k, 0)
                        if g.real:
                            act.wait_ge(c_T, g.n + 1)
                            need(act, c_S, g.n - 1)
                            act.copy(x_t[:, g.slot % 2, :], pT[:, :]).then_inc(c_xt, 1)
                        g = at(turn, k, 1)
                        if g.real:
                            act.wait_ge(c_S, g.n + 1)
                            need(act, c_x1, g.n - 1)
                            act.copy(z[:, g.slot % 2].rearrange("p j f -> p (j f)"), pS[:, :]).then_inc(c_z, 1)
                        g = at(turn, k, 2)
                        if g.real:
                            act.wait_ge(c_X, g.n + 1)
                            need(act, c_U, g.n - 1)
                            act.copy(x1_t[:, g.slot % 2, :], pX[:, :]).then_inc(c_x1t, 1)
                        g = at(turn, k, 3)
                        if g.real:
                            act.wait_ge(c_U, g.n + 1)
                            need(act, c_V, g.n - 1)
                            act.activation(hid_t[:, g.slot % 2, :], pU[:, :], ACT.Relu, bias=u1_bias[:, 0:1]).then_inc(c_hid, 1)
                        g = at(turn, k, 1)
                        if g.real:
                            need(act, c_rs1, g.n)
                            act.wait_ge(c_mv1, 2 * g.n + 2)
                            act.activation(sd1[:, :], mv1[:, g.slot % 2, :, 1], ACT.Sqrt, bias=eps_col[:, 0:1], scale=1.0 / F).then_inc(c_sd1, 1)
                        g = at(turn, k, 4)
                        if g.real:
                            root(act, g, S, B, 2)
                        g = at(turn, k, 5)
                        if g.real:
                            need(act, s_out[g.slot // 2], 16 * g.turn)
                            tail_scalar_out(act, g, S, B, rows_of(o_out, g))
                        if has_edges(turn) and k == 2:
                            act.wait_ge(e_T, turn + 1)
                            need(act, e_L, turn)
                            for c, (frm, keep) in enumerate(((pEs, src_t), (pEd, dst_t))):
                                act.copy(e_t[:, c, :], frm[:, :]).then_inc(e_ts, 1)
                                act.copy(keep[:, bass.ds(turn * GROUP, GROUP)], frm[:, :]).then_inc(e_kept, 1)
                    steps(act, step)

                @block.vector
                def _(dve):
                    def step(turn, k):
                        b, a, f = at(turn, k, 1), at(turn, k, 4), at(turn, k, 5)
                        if b.real:
                            dve.wait_ge(c_z, b.n + 1)
                            stats(dve, z[:, b.slot % 2], st1, c_st1)
                        if a.real:
                            tail_vector_add(dve, a, S, B, pV, c_V, a.n + 1, rows_of(x1, a))
                        if b.real:
                            dve.wait_ge(c_st1, b.n + 1)
                            means(dve, b.n, st1, mid1, mv1[:, b.slot % 2], c_hv1, c_sp1, c_mv1)
                        if a.real:
                            tail_vector_stats2(dve, a, S, B)
                        if b.real:
                            dve.wait_ge(c_sd1, b.n + 1)
                            dve.reciprocal(rs1[:, :], sd1[:, :]).then_inc(c_rs1, 1)
                        if a.real:
                            tail_vector_means2(dve, a, S, B)
                        if b.real:
                            dve.wait_ge(c_rs1, b.n + 1)
                            need(dve, s_x1[b.slot // 2], 16 * b.turn)
                            for j in range(QUAD):
                                ins = dve.tensor_scalar(rows_of(x1, b)[:, j, :], z[:, b.slot % 2, j, :],
                                                        mv1[:, b.slot % 2, j, 0:1], rs1[:, j:j + 1], ALU.subtract, ALU.mult)
                            ins.then_inc(c_x1, 1)
                        if f.real:
                            tail_vector_rs3(dve, f, S, B)
                        if a.real:
                            need(dve, S["out"], a.n - 1)
                            tail_vector_scale(dve, a, S, B)
                            tail_vector_y(dve, a, S, B)
                            tail_vector_stats3(dve, a, S, B)
                        if has_edges(turn) and k == 3:
                            dve.wait_ge(e_L, turn + 1)
                            dve.tensor_scalar(l_low[:, :], pL[:, 0:QUAD * RH], SLOPE, None, ALU.mult).then_inc(e_low, 1)
                            dve.wait_ge(e_low, turn + 1)
                            dve.tensor_tensor(l_leaky[:, :], pL[:, 0:QUAD * RH], l_low[:, :], ALU.max).then_inc(e_lk, 1)
                            dve.wait_ge(e_lk, turn + 1)
                            dve.tensor_tensor(
                                logit[:, bass.ds(turn * QUAD * RH, QUAD * RH)].rearrange("p (t h) -> p t h", h=H),
                                l_leaky[:, :].rearrange("p (t h) -> p t h", h=H),
                                off_rel[:, bass.ds(turn * QUAD * R, QUAD * R)].unsqueeze(2).broadcast_to([P, QUAD * R, H]),
                                ALU.add).then_inc(e_log, 1)
                    steps(dve, step)

        weight = logit
        with ExitStack() as ctx:
            buf0 = sb("buf0", [P, BE], F32, ctx)
            buf1 = sb("buf1", [P, BE], F32, ctx)
            buf2 = sb("buf2", [P, BE], F32, ctx)
            buf3 = sb("buf3", [P, BE], F32, ctx)
            same_f = sb("same_f", [P, BE], BF16, ctx)
            apart = sb("apart", [P, BE], BF16, ctx)
            last_f = sb("last_f", [P, BE], BF16, ctx)
            more_f = sb("more_f", [P, BE], BF16, ctx)
            through = sb("through", [P, 3], F32, ctx)
            carry = sb("carry", [P, 5], F32, ctx)
            s_flag = [sem(f"s_flag{i}") for i in range(2)]
            s_pack, s_packed, s_vec, s_exp, s_back, s_backed, s_rc = (
                sem("s_pack"), sem("s_packed"), sem("s_vec"), sem("s_exp"), sem("s_back"), sem("s_backed"), sem("s_rc"))
            s_order = sem("s_order")
            s_pen_ready, s_alpha_ready, s_arg_ready, s_rc_ready = (
                sem("s_pen_ready"), sem("s_alpha_ready"), sem("s_arg_ready"), sem("s_rc_ready"))
            BANKS_USED = -(-BT // QUAD)

            def cols(q):
                return min(QUAD, BT - QUAD * q)

            with nc.Block() as block:
                @block.sync
                def _(sp):
                    for n, (flag, dest) in enumerate(((same_dram, buf2), (last_dram, buf3))):
                        for b in range(BLOCKS):
                            sp.dma_start(dest[b * RH:(b + 1) * RH, :],
                                         flag[b * BE:(b + 1) * BE].unsqueeze(0).broadcast_to([RH, BE])).then_inc(s_flag[n], 16)
                    sp.wait_ge(s_rc_ready, 1)
                    for b in range(BLOCKS):
                        sp.dma_start(rcnt_dram[b:b + 1, :], buf3[b * RH:b * RH + 1, :]).then_inc(s_rc, 16)
                    sp.wait_ge(s_rc, 16 * BLOCKS)

                @block.tensor
                def _(pe):
                    pe.wait_ge(s_order, 1)
                    for i in range(BT):
                        pe.transpose(bank[i // QUAD][:, (i % QUAD) * P:(i % QUAD + 1) * P], buf1[:, i * P:(i + 1) * P],
                                     ident[:, :]).then_inc(s_pack, 1)
                    for n, (ready, frm) in enumerate(((s_pen_ready, buf3), (s_alpha_ready, buf0))):
                        pe.wait_ge(ready, 1)
                        for i in range(BT):
                            if i % QUAD == 0:
                                if n == 0:
                                    pe.wait_ge(s_packed, i // QUAD + 1)
                                else:
                                    pe.wait_ge(s_backed, i // QUAD + 1)
                            pe.transpose(bank[i // QUAD][:, (i % QUAD) * P:(i % QUAD + 1) * P],
                                         frm[:, i * P:(i + 1) * P], ident[:, :]).then_inc(s_back, 1)

                @block.scalar
                def _(act):
                    act.copy(buf1[:, :].rearrange("p (i b c) -> p i b c", b=BLOCKS, c=RH),
                             logit[:, :].rearrange("p (b i c) -> p i b c", b=BLOCKS, c=RH)).then_inc(s_order, 1)
                    for q in range(BANKS_USED):
                        act.wait_ge(s_pack, QUAD * q + cols(q))
                        act.copy(buf0[:, q * GROUP:q * GROUP + cols(q) * P], bank[q][:, 0:cols(q) * P]).then_inc(s_packed, 1)
                    for q in range(BANKS_USED):
                        act.wait_ge(s_back, QUAD * q + cols(q))
                        frm = bank[q][:, 0:cols(q) * P].rearrange("p (i b r h) -> p i b r h", b=BLOCKS, r=R, h=H)
                        to = absent[:, :].rearrange("p (b i r) -> p i b r", b=BLOCKS, r=R)
                        act.copy(to[:, QUAD * q:QUAD * q + cols(q)], frm[:, :, :, :, 0]).then_inc(s_backed, 1)
                    act.wait_ge(s_arg_ready, 1)
                    act.activation(buf1[:, :], buf1[:, :], ACT.Exp, scale=-1.0).then_inc(s_exp, 1)
                    for q in range(BANKS_USED):
                        act.wait_ge(s_back, BT + QUAD * q + cols(q))
                        frm = bank[q][:, 0:cols(q) * P].rearrange("p (i b c) -> p i b c", b=BLOCKS, c=RH)
                        to = weight[:, :].rearrange("p (b i c) -> p i b c", b=BLOCKS, c=RH)
                        act.copy(to[:, QUAD * q:QUAD * q + cols(q)], frm).then_inc(s_backed, 1)

                @block.vector
                def _(dve):
                    chain = [0]

                    def link(ins):
                        chain[0] += 1
                        ins.then_inc(s_vec, 1)
                        dve.wait_ge(s_vec, chain[0])

                    def last_inc(ins, done):
                        ins.then_inc(done, 1)

                    def quarter(v, b):
                        return v[b * RH:(b + 1) * RH]

                    def run(outp, data0, data1, op0, op1, n, thr, start, forward):
                        order = slice(None, None, 1 if forward else -1)
                        edge = slice(BE - 1, BE) if forward else slice(0, 1)
                        link(dve.memset(carry[:, n:n + 1], start))
                        link(dve.tensor_tensor_scan(outp[:, order], data0[:, order], data1[:, order], start, op0, op1))
                        for b in range(BLOCKS - 1):
                            here, there = (b, b + 1) if forward else (BLOCKS - 1 - b, BLOCKS - 2 - b)
                            link(dve.scalar_tensor_tensor(
                                quarter(carry, there)[:, n:n + 1], quarter(carry, here)[:, n:n + 1],
                                quarter(through, here)[:, thr:thr + 1], quarter(outp, here)[:, edge], op0, op1))
                        link(dve.tensor_tensor_scan(outp[:, order], data0[:, order], data1[:, order],
                                                    carry[:, n:n + 1], op0, op1))

                    dve.wait_ge(s_flag[0], 16 * BLOCKS)
                    dve.wait_ge(s_flag[1], 16 * BLOCKS)
                    link(dve.tensor_copy(same_f[:, :], buf2[:, :]))
                    link(dve.tensor_scalar(apart[:, :], buf2[:, :], 1.0, -NEG, ALU.subtract, ALU.mult))
                    link(dve.tensor_copy(last_f[:, :], buf3[:, :]))
                    link(dve.tensor_scalar(more_f[:, :], buf3[:, :], -1.0, 1.0, ALU.mult, ALU.add))
                    for n, v in enumerate((apart, same_f, more_f)):
                        link(dve.tensor_reduce(through[:, n:n + 1], v[:, :], AX_X, ALU.min))
                    dve.wait_ge(s_packed, BANKS_USED)
                    run(buf1, apart, buf0, ALU.add, ALU.max, 0, 0, NEG, True)
                    link(dve.tensor_tensor(buf3[:, :], buf1[:, :], last_f[:, :], ALU.mult))
                    run(buf2, more_f, buf3, ALU.mult, ALU.add, 1, 2, 0.0, False)
                    last_inc(dve.tensor_scalar(buf3[:, :], buf2[:, :], 0.1 * NEG, NEG, ALU.is_lt, ALU.mult), s_pen_ready)
                    last_inc(dve.scalar_tensor_tensor(buf1[:, :], buf2[:, :], 0.1 * NEG, buf0[:, :], ALU.max, ALU.subtract),
                             s_arg_ready)
                    dve.wait_ge(s_exp, 1)
                    run(buf0, same_f, buf1, ALU.mult, ALU.add, 2, 1, 0.0, True)
                    link(dve.tensor_tensor(buf2[:, :], buf0[:, :], last_f[:, :], ALU.mult))
                    run(buf0, more_f, buf2, ALU.mult, ALU.add, 3, 2, 0.0, False)
                    link(dve.tensor_scalar(buf0[:, :], buf0[:, :], 1e-30, None, ALU.max))
                    link(dve.reciprocal(buf2[:, :], buf0[:, :]))
                    last_inc(dve.tensor_tensor(buf0[:, :], buf1[:, :], buf2[:, :], ALU.mult), s_alpha_ready)
                    dve.wait_ge(s_alpha_ready, 1)
                    link(dve.memset(buf1[:, :], 1.0))
                    run(buf2, same_f, buf1, ALU.mult, ALU.add, 4, 1, 0.0, True)
                    dve.wait_ge(s_back, BT)
                    dve.reciprocal(buf3[:, :], buf2[:, :]).then_inc(s_rc_ready, 1)

        with ExitStack() as ctx:
            same_g = sb("same_g", [P, 2, GROUP], F32, ctx)
            s_t = sb("s_t", [P, GROUP], F32, ctx)
            d_t = sb("d_t", [P, GROUP], F32, ctx)
            val = sb("val", [P, 2, R * F], F32, ctx)
            rel_t = sb("rel_t", [P, R, GROUP], F32, ctx)
            act_t = sb("act_t", [P, R, GROUP], F32, ctx)
            tails = sb("tails", [P, R], F32, ctx)
            ent = sb("ent", [P, 2, QUAD, 6 * EB], F32, ctx)
            lg = sb("lg", [P, QUAD * K5 * H], F32, ctx)
            lg2 = sb("lg2", [P, QUAD * K5 * H], F32, ctx)
            ex = sb("ex", [P, QUAD * K5 * H], F32, ctx)
            top = sb("top", [P, QUAD * H], F32, ctx)
            rsum = sb("rsum", [P, QUAD * H], F32, ctx)
            rinv = sb("rinv", [P, QUAD * H], F32, ctx)
            z_e = sb("z_e", [P, 2, QUAD, F], F32, ctx)
            x1_e = sb("x1_e", [P, 2, QUAD, F], F32, ctx)
            st_e = sb("st_e", [P, QUAD, 6], F32, ctx)
            mv_e = sb("mv_e", [P, QUAD, 2], F32, ctx)
            mid_e = sb("mid_e", [P, QUAD, 4], F32, ctx)
            sd_e = sb("sd_e", [P, QUAD], F32, ctx)
            rs_e = sb("rs_e", [P, QUAD], F32, ctx)
            put_ix = sb("put_ix", [P, 2, QUAD], I32, ctx)
            pXW, pM, pE = bank[0:2], bank[2:6], bank[6:8]
            f_hv, f_sp = sem("f_hv"), sem("f_sp")
            f_same = [sem(f"f_same{i}") for i in range(2)]
            f_put = [sem(f"f_put{i}") for i in range(2)]
            (f_s, f_d, f_XW, f_val, f_M, f_scan, f_tail, f_gelu, f_E0, f_E1, f_ent0, f_ent1, f_ls, f_ld, f_low, f_lg, f_top, f_arg,
             f_ex, f_sum, f_inv, f_al, f_wt, f_p1, f_p2, f_z, f_st, f_mv, f_sd, f_rs, f_x1, f_ix) = [sem("f_" + s) for s in (
                "s", "d", "XW", "val", "M", "scan", "tail", "gelu", "E0", "E1", "ent0", "ent1", "ls", "ld", "low", "lg", "top", "arg",
                "ex", "sum", "inv", "al", "wt", "p1", "p2", "z", "st", "mv", "sd", "rs", "x1", "ix")]

            def at(turn, k, offset):
                return behind(turn, k, 2, offset, EG)

            def steps(eng, step):
                for turn in (0, 1):
                    for k in range(2):
                        step(turn, k)
                with eng.Fori(2, EG // 2) as turn:
                    for k in range(2):
                        step(turn, k)
                for turn in range(EG // 2, EG // 2 + 3):
                    for k in range(2):
                        step(turn, k)

            def entry(s):
                return ent[:, s].rearrange("p j (k c) -> p j k c", k=6)

            with nc.Block() as block:
                @block.sync
                def _(sp):
                    def step(turn, k):
                        g = at(turn, k, 0)
                        if g.real:
                            need(sp, f_scan, R * (g.n - 1))
                            sp.dma_start(same_g[:, k, :], same_dram[bass.ds(g.n * GROUP, GROUP)].unsqueeze(0)
                                         .broadcast_to([P, GROUP])).then_inc(f_same[k], 16)
                    steps(sp, step)

                @block.tensor
                def _(pe):
                    def product(g, j):
                        need(pe, f_val, 4 * g.n + j - 1)
                        pe.matmul(pXW[j % 2][:, :], s_t[:, j * P:(j + 1) * P], w_rel[:, :], start=True, stop=True).then_inc(f_XW, 1)

                    def turn_over(g, j):
                        pe.wait_ge(f_val, 4 * g.n + j + 1)
                        for r in range(R):
                            if j == 0:
                                need(pe, f_scan, R * (g.n - 1) + r + 1)
                            ins = pe.transpose(pM[r][:, j * P:(j + 1) * P], val[:, j % 2, r * F:(r + 1) * F], ident[:, :])
                        ins.then_inc(f_M, 1)

                    def step(turn, k):
                        g, e = at(turn, k, 0), at(turn, k, 1)
                        if g.real:
                            pe.wait_ge(f_s, g.n + 1)
                            product(g, 0)
                            product(g, 1)
                            turn_over(g, 0)
                            product(g, 2)
                            turn_over(g, 1)
                            product(g, 3)
                            turn_over(g, 2)
                            turn_over(g, 3)
                        if e.real:
                            pe.wait_ge(f_gelu, R * (e.n + 1))
                            pe.wait_ge(f_d, e.n + 1)
                            for j in range(QUAD):
                                need(pe, f_ent0, 4 * e.n + j)
                                for r in range(3):
                                    ins = pe.matmul(pE[0][:, r * EB:(r + 1) * EB], act_t[:, r, j * P:(j + 1) * P],
                                                    w_cross[:, :], start=(r == 0), stop=(r == 2), skip_group_check=True)
                                ins.then_inc(f_E0, 1)
                                need(pe, f_ent1, 4 * e.n + j)
                                pe.matmul(pE[1][:, 0:EB], act_t[:, 3, j * P:(j + 1) * P], w_cross[:, :],
                                          start=True, stop=False, skip_group_check=True)
                                pe.matmul(pE[1][:, EB:3 * EB], d_t[:, j * P:(j + 1) * P], w_node[:, :],
                                          start=False, stop=False, skip_group_check=True)
                                pe.matmul(pE[1][:, 2 * EB:2 * EB + F], ones_b[:, :], lang3[:, :],
                                          start=False, stop=True, skip_group_check=True).then_inc(f_E1, 1)
                    steps(pe, step)

                @block.scalar
                def _(act):
                    def step(turn, k):
                        g, e, s, w = at(turn, k, 0), at(turn, k, 1), at(turn, k, 2), at(turn, k, 3)
                        if s.real:
                            act.wait_ge(f_arg, s.n + 1)
                            need(act, f_al, s.n)
                            act.activation(ex[:, :], lg[:, :], ACT.Exp).then_inc(f_ex, 1)
                        if e.real:
                            need(act, f_z, e.n - 1)
                            for j in range(QUAD):
                                act.wait_ge(f_E0, 4 * e.n + j + 1)
                                act.copy(ent[:, e.slot, j, 0:3 * EB], pE[0][:, 0:3 * EB]).then_inc(f_ent0, 1)
                                act.wait_ge(f_E1, 4 * e.n + j + 1)
                                act.copy(ent[:, e.slot, j, 3 * EB:6 * EB], pE[1][:, 0:3 * EB]).then_inc(f_ent1, 1)
                        if w.real:
                            act.wait_ge(f_mv, 2 * w.n + 2)
                            act.activation(sd_e[:, :], mv_e[:, :, 1], ACT.Sqrt, bias=eps_col[:, 0:1], scale=1.0 / F).then_inc(f_sd, 1)
                        if g.real:
                            need(act, f_E1, 4 * g.n)
                            for r in range(R):
                                act.wait_ge(f_scan, R * g.n + r + 1)
                                act.activation(act_t[:, r, :], rel_t[:, r, :], ACT.Gelu, bias=rel_bias[:, r:r + 1]).then_inc(f_gelu, 1)
                    steps(act, step)

                @block.vector
                def _(dve):
                    def messages(g, j):
                        dve.wait_ge(f_XW, 4 * g.n + j + 1)
                        need(dve, f_M, 4 * g.n + j - 1)
                        dve.tensor_tensor(
                            val[:, j % 2, :].rearrange("p (c d) -> p c d", d=D),
                            pXW[j % 2][:, :].rearrange("p (c d) -> p c d", d=D),
                            weight[:, bass.ds((g.n * QUAD + j) * RH, RH)].unsqueeze(2).broadcast_to([P, RH, D]),
                            ALU.mult).then_inc(f_val, 1)

                    def scale(s, j):
                        e4 = entry(s.slot)[:, j, 0:K5, 0:F].rearrange("p k (h d) -> p k h d", d=D)
                        al = lg2[:, :].rearrange("p (j k h) -> p j k h", j=QUAD, h=H)[:, j]
                        dve.tensor_tensor(e4, e4, al.unsqueeze(3).broadcast_to([P, K5, H, D]), ALU.mult).then_inc(f_wt, 1)

                    def step(turn, k):
                        g, e, s, w = at(turn, k, 0), at(turn, k, 1), at(turn, k, 2), at(turn, k, 3)
                        if g.real:
                            need(dve, f_XW, 4 * g.n)
                            dve.tensor_copy(s_t[:, :], src_t[:, bass.ds(g.n * GROUP, GROUP)]).then_inc(f_s, 1)
                        if e.real:
                            need(dve, f_E1, 4 * e.n)
                            dve.tensor_copy(d_t[:, :], dst_t[:, bass.ds(e.n * GROUP, GROUP)]).then_inc(f_d, 1)
                        lg4 = lg[:, :].rearrange("p (j k h) -> p j k h", j=QUAD, h=H)
                        low4 = lg2[:, :].rearrange("p (j k h) -> p j k h", j=QUAD, h=H)
                        if s.real:
                            dve.wait_ge(f_ent1, 4 * (s.n + 1))
                            dve.wait_ge(f_ent0, 4 * (s.n + 1))
                            en = entry(s.slot)
                            dve.tensor_tensor(lg4, en[:, :, 0:K5, F:EB],
                                              en[:, :, K5, F:EB].unsqueeze(2).broadcast_to([P, QUAD, K5, H]), ALU.add).then_inc(f_ls, 1)
                            dve.wait_ge(f_ls, s.n + 1)
                            dve.scalar_tensor_tensor(lg2[:, :], lg[:, :], SLOPE, lg[:, :], ALU.mult, ALU.max).then_inc(f_low, 1)
                            dve.wait_ge(f_low, s.n + 1)
                            dve.tensor_tensor(low4[:, :, 0:R, :], low4[:, :, 0:R, :],
                                              absent[:, bass.ds(s.n * QUAD * R, QUAD * R)].rearrange("p (j r) -> p j r", r=R)
                                              .unsqueeze(3).broadcast_to([P, QUAD, R, H]), ALU.add).then_inc(f_lg, 1)
                            dve.wait_ge(f_lg, s.n + 1)
                            top3 = top[:, :].rearrange("p (j h) -> p j h", h=H)
                            dve.tensor_reduce(top3, low4.rearrange("p j k h -> p j h k"), AX_X, ALU.max).then_inc(f_top, 1)
                            dve.wait_ge(f_top, s.n + 1)
                            dve.tensor_tensor(lg4, low4, top3.unsqueeze(2).broadcast_to([P, QUAD, K5, H]), ALU.subtract).then_inc(f_arg, 1)
                        if g.real:
                            messages(g, 0)
                            messages(g, 1)
                        if s.real:
                            dve.wait_ge(f_ex, s.n + 1)
                            ex4 = ex[:, :].rearrange("p (j k h) -> p j k h", j=QUAD, h=H)
                            sum3 = rsum[:, :].rearrange("p (j h) -> p j h", h=H)
                            dve.tensor_reduce(sum3, ex4.rearrange("p j k h -> p j h k"), AX_X, ALU.add).then_inc(f_sum, 1)
                            dve.wait_ge(f_sum, s.n + 1)
                            dve.reciprocal(rinv[:, :], rsum[:, :]).then_inc(f_inv, 1)
                            dve.wait_ge(f_inv, s.n + 1)
                            inv3 = rinv[:, :].rearrange("p (j h) -> p j h", h=H)
                            dve.tensor_tensor(low4, ex4, inv3.unsqueeze(2).broadcast_to([P, QUAD, K5, H]), ALU.mult).then_inc(f_al, 1)
                        if g.real:
                            messages(g, 2)
                        if s.real:
                            dve.wait_ge(f_al, s.n + 1)
                            scale(s, 0)
                        if g.real:
                            messages(g, 3)
                        if s.real:
                            for j in range(1, QUAD):
                                scale(s, j)
                        if w.real:
                            dve.wait_ge(f_z, w.n + 1)
                            stats(dve, z_e[:, w.slot], st_e, f_st)
                            dve.wait_ge(f_st, w.n + 1)
                            means(dve, w.n, st_e, mid_e, mv_e, f_hv, f_sp, f_mv)
                        if g.real:
                            dve.wait_ge(f_same[k], 16 * (g.turn + 1))
                            need(dve, f_tail, g.n)
                            for r in range(R):
                                dve.wait_ge(f_M, 4 * (g.n + 1))
                                need(dve, f_gelu, R * (g.n - 1) + r + 1)
                                start = tails[:, r:r + 1] if not isinstance(g.n, int) or g.n > 0 else 0.0
                                dve.tensor_tensor_scan(rel_t[:, r, :], same_g[:, k, :], pM[r][:, :], start,
                                                       ALU.mult, ALU.add).then_inc(f_scan, 1)
                            dve.wait_ge(f_scan, R * (g.n + 1))
                            dve.tensor_copy(tails[:, :], rel_t[:, :, GROUP - 1]).then_inc(f_tail, 1)
                        if w.real:
                            dve.wait_ge(f_sd, w.n + 1)
                            dve.reciprocal(rs_e[:, :], sd_e[:, :]).then_inc(f_rs, 1)
                            dve.wait_ge(f_rs, w.n + 1)
                            need(dve, f_put[w.slot], 64 * w.turn)
                            for j in range(QUAD):
                                ins = dve.tensor_scalar(x1_e[:, w.slot, j, :], z_e[:, w.slot, j, :], mv_e[:, j, 0:1],
                                                        rs_e[:, j:j + 1], ALU.subtract, ALU.mult)
                            ins.then_inc(f_x1, 1)
                    steps(dve, step)

                @block.gpsimd
                def _(pool):
                    def step(turn, k):
                        s, o = at(turn, k, 2), at(turn, k, 4)
                        if o.real:
                            need(pool, f_put[o.slot], 64 * o.turn)
                            pool.tensor_copy(put_ix[:, o.slot, :], idx_put[:, bass.ds(o.n * QUAD, QUAD)]).then_inc(f_ix, 1)
                            pool.wait_ge(f_ix, o.n + 1)
                            pool.wait_ge(f_x1, o.n + 1)
                        if s.real:
                            pool.wait_ge(f_wt, 4 * (s.n + 1))
                            en = entry(s.slot)

                            def plus(a, b, dest, done):
                                pool.tensor_tensor(dest, en[:, :, a, 0:F], en[:, :, b, 0:F], ALU.add).then_inc(done, 1)
                            plus(0, 1, en[:, :, 0, 0:F], f_p1)
                            plus(2, 3, en[:, :, 2, 0:F], f_p1)
                            plus(4, 5, en[:, :, 4, 0:F], f_p1)
                            pool.wait_ge(f_p1, 3 * (s.n + 1))
                            plus(0, 2, en[:, :, 0, 0:F], f_p2)
                            pool.wait_ge(f_p2, s.n + 1)
                            need(pool, f_x1, s.n - 1)
                            plus(0, 4, z_e[:, s.slot], f_z)
                        if o.real:
                            for j in range(QUAD):
                                pool.indirect_dma_start(
                                    x1_dram[:, :], bass.IndirectOffsetOnAxis(ap=put_ix[:, o.slot, j:j + 1], axis=0),
                                    x1_e[:, o.slot, j, :], None, bounds_check=N - 1, oob_is_err=False).then_inc(f_put[o.slot], 16)
                    steps(pool, step)
                    for slot in range(2):
                        pool.wait_ge(f_put[slot], 64 * ((EG + 1 - slot) // 2))
        edges_only.close()

        with ExitStack() as ctx:
            same_h = sb("same_h", [P, 4, GROUP], F32, ctx)
            rcnt_h = sb("rcnt_h", [P, 4, GROUP], F32, ctx)
            attr_h = sb("attr_h", [2, 4, GROUP], F32, ctx)
            xs_r = sb("xs_r", [P, 4, QUAD, F], F32, ctx)
            xd_r = sb("xd_r", [P, 4, QUAD, F], F32, ctx)
            xs_t = sb("xs_t", [P, 4, GROUP], F32, ctx)
            xd_t = sb("xd_t", [P, 4, GROUP], F32, ctx)
            msg_t = sb("msg_t", [P, 2, GROUP], F32, ctx)
            sum_t = sb("sum_t", [P, 2, GROUP], F32, ctx)
            mean_t = sb("mean_t", [P, 2, GROUP], F32, ctx)
            up_t = sb("up_t", [P, 2, GROUP], F32, ctx)
            o_e = sb("o_e", [P, 4, QUAD, F], F32, ctx)
            get_ix = sb("get_ix", [P, 4, 2 * QUAD], I32, ctx)
            out_ix = sb("out_ix", [P, 4, QUAD], I32, ctx)
            B2 = tail_buffers("e", ctx)
            qS, qD, qH, qU, qV = bank[0:5]
            h_row = [sem(f"h_row{i}") for i in range(4)]
            h_got = [sem(f"h_got{i}") for i in range(4)]
            h_put = [sem(f"h_put{i}") for i in range(4)]
            h_ix, h_T, h_t, h_H, h_msg, h_sum, h_mean, h_U, h_up, h_V, h_oix = (
                sem("h_ix"), sem("h_T"), sem("h_t"), sem("h_H"), sem("h_msg"), sem("h_sum"), sem("h_mean"), sem("h_U"),
                sem("h_up"), sem("h_V"), sem("h_oix"))

            def at(turn, k, offset):
                return behind(turn, k, 4, offset, EG)

            def late(g):
                return g._replace(n=g.n + GROUPS)

            def steps(eng, step):
                for turn in (0, 1):
                    for k in range(4):
                        step(turn, k)
                with eng.Fori(2, EG // 4) as turn:
                    for k in range(4):
                        step(turn, k)
                for turn in (EG // 4, EG // 4 + 1):
                    for k in range(4):
                        step(turn, k)

            with nc.Block() as block:
                @block.sync
                def _(sp):
                    def step(turn, k):
                        g = at(turn, k, 0)
                        if g.real:
                            need(sp, h_mean, g.n - 3)
                            need(sp, h_H, g.n - 3)
                            cols = bass.ds(g.n * GROUP, GROUP)
                            sp.dma_start(same_h[:, k, :], same_dram[cols].unsqueeze(0).broadcast_to([P, GROUP])).then_inc(h_row[k], 16)
                            sp.dma_start(rcnt_h[:, k, :], rcnt_dram.rearrange("b e -> (b e)")[cols].unsqueeze(0)
                                         .broadcast_to([P, GROUP])).then_inc(h_row[k], 16)
                            sp.dma_start(attr_h[:, k, :], attr_dram[:, cols]).then_inc(h_row[k], 16)
                    steps(sp, step)

                @block.gpsimd
                def _(pool):
                    def step(turn, k):
                        g, x, o = at(turn, k, 0), at(turn, k, 3), at(turn, k, 6)
                        if g.real:
                            need(pool, h_T, g.n - 3)
                            need(pool, S["v"], late(g).n - 3)
                            for c, table in enumerate((idx_src, idx_dst)):
                                pool.tensor_copy(get_ix[:, k, QUAD * c:QUAD * (c + 1)],
                                                 table[:, bass.ds(g.n * QUAD, QUAD)]).then_inc(h_ix, 1)
                            pool.wait_ge(h_ix, 2 * (g.n + 1))
                        if o.real:
                            need(pool, h_put[o.slot], 64 * o.turn)
                            pool.tensor_copy(out_ix[:, o.slot, :], idx_put[:, bass.ds(o.n * QUAD, QUAD)]).then_inc(h_oix, 1)
                            pool.wait_ge(h_oix, o.n + 1)
                            pool.wait_ge(S["out"], late(o).n + 1)
                        if x.real:
                            tail_pool(pool, late(x), S, B2, h_T, (x.n + 1, xd_r[:, x.slot]))
                        if g.real:
                            for c, rows_to in enumerate((xs_r, xd_r)):
                                for j in range(QUAD):
                                    pool.indirect_dma_start(
                                        rows_to[:, k, j, :], None, x1_dram[:, :],
                                        bass.IndirectOffsetOnAxis(ap=get_ix[:, k, QUAD * c + j:QUAD * c + j + 1], axis=0)
                                    ).then_inc(h_got[k], 16)
                        if o.real:
                            for j in range(QUAD):
                                pool.indirect_dma_start(
                                    out[:, :], bass.IndirectOffsetOnAxis(ap=out_ix[:, o.slot, j:j + 1], axis=0),
                                    o_e[:, o.slot, j, :], None, bounds_check=N - 1, oob_is_err=False).then_inc(h_put[o.slot], 16)
                    steps(pool, step)
                    for slot in range(4):
                        pool.wait_ge(h_put[slot], 64 * ((EG + 3 - slot) // 4))

                @block.tensor
                def _(pe):
                    def step(turn, k):
                        g = at(turn, k, 1)
                        if g.real:
                            pe.wait_ge(h_got[g.slot], 128 * (g.turn + 1))
                            need(pe, h_t, 2 * g.n)
                            for to, frm in ((qS, xs_r), (qD, xd_r)):
                                for j in range(QUAD):
                                    ins = pe.transpose(to[:, j * P:(j + 1) * P], frm[:, g.slot, j, :], ident[:, :])
                            ins.then_inc(h_T, 1)
                        g = at(turn, k, 2)
                        if g.real:
                            pe.wait_ge(h_t, 2 * (g.n + 1))
                            pe.wait_ge(h_row[g.slot], 48 * (g.turn + 1))
                            need(pe, h_msg, g.n)
                            pe.matmul(qH[:, :], w_m1s[:, :], xs_t[:, g.slot, :], start=True, stop=False)
                            pe.matmul(qH[:, :], w_m1d[:, :], xd_t[:, g.slot, :], start=False, stop=False)
                            pe.matmul(qH[:, :], w_m1a[:, :], attr_h[:, g.slot, :], start=False, stop=True).then_inc(h_H, 1)
                        g = at(turn, k, 3)
                        if g.real:
                            pe.wait_ge(h_mean, g.n + 1)
                            need(pe, h_up, g.n)
                            pe.matmul(qU[:, :], w_u1x[:, :], xd_t[:, g.slot, :], start=True, stop=False)
                            pe.matmul(qU[:, :], w_u1m[:, :], mean_t[:, g.slot % 2, :], start=False, stop=True).then_inc(h_U, 1)
                        g = at(turn, k, 4)
                        if g.real:
                            pe.wait_ge(h_up, g.n + 1)
                            need(pe, S["v"], late(g).n)
                            pe.matmul(qV[:, :], ones_b[:, :], u2b3[:, :].unsqueeze(1).broadcast_to([P, QUAD, F]),
                                      start=True, stop=False)
                            for j in range(QUAD):
                                ins = pe.matmul(qV[:, j * F:(j + 1) * F], up_t[:, g.slot % 2, j * P:(j + 1) * P],
                                                w_u2[:, :], start=False, stop=(j == QUAD - 1))
                            ins.then_inc(h_V, 1)
                    steps(pe, step)

                @block.scalar
                def _(act):
                    def step(turn, k):
                        g = at(turn, k, 5)
                        if g.real:
                            root(act, late(g), S, B2, 3)
                        g = at(turn, k, 1)
                        if g.real:
                            act.wait_ge(h_T, g.n + 1)
                            need(act, h_H, g.n - 3)
                            need(act, h_U, g.n - 3)
                            act.copy(xs_t[:, g.slot, :], qS[:, :]).then_inc(h_t, 1)
                            act.copy(xd_t[:, g.slot, :], qD[:, :]).then_inc(h_t, 1)
                        g = at(turn, k, 2)
                        if g.real:
                            act.wait_ge(h_H, g.n + 1)
                            need(act, h_sum, g.n - 1)
                            act.activation(msg_t[:, g.slot % 2, :], qH[:, :], ACT.Relu, bias=m1_bias[:, 0:1]).then_inc(h_msg, 1)
                        g = at(turn, k, 3)
                        if g.real:
                            act.wait_ge(h_U, g.n + 1)
                            need(act, h_V, g.n - 1)
                            act.activation(up_t[:, g.slot % 2, :], qU[:, :], ACT.Relu, bias=u1m_bias[:, 0:1]).then_inc(h_up, 1)
                        g = at(turn, k, 4)
                        if g.real:
                            root(act, late(g), S, B2, 2)
                        g = at(turn, k, 5)
                        if g.real:
                            need(act, h_put[g.slot], 64 * g.turn)
                            tail_scalar_out(act, late(g), S, B2, o_e[:, g.slot])
                    steps(act, step)

                @block.vector
                def _(dve):
                    def step(turn, k):
                        m, a, f = at(turn, k, 2), at(turn, k, 4), at(turn, k, 5)
                        if a.real:
                            tail_vector_add(dve, late(a), S, B2, qV, h_V, a.n + 1, xd_r[:, a.slot])
                            tail_vector_stats2(dve, late(a), S, B2)
                            tail_vector_means2(dve, late(a), S, B2)
                        if f.real:
                            tail_vector_rs3(dve, late(f), S, B2)
                        if m.real:
                            dve.wait_ge(h_msg, m.n + 1)
                            dve.wait_ge(h_row[m.slot], 48 * (m.turn + 1))
                            first = isinstance(m.n, int) and m.n == 0
                            if not first:
                                dve.wait_ge(h_sum, m.n)
                            dve.tensor_tensor_scan(sum_t[:, m.slot % 2, :], same_h[:, m.slot, :], msg_t[:, m.slot % 2, :],
                                                   0.0 if first else sum_t[:, (m.slot + 1) % 2, GROUP - 1:GROUP],
                                                   ALU.mult, ALU.add).then_inc(h_sum, 1)
                            dve.wait_ge(h_sum, m.n + 1)
                            need(dve, h_U, m.n - 1)
                            dve.tensor_tensor(mean_t[:, m.slot % 2, :], sum_t[:, m.slot % 2, :], rcnt_h[:, m.slot, :],
                                              ALU.mult).then_inc(h_mean, 1)
                        if a.real:
                            need(dve, S["out"], late(a).n - 1)
                            tail_vector_scale(dve, late(a), S, B2)
                            tail_vector_y(dve, late(a), S, B2)
                            tail_vector_stats3(dve, late(a), S, B2)
                    steps(dve, step)


_INS = ['x', 'src', 'dst', 'edge_attr_2', 'edge_type_4', 'L0_gnn_W_rel', 'L0_gnn_att_src_rel', 'L0_gnn_att_dst_rel',
        'L0_gnn_bias_rel', 'L0_gnn_W_self', 'L0_gnn_W_cross', 'L0_gnn_att_src_lang', 'L0_gnn_att_dst_lang',
        'L0_gnn_bias_lang', 'L1_gnn_mW1', 'L1_gnn_mb1', 'L1_gnn_mW2', 'L1_gnn_mb2', 'L1_gnn_uW1', 'L1_gnn_ub1',
        'L1_gnn_uW2', 'L1_gnn_ub2', 'L1_gnn_gamma', 'L1_gnn_beta']


def kernel(**inputs):
    import numpy as _np
    import concourse.bacc as _bacc
    from concourse import mybir as _mybir
    from concourse.bass_utils import run_bass_kernel_spmd as _run

    nc = _bacc.Bacc("TRN2", target_bir_lowering=False, num_devices=1)
    arrays, args = {}, []
    for name in _INS:
        a = _np.ascontiguousarray(inputs[name])
        arrays[f"in_{name}_dram"] = a
        args.append(nc.dram_tensor(f"in_{name}_dram", a.shape, _mybir.dt.from_np(a.dtype), kind="ExternalInput").ap())
    x = arrays["in_x_dram"]
    args.append(nc.dram_tensor("out_0_dram", x.shape, _mybir.dt.from_np(x.dtype), kind="ExternalOutput").ap())
    build(nc, *args)
    r = _run(nc, [arrays], core_ids=[0])
    return r.results[0]["out_0_dram"]
```

```python
from contextlib import ExitStack
from collections import namedtuple

import concourse.bass as bass
from concourse import mybir

P = 128
QUAD = 4
F32 = mybir.dt.float32
BF16 = mybir.dt.bfloat16
I32 = mybir.dt.int32
ALU = mybir.AluOpType
ACT = mybir.ActivationFunctionType
AX_X = mybir.AxisListType.X
LN_EPS = 1e-5
SLOPE = 0.2
NEG = -1e30

Group = namedtuple("Group", "n turn slot real")


def need(eng, sem, value):
    if not isinstance(value, int) or value > 0:
        eng.wait_ge(sem, value)


def behind(turn, k, unroll, offset, total, first=0):
    t, slot = turn + (k - offset) // unroll, (k - offset) % unroll
    n = unroll * t + slot + first
    real = 0 <= n < total if isinstance(n, int) else True
    return Group(n, t, slot, real)


def split(v):
    return v.rearrange("p (j f) -> p j f", j=QUAD)


def build(nc, x, src, dst, edge_attr, edge_type, W_rel, a_src_rel, a_dst_rel, b_rel, W_self, W_cross,
          a_src_lang, a_dst_lang, b_lang, mW1, mb1, mW2, mb2, uW1, ub1, uW2, ub2, gamma, beta, out):
    N, F = x.shape
    E = src.shape[0]
    R, H, D = a_src_rel.shape
    RH = R * H
    K5 = R + 1
    EB = F + H
    GROUP = QUAD * P
    SUPER = 2 * GROUP
    SUPERS = -(-N // SUPER)
    GROUPS = 2 * SUPERS
    TAIL = N - SUPER
    SKIP = ((SUPERS - 1) * SUPER - TAIL) // 8
    BLOCKS = P // RH
    BT = -(-E // (P * BLOCKS))
    TILES = BLOCKS * BT
    EP = TILES * P
    EG = TILES // QUAD
    BE = BT * P
    FULL = E // P
    REST = E - FULL * P
    assert F == P and H * D == F and RH * BLOCKS == P and TILES % QUAD == 0 and TILES <= P
    assert SUPERS == 2 * (EG - 1) + 1 and N < 2 ** 24 and ((SUPERS - 1) * SUPER - TAIL) % 8 == 0

    x1_dram = nc.dram_tensor("x1_rows", (N, F), F32, kind="Internal").ap()
    same_dram = nc.dram_tensor("same_run", (EP,), F32, kind="Internal").ap()
    last_dram = nc.dram_tensor("last_of_run", (EP,), F32, kind="Internal").ap()
    more_dram = nc.dram_tensor("more_of_run", (EP,), F32, kind="Internal").ap()
    reached_dram = nc.dram_tensor("reached_rows", (EP, F), F32, kind="Internal").ap()
    attr_dram = nc.dram_tensor("attr_t", (2, EP), F32, kind="Internal").ap()
    rcnt_dram = nc.dram_tensor("inverse_count", (BLOCKS, BE), F32, kind="Internal").ap()

    whole = ExitStack()
    with whole:
        def sb(name, shape, dt=F32, ctx=whole):
            return ctx.enter_context(nc.sbuf_tensor(name, shape, dt))

        def sem(name):
            return whole.enter_context(nc.semaphore(name))

        bank = [whole.enter_context(nc.psum_tensor(f"bank{i}", [P, 512], F32)) for i in range(8)]

        ident = sb("ident", [P, P])
        w_self_id = sb("w_self_id", [P, F])
        w_node = sb("w_node", [P, 2 * EB])
        w_rel = sb("w_rel", [P, R * F])
        w_log_s = sb("w_log_s", [P, RH])
        w_log_d = sb("w_log_d", [P, RH])
        w_cross = sb("w_cross", [P, EB])
        w_m1s = sb("w_m1s", [P, F])
        w_m1d = sb("w_m1d", [P, F])
        w_m1a = sb("w_m1a", [2, F])
        w_u1x = sb("w_u1x", [P, F])
        w_u1m = sb("w_u1m", [P, F])
        w_u2 = sb("w_u2", [P, F])
        rel_bias = sb("rel_bias", [P, R])
        m1_bias = sb("m1_bias", [P, 1])
        u1_bias = sb("u1_bias", [P, 1])
        u1m_bias = sb("u1m_bias", [P, 1])
        gamma_b = sb("gamma_b", [P, F])
        beta_b = sb("beta_b", [P, F])
        eps_col = sb("eps_col", [P, 1])
        ones_b = sb("ones_b", [P, P], BF16)
        lang3 = sb("lang3", [P, F], BF16)
        lang3c = sb("lang3c", [P, F], BF16)
        u2b3 = sb("u2b3", [P, F], BF16)
        beta3 = sb("beta3", [P, F], BF16)
        idx_src = sb("idx_src", [P, TILES], I32)
        idx_dst = sb("idx_dst", [P, TILES], I32)
        idx_last = sb("idx_last", [P, TILES], I32)
        idx_first = sb("idx_first", [P, TILES], I32)
        last_e = sb("last_e", [P, TILES])
        off_rel = sb("off_rel", [P, TILES * R])
        logit = sb("logit", [P, TILES * RH])
        absent = sb("absent", [P, TILES * R])
        edges_only = whole.enter_context(ExitStack())
        src_t = sb("src_t", [P, EP], F32, edges_only)
        dst_t = sb("dst_t", [P, EP], F32, edges_only)

        with ExitStack() as ctx:
            w_self = sb("w_self", [P, F], F32, ctx)
            w_m2 = sb("w_m2", [P, F], F32, ctx)
            w_m2t = sb("w_m2t", [P, F], F32, ctx)
            w_u1b = sb("w_u1b", [P, F], F32, ctx)
            mb2_col = sb("mb2_col", [P, 1], F32, ctx)
            a_s = sb("a_s", [P, R * F], F32, ctx)
            a_d = sb("a_d", [P, R * F], F32, ctx)
            al_s = sb("al_s", [P, F], F32, ctx)
            al_d = sb("al_d", [P, F], F32, ctx)
            bias2 = sb("bias2", [P, 4, F], F32, ctx)
            part = sb("part", [P, 3, 4, F], BF16, ctx)
            left = sb("left", [P, 2, 4, F], F32, ctx)
            w_u2_raw = sb("w_u2_raw", [P, F], F32, ctx)
            w_sum = sb("w_sum", [P, F], F32, ctx)
            means4 = sb("means4", [P, 4], F32, ctx)
            prod = sb("prod", [P, 5, R * F], F32, ctx)
            rows_i = sb("rows_i", [P, 5, P], I32, ctx)
            rows = sb("rows", [P, 5, P], F32, ctx)
            flags = sb("flags", [P, 6, P], F32, ctx)
            attr = sb("attr", [P, 2 * P], F32, ctx)
            attr2 = sb("attr2", [P, 2, P], F32, ctx)
            type_e = sb("type_e", [P, TILES], F32, ctx)
            s_weights = sem("s_weights")
            s_ident0 = sem("s_ident0")
            s_ident = sem("s_ident")
            s_pads = sem("s_pads")
            s_rows = sem("s_rows")
            s_const = sem("s_const")
            s_centre = sem("s_centre")
            s_split = sem("s_split")
            s_prod = sem("s_prod")
            s_rowsf = sem("s_rowsf")
            s_flags = sem("s_flags")
            s_scratch = sem("s_scratch")
            s_tabs = sem("s_tabs")
            s_taken = sem("s_taken")
            s_type = sem("s_type")
            s_m2t = sem("s_m2t")
            s_m2ts = sem("s_m2ts")
            s_fold = sem("s_fold")
            s_done = sem("s_done")

            def row_of(v):
                return v.unsqueeze(0)

            loads = [
                (w_self[:, :], W_self), (w_rel[:, :].rearrange("i (r o) -> i r o", r=R), W_rel.rearrange("r i o -> i r o")),
                (w_cross[:, 0:F], W_cross), (w_m1s[:, :], mW1[0:F, :]), (w_m1d[:, :], mW1[F:2 * F, :]),
                (w_m1a[:, :], mW1[2 * F:2 * F + 2, :]), (w_m2[:, :], mW2), (w_u1x[:, :], uW1[0:F, :]),
                (w_u1b[:, :], uW1[F:2 * F, :]), (w_u2_raw[:, :], uW2),
                (m1_bias[:, :], mb1.unsqueeze(1)), (u1_bias[:, :], ub1.unsqueeze(1)), (mb2_col[:, :], mb2.unsqueeze(1)),
                (gamma_b[:, :], row_of(gamma).broadcast_to([P, F])), (beta_b[:, :], row_of(beta).broadcast_to([P, F])),
                (al_s[:, :], row_of(a_src_lang.rearrange("h d -> (h d)")).broadcast_to([P, F])),
                (al_d[:, :], row_of(a_dst_lang.rearrange("h d -> (h d)")).broadcast_to([P, F])),
                (a_s[:, :], row_of(a_src_rel.rearrange("r h d -> (r h d)")).broadcast_to([P, R * F])),
                (a_d[:, :], row_of(a_dst_rel.rearrange("r h d -> (r h d)")).broadcast_to([P, R * F])),
                (bias2[:, 0, :], row_of(b_lang).broadcast_to([P, F])), (bias2[:, 1, :], row_of(ub2).broadcast_to([P, F])),
                (bias2[:, 2, :], row_of(b_lang).broadcast_to([P, F])), (bias2[:, 3, :], row_of(beta).broadcast_to([P, F])),
            ] + [(rel_bias[:, r:r + 1], b_rel[r, :].unsqueeze(1)) for r in range(R)]

            def tiled(v, start, count):
                return v[start:start + count * P].rearrange("(t p) -> t p", p=P)

            n_loads = 0
            with nc.Block() as block:
                @block.sync
                def _(sp):
                    for dest, source in loads:
                        sp.dma_start(dest, source).then_inc(s_weights, 16)

                @block.scalar
                def _(act):
                    act.wait_ge(s_pads, 6)
                    for kind, v in ((0, src), (1, edge_type), (2, dst)):
                        act.dma_start(rows_i[0:FULL, kind, :], tiled(v, 0, FULL)).then_inc(s_rows, 16)
                        act.dma_start(rows_i[FULL:FULL + 1, kind, 0:REST], row_of(v[FULL * P:E])).then_inc(s_rows, 16)
                    act.dma_start(rows_i[0:1, 3, 1:P], row_of(dst[0:P - 1])).then_inc(s_rows, 16)
                    act.dma_start(rows_i[1:FULL, 3, :], tiled(dst, P - 1, FULL - 1)).then_inc(s_rows, 16)
                    act.dma_start(rows_i[FULL:FULL + 1, 3, 0:REST + 1], row_of(dst[FULL * P - 1:E])).then_inc(s_rows, 16)
                    act.dma_start(rows_i[0:FULL, 4, :], tiled(dst, 1, FULL)).then_inc(s_rows, 16)
                    act.dma_start(rows_i[FULL:FULL + 1, 4, 0:REST - 1], row_of(dst[FULL * P + 1:E])).then_inc(s_rows, 16)
                    act.dma_start(attr[0:FULL, :], edge_attr[0:FULL * P, :].rearrange("(t p) c -> t (p c)", p=P)).then_inc(s_rows, 16)
                    act.dma_start(attr[FULL:FULL + 1, 0:2 * REST],
                                  row_of(edge_attr[FULL * P:E, :].rearrange("p c -> (p c)"))).then_inc(s_rows, 16)

                @block.gpsimd
                def _(pool):
                    for kind, value in ((0, 0), (1, 0), (2, N), (3, N), (4, N + 1)):
                        pool.memset(rows_i[:, kind, :], value).then_inc(s_pads, 1)
                    pool.memset(attr[:, :], 0.0).then_inc(s_pads, 1)
                    pool.memset(ident[:, :], 0.0).then_inc(s_ident0, 1)
                    pool.wait_ge(s_ident0, 1)
                    pool.affine_select(out=ident[:, :], in_=ident[:, :], compare_op=ALU.not_equal, fill=1.0, base=0,
                                       pattern=[[-1, P]], channel_multiplier=1).then_inc(s_ident, 1)
                    pool.memset(ones_b[:, :], 1.0).then_inc(s_const, 1)
                    pool.memset(eps_col[:, :], LN_EPS).then_inc(s_const, 1)
                    pool.memset(lang3[:, :], 0.0).then_inc(s_const, 1)
                    pool.memset(lang3c[:, :], 0.0).then_inc(s_const, 1)
                    pool.memset(u2b3[:, :], 0.0).then_inc(s_const, 1)
                    pool.memset(beta3[:, :], 0.0).then_inc(s_const, 1)

            ROW_LOADS = 13
            with nc.Block() as block:
                @block.vector
                def _(dve):
                    dve.wait_ge(s_rows, 16 * ROW_LOADS)
                    dve.tensor_copy(rows[:, :, :], rows_i[:, :, :]).then_inc(s_rowsf, 1)
                    dve.tensor_copy(attr2[:, :, :], attr[:, :].rearrange("t (p c) -> t c p", c=2)).then_inc(s_rowsf, 1)
                    dve.wait_ge(s_rowsf, 2)
                    dve.tensor_tensor(flags[:, 0, :], rows[:, 2, :], rows[:, 3, :], ALU.is_equal).then_inc(s_flags, 1)
                    dve.tensor_tensor(flags[:, 1, :], rows[:, 2, :], rows[:, 4, :], ALU.not_equal).then_inc(s_flags, 1)
                    dve.tensor_scalar(flags[:, 2, :], rows[:, 2, :], float(N - 1), None, ALU.min).then_inc(s_flags, 1)
                    dve.wait_ge(s_flags, 3)
                    dve.scalar_tensor_tensor(flags[:, 3, :], rows[:, 2, :], float(N), flags[:, 1, :],
                                             ALU.subtract, ALU.mult).then_inc(s_flags, 1)
                    dve.tensor_scalar(flags[:, 4, :], flags[:, 0, :], -1.0, 1.0, ALU.mult, ALU.add).then_inc(s_flags, 1)
                    dve.tensor_scalar(flags[:, 5, :], flags[:, 1, :], -1.0, 1.0, ALU.mult, ALU.add).then_inc(s_flags, 1)
                    dve.wait_ge(s_flags, 6)
                    dve.scalar_tensor_tensor(flags[:, 4, :], rows[:, 2, :], float(N), flags[:, 4, :],
                                             ALU.subtract, ALU.mult).then_inc(s_flags, 1)
                    dve.wait_ge(s_flags, 7)
                    dve.tensor_scalar(flags[:, 3:5, :], flags[:, 3:5, :], float(N), None, ALU.add).then_inc(s_flags, 1)
                    dve.wait_ge(s_weights, 16 * len(loads))
                    dve.wait_ge(s_ident, 1)
                    dve.tensor_tensor(w_sum[:, :], w_self[:, :], ident[:, :], ALU.add).then_inc(s_centre, 1)
                    dve.wait_ge(s_centre, 1)
                    centred = [(w_sum[:, :], w_self_id[:, :]), (w_u2_raw[:, :], w_u2[:, :]),
                               (bias2[:, 1, :], bias2[:, 1, :]), (bias2[:, 2, :], bias2[:, 2, :])]
                    for n, (v, _) in enumerate(centred):
                        dve.tensor_reduce(means4[:, n:n + 1], v, AX_X, ALU.add).then_inc(s_centre, 1)
                    dve.wait_ge(s_centre, 5)
                    dve.tensor_scalar(means4[:, :], means4[:, :], 1.0 / F, None, ALU.mult).then_inc(s_centre, 1)
                    dve.wait_ge(s_centre, 6)
                    for n, (v, dest) in enumerate(centred):
                        dve.tensor_scalar(dest, v, means4[:, n:n + 1], None, ALU.subtract).then_inc(s_centre, 1)
                    dve.wait_ge(s_centre, 10)
                    dve.tensor_copy(part[:, 0], bias2[:, :, :]).then_inc(s_split, 1)
                    dve.wait_ge(s_split, 1)
                    dve.tensor_tensor(left[:, 0], bias2[:, :, :], part[:, 0], ALU.subtract).then_inc(s_split, 1)
                    dve.wait_ge(s_split, 2)
                    dve.tensor_copy(part[:, 1], left[:, 0]).then_inc(s_split, 1)
                    dve.wait_ge(s_split, 3)
                    dve.tensor_tensor(left[:, 1], left[:, 0], part[:, 1], ALU.subtract).then_inc(s_split, 1)
                    dve.wait_ge(s_split, 4)
                    dve.tensor_copy(part[:, 2], left[:, 1]).then_inc(s_split, 1)
                    dve.wait_ge(s_split, 5)
                    dve.wait_ge(s_const, 6)
                    for k in range(3):
                        for b, dest in ((0, lang3), (1, u2b3), (2, lang3c), (3, beta3)):
                            dve.tensor_copy(dest[32 * k:32 * k + 1, :], part[32 * k:32 * k + 1, k, b, :]).then_inc(s_done, 1)
                    pairs = [(w_rel[:, :], a_s[:, :], w_log_s[:, :], R * F), (w_rel[:, :], a_d[:, :], w_log_d[:, :], R * F),
                             (w_cross[:, 0:F], al_s[:, :], w_cross[:, F:EB], F),
                             (w_self[:, :], al_s[:, :], w_node[:, F:EB], F),
                             (w_self[:, :], al_d[:, :], w_node[:, EB + F:2 * EB], F)]
                    for n, (w, a, _, size) in enumerate(pairs):
                        dve.tensor_tensor(prod[:, n, 0:size], w, a, ALU.mult).then_inc(s_prod, 1)
                    for n, (_, _, dest, size) in enumerate(pairs):
                        dve.wait_ge(s_prod, n + 1)
                        dve.tensor_reduce(dest, prod[:, n, 0:size].rearrange("p (h d) -> p h d", d=D), AX_X, ALU.add).then_inc(s_done, 1)
                    dve.tensor_copy(w_node[:, 0:F], w_self[:, :]).then_inc(s_done, 1)
                    dve.tensor_copy(w_node[:, EB:EB + F], ident[:, :]).then_inc(s_done, 1)
                    dve.wait_ge(s_tabs, 6)
                    for k, dest in enumerate((idx_src, idx_dst, idx_last, idx_first, type_e, last_e)):
                        dve.tensor_copy(dest[:, :], bank[4 * (k // 4)][:, (k % 4) * P:(k % 4) * P + TILES]).then_inc(s_type, 1)
                    dve.wait_ge(s_type, 6)
                    for r in range(R):
                        dve.tensor_scalar(off_rel[:, r::R], type_e[:, :], float(r), NEG, ALU.not_equal, ALU.mult).then_inc(s_done, 1)
                    dve.wait_ge(s_m2t, 1)
                    dve.tensor_copy(w_m2t[:, :], bank[1][:, 0:F]).then_inc(s_m2ts, 1)
                    dve.wait_ge(s_fold, 2)
                    dve.tensor_copy(w_u1m[:, :], bank[2][:, 0:F]).then_inc(s_done, 1)
                    dve.tensor_tensor(u1m_bias[:, :], bank[3][:, 0:1], u1_bias[:, :], ALU.add).then_inc(s_done, 1)

                @block.tensor
                def _(pe):
                    pe.wait_ge(s_ident, 1)
                    pe.wait_ge(s_flags, 8)
                    for k, table in enumerate((rows[:, 0, :], flags[:, 2, :], flags[:, 3, :], flags[:, 4, :],
                                               rows[:, 1, :], flags[:, 1, :])):
                        pe.transpose(bank[4 * (k // 4)][:, (k % 4) * P:(k % 4 + 1) * P], table, ident[:, :]).then_inc(s_tabs, 1)
                    pe.wait_ge(s_weights, 16 * len(loads))
                    pe.transpose(bank[1][:, 0:F], w_m2[:, :], ident[:, :]).then_inc(s_m2t, 1)
                    pe.wait_ge(s_m2ts, 1)
                    pe.matmul(bank[2][:, 0:F], w_m2t[:, :], w_u1b[:, :], start=True, stop=True).then_inc(s_fold, 1)
                    pe.matmul(bank[3][:, 0:1], w_u1b[:, :], mb2_col[:, :], start=True, stop=True).then_inc(s_fold, 1)

                @block.sync
                def _(sp):
                    sp.wait_ge(s_flags, 6)
                    sp.dma_start(same_dram.rearrange("(t p) -> t p", p=P), flags[0:TILES, 0, :]).then_inc(s_scratch, 16)
                    sp.dma_start(last_dram.rearrange("(t p) -> t p", p=P), flags[0:TILES, 1, :]).then_inc(s_scratch, 16)
                    sp.dma_start(more_dram.rearrange("(t p) -> t p", p=P), flags[0:TILES, 5, :]).then_inc(s_scratch, 16)
                    for c in range(2):
                        sp.dma_start(attr_dram[c].rearrange("(t p) -> t p", p=P), attr2[0:TILES, c, :]).then_inc(s_scratch, 16)
                    sp.wait_ge(s_scratch, 80)

        ADD, SCALE, OUT = 5, 6, 7
        NORM1, NORM2, NORM3 = 0, 1, 2
        t_v, t_w, t_xb, t_y, t_nm, t_out = [sem("t_" + s) for s in ("sum", "gamma", "residual", "scaled", "shift", "out")]
        b_st = [sem(f"b_stats{i + 1}") for i in range(3)]
        b_half, b_spread, b_mv, b_sd, b_rs = [sem("b_" + s) for s in ("halves", "spread", "means", "deviation", "inverse")]
        BATCHES = GROUPS + SCALE

        def tail_buffers(tag, ctx):
            return {
                "v": sb(f"{tag}_v", [P, 2, QUAD, F], F32, ctx), "w": sb(f"{tag}_w", [P, 4, QUAD, F], F32, ctx),
                "xb": sb(f"{tag}_xb", [P, 2, QUAD, F], F32, ctx), "st": sb(f"{tag}_st", [P, 3, QUAD, 6], F32, ctx),
                "mid": sb(f"{tag}_mid", [P, 3, QUAD, 4], F32, ctx), "mv": sb(f"{tag}_mv", [P, 2, 3, QUAD, 2], F32, ctx),
                "sd": sb(f"{tag}_sd", [P, 3, QUAD], F32, ctx), "rs": sb(f"{tag}_rs", [P, 2, 3, QUAD], F32, ctx),
                "nm": sb(f"{tag}_nm", [P, 2, QUAD], F32, ctx)}

        def stats(dve, rows_in, st):
            for j in range(QUAD):
                ins = dve.bn_stats(st[:, j, :], rows_in[:, j, :])
            return ins

        def batch_means(dve, n, slot, B):
            st, mid, mv = B["st"], B["mid"], B["mv"][:, slot]
            dve.tensor_tensor(mid[:, :, :, 0:2], st[:, :, :, 1:3], st[:, :, :, 4:6], ALU.add).then_inc(b_half, 1)
            dve.tensor_tensor(mid[:, :, :, 2], st[:, :, :, 1], st[:, :, :, 4], ALU.subtract).then_inc(b_half, 1)
            dve.wait_ge(b_half, 2 * (n + 1))
            dve.scalar_tensor_tensor(mid[:, :, :, 3], mid[:, :, :, 2], F / 4.0, mid[:, :, :, 2], ALU.mult, ALU.mult).then_inc(b_spread, 1)
            dve.tensor_scalar(mv[:, :, :, 0], mid[:, :, :, 0], 0.5, None, ALU.mult).then_inc(b_mv, 1)
            dve.wait_ge(b_spread, n + 1)
            dve.tensor_tensor(mv[:, :, :, 1], mid[:, :, :, 3], mid[:, :, :, 1], ALU.add).then_inc(b_mv, 1)

        def batch_root(act, n, slot, B):
            need(act, b_rs, n)
            act.wait_ge(b_mv, 2 * (n + 1))
            act.activation(B["sd"][:, :, :], B["mv"][:, slot, :, :, 1], ACT.Sqrt, bias=eps_col[:, 0:1],
                           scale=1.0 / F).then_inc(b_sd, 1)

        def batch_inverse(dve, n, slot, B):
            dve.wait_ge(b_sd, n + 1)
            dve.reciprocal(B["rs"][:, slot], B["sd"][:, :, :]).then_inc(b_rs, 1)

        def tail_add(dve, g, B, pV, c_V, count, x1_rows):
            need(dve, t_w, g.n - 1)
            dve.wait_ge(c_V, count)
            dve.tensor_tensor(B["v"][:, g.slot % 2], split(pV[:, :]), x1_rows, ALU.add).then_inc(t_v, 1)

        def tail_shift(dve, g, n, slot, B):
            need(dve, t_out, g.n - 1)
            dve.wait_ge(b_rs, n + 1)
            dve.scalar_tensor_tensor(B["nm"][:, g.slot % 2, :], B["mv"][:, slot, NORM3, :, 0], -1.0, B["rs"][:, slot, NORM3, :],
                                     ALU.mult, ALU.mult).then_inc(t_nm, 1)

        def tail_scale(dve, g, n, slot, B, xb_rows, c_xb, count):
            dve.wait_ge(b_rs, n + 1)
            dve.wait_ge(t_w, g.n + 1)
            dve.wait_ge(c_xb, count)
            for j in range(QUAD):
                w = B["w"][:, g.slot, j, :]
                ins = dve.scalar_tensor_tensor(w, w, B["rs"][:, slot, NORM2, j:j + 1], xb_rows[:, j, :],
                                               ALU.mult, ALU.add)
            ins.then_inc(t_y, 1)

        def along(v):
            return v[:, :].unsqueeze(1).broadcast_to([P, QUAD, F])

        def tail_residual(pool, g, B, x1_rows):
            need(pool, t_y, g.n - 1)
            pool.tensor_tensor(B["xb"][:, g.slot % 2], x1_rows, along(beta_b), ALU.add).then_inc(t_xb, 1)

        def tail_gamma(pool, g, B):
            need(pool, t_out, g.n - 3)
            pool.wait_ge(t_v, g.n + 1)
            pool.tensor_tensor(B["w"][:, g.slot], B["v"][:, g.slot % 2], along(gamma_b), ALU.mult).then_inc(t_w, 1)

        def tail_out(act, g, slot, B, out_rows):
            act.wait_ge(t_nm, g.n + 1)
            for j in range(QUAD):
                ins = act.activation(out_rows[:, j, :], B["w"][:, g.slot, j, :], ACT.Identity,
                                     bias=B["nm"][:, g.slot % 2, j:j + 1], scale=B["rs"][:, slot, NORM3, j:j + 1])
            ins.then_inc(t_out, 1)

        with ExitStack() as ctx:
            x_in = sb("x_in", [P, 2, 8 * F], F32, ctx)
            x_t = sb("x_t", [P, 2, GROUP], F32, ctx)
            x1 = sb("x1", [P, 2, 8, F], F32, ctx)
            x1_t = sb("x1_t", [P, 2, GROUP], F32, ctx)
            hid_t = sb("hid_t", [P, 2, GROUP], F32, ctx)
            o_out = sb("o_out", [P, 2, 8, F], F32, ctx)
            B = tail_buffers("n", ctx)
            e_rows = sb("e_rows", [P, 2 * QUAD, F], F32, ctx)
            e_idx = sb("e_idx", [P, 2 * QUAD], I32, ctx)
            e_t = sb("e_t", [P, 2, GROUP], F32, ctx)
            l_low = sb("l_low", [P, QUAD * RH], F32, ctx)
            l_leaky = sb("l_leaky", [P, QUAD * RH], F32, ctx)
            pT, pS, pX, pU, pV, pE, pL = bank[0], bank[1:3], bank[3], bank[4], bank[5], bank[6], bank[7]

            s_x = [sem(f"s_x{i}") for i in range(2)]
            s_x1 = [sem(f"s_x1out{i}") for i in range(2)]
            s_out = [sem(f"s_out{i}") for i in range(2)]
            c_zero, c_T, c_xt, c_S, c_x1, c_X, c_x1t, c_U, c_hid, c_V = [sem("c_" + s) for s in (
                "zero", "T", "xt", "S", "x1", "X", "x1t", "U", "hid", "V")]
            e_got = [sem(f"e_got{i}") for i in range(2)]
            e_ix, e_T, e_ts, e_kept, e_L, e_low, e_lk, e_log = [sem("e_" + s) for s in (
                "ix", "T", "ts", "kept", "L", "low", "lk", "log")]

            def rows_of(buf, g):
                return buf[:, g.slot // 2, 4 * (g.slot % 2):4 * (g.slot % 2) + 4, :]

            def steps(eng, step):
                for turn in (0, 1):
                    for k in range(4):
                        step(turn, k)
                with eng.Fori(2, EG - 1) as turn:
                    for k in range(4):
                        step(turn, k)
                for turn in (EG - 1, EG, EG + 1):
                    for k in range(4):
                        step(turn, k)

            def at(turn, k, offset):
                return behind(turn, k, 4, offset, GROUPS)

            def batch(turn, k, offset=0):
                n = 4 * turn + k - offset
                real = 0 <= n < BATCHES if isinstance(n, int) else True
                return n, (k - offset) % 2, real

            def turn_has_logits(turn):
                return not isinstance(turn, int) or 1 <= turn <= EG

            def has_edges(turn):
                return not isinstance(turn, int) or turn < EG

            with nc.Block() as block:
                @block.sync
                def _(sp):
                    def view(dram, turn, q):
                        s = 2 * turn + q
                        base = TAIL if isinstance(s, int) and s == SUPERS - 1 else s * SUPER
                        return dram[bass.ds(base, SUPER), :].rearrange("(p j) f -> p (j f)", p=P)

                    def load(turn, q):
                        if isinstance(turn, int) and 2 * turn + q >= SUPERS:
                            return
                        need(sp, c_T, 4 * turn + 2 * q - 2)
                        sp.dma_start(x_in[:, q, :], view(x, turn, q)).then_inc(s_x[q], 16)

                    def store(turn, q, buf, dram, ready, done):
                        if isinstance(turn, int) and not 0 <= 2 * turn + q < SUPERS:
                            return
                        sp.wait_ge(ready, 4 * turn + 2 * q + 2)
                        flat = buf[:, q].rearrange("p j f -> p (j f)")
                        to = view(dram, turn, q)
                        if isinstance(turn, int) and 2 * turn + q == SUPERS - 1:
                            for lo, hi in ((SKIP, 32), (32, P)):
                                sp.dma_start(to[lo:hi, :], flat[lo:hi, :]).then_inc(done[q], 16)
                        else:
                            sp.dma_start(to, flat).then_inc(done[q], 16)

                    def turn_of(turn):
                        load(turn + 1, 0)
                        store(turn, 0, x1, x1_dram, c_x1, s_x1)
                        store(turn - 1, 0, o_out, out, t_out, s_out)
                        load(turn + 1, 1)
                        store(turn, 1, x1, x1_dram, c_x1, s_x1)
                        store(turn - 1, 1, o_out, out, t_out, s_out)
                    load(0, 0)
                    load(0, 1)
                    turn_of(0)
                    turn_of(1)
                    with sp.Fori(2, EG - 2) as turn:
                        turn_of(turn)
                    for turn in range(EG - 2, EG + 1):
                        turn_of(turn)
                    for q in range(2):
                        count = 16 * (EG - 1) + (32 if q == 0 else 0)
                        sp.wait_ge(s_x1[q], count)
                        sp.wait_ge(s_out[q], count)

                @block.gpsimd
                def _(pool):
                    def indices(e, half):
                        need(pool, e_T, 2 * e + half - 1)
                        pool.tensor_copy(e_idx[:, 4 * half:4 * half + 4],
                                         (idx_src, idx_dst)[half][:, bass.ds(e * QUAD, QUAD)]).then_inc(e_ix, 1)
                        pool.wait_ge(e_ix, 2 * e + half + 1)

                    def gather(half):
                        for j in range(4 * half, 4 * half + 4):
                            pool.indirect_dma_start(e_rows[:, j, :], None, x[:, :],
                                                    bass.IndirectOffsetOnAxis(ap=e_idx[:, j:j + 1], axis=0)).then_inc(e_got[half], 16)

                    pool.memset(B["st"][:, :, :, :], 0.0).then_inc(c_zero, 1)

                    for half in range(2):
                        indices(0, half)
                        gather(half)

                    def step(turn, k):
                        ahead = has_edges(turn + 1) and k >= 2
                        if ahead:
                            indices(turn + 1, k - 2)
                        g = at(turn, k, ADD)
                        if g.real:
                            pool.wait_ge(c_x1, g.n + 1)
                            tail_residual(pool, g, B, rows_of(x1, g))
                        if ahead:
                            gather(k - 2)
                        if g.real:
                            tail_gamma(pool, g, B)
                    steps(pool, step)

                @block.tensor
                def _(pe):
                    def step(turn, k):
                        g = at(turn, k, ADD)
                        if g.real:
                            pe.wait_ge(c_hid, g.n + 1)
                            need(pe, t_v, g.n)
                            pe.matmul(pV[:, :], ones_b[:, :], along(u2b3), start=True, stop=False)
                            for j in range(QUAD):
                                ins = pe.matmul(pV[:, j * F:(j + 1) * F], hid_t[:, g.slot % 2, j * P:(j + 1) * P],
                                                w_u2[:, :], start=False, stop=(j == QUAD - 1))
                            ins.then_inc(c_V, 1)
                        g = at(turn, k, 4)
                        if g.real:
                            pe.wait_ge(c_x1t, g.n + 1)
                            need(pe, c_hid, g.n)
                            pe.matmul(pU[:, :], w_u1x[:, :], x1_t[:, g.slot % 2, :], start=True, stop=True).then_inc(c_U, 1)
                        g = at(turn, k, 1)
                        if g.real:
                            pe.wait_ge(c_xt, g.n + 1)
                            need(pe, c_x1, g.n - 1)
                            to = pS[g.slot % 2]
                            pe.matmul(to[:, :], ones_b[:, :], along(lang3c), start=True, stop=False)
                            for j in range(QUAD):
                                ins = pe.matmul(to[:, j * F:(j + 1) * F], x_t[:, g.slot % 2, j * P:(j + 1) * P],
                                                w_self_id[:, :], start=False, stop=(j == QUAD - 1))
                            ins.then_inc(c_S, 1)
                        g = at(turn, k, 0)
                        if g.real:
                            pe.wait_ge(s_x[g.slot // 2], 16 * (g.turn + 1))
                            need(pe, c_xt, g.n)
                            for j in range(QUAD):
                                r = 4 * (g.slot % 2) + j
                                ins = pe.transpose(pT[:, j * P:(j + 1) * P], x_in[:, g.slot // 2, r * F:(r + 1) * F], ident[:, :])
                            ins.then_inc(c_T, 1)
                        g = at(turn, k, 3)
                        if g.real:
                            pe.wait_ge(c_x1, g.n + 1)
                            need(pe, c_x1t, g.n)
                            for j in range(QUAD):
                                ins = pe.transpose(pX[:, j * P:(j + 1) * P], rows_of(x1, g)[:, j, :], ident[:, :])
                            ins.then_inc(c_X, 1)
                        if has_edges(turn) and k in (1, 2):
                            pe.wait_ge(e_got[k - 1], 64 * (turn + 1))
                            need(pe, e_ts, 2 * turn + k - 1)
                            need(pe, e_kept, 2 * turn + k - 1)
                            for j in range(QUAD):
                                ins = pe.transpose(pE[:, j * P:(j + 1) * P], e_rows[:, QUAD * (k - 1) + j, :], ident[:, :])
                            ins.then_inc(e_T, 1)
                        if has_edges(turn) and k == 3:
                            pe.wait_ge(e_ts, 2 * turn + 2)
                            need(pe, e_low, turn)
                            need(pe, e_lk, turn)
                            for j in range(QUAD):
                                pe.matmul(pL[:, j * RH:(j + 1) * RH], e_t[:, 0, j * P:(j + 1) * P], w_log_s[:, :],
                                          start=True, stop=False)
                                ins = pe.matmul(pL[:, j * RH:(j + 1) * RH], e_t[:, 1, j * P:(j + 1) * P], w_log_d[:, :],
                                                start=False, stop=True)
                            ins.then_inc(e_L, 1)
                    steps(pe, step)

                @block.scalar
                def _(act):
                    def step(turn, k):
                        n, slot, real = batch(turn, k, 1)
                        if real:
                            batch_root(act, n, slot, B)
                        g = at(turn, k, 4)
                        if g.real:
                            act.wait_ge(c_U, g.n + 1)
                            need(act, c_V, g.n - 1)
                            act.activation(hid_t[:, g.slot % 2, :], pU[:, :], ACT.Relu, bias=u1_bias[:, 0:1]).then_inc(c_hid, 1)
                        g = at(turn, k, 0)
                        if g.real:
                            act.wait_ge(c_T, g.n + 1)
                            need(act, c_S, g.n - 1)
                            act.copy(x_t[:, g.slot % 2, :], pT[:, :]).then_inc(c_xt, 1)
                        if has_edges(turn) and k in (1, 2):
                            c = k - 1
                            act.wait_ge(e_T, 2 * turn + c + 1)
                            need(act, e_L, turn)
                            act.copy(e_t[:, c, :], pE[:, :]).then_inc(e_ts, 1)
                            act.copy((src_t, dst_t)[c][:, bass.ds(turn * GROUP, GROUP)], pE[:, :]).then_inc(e_kept, 1)
                        g = at(turn, k, 3)
                        if g.real:
                            act.wait_ge(c_X, g.n + 1)
                            need(act, c_U, g.n - 1)
                            act.copy(x1_t[:, g.slot % 2, :], pX[:, :]).then_inc(c_x1t, 1)
                        g, (n, slot, _) = at(turn, k, 2), batch(turn, k, 1)
                        if g.real:
                            act.wait_ge(b_rs, n + 1)
                            need(act, s_x1[g.slot // 2], 16 * g.turn)
                            need(act, t_xb, g.n - 3)
                            need(act, t_v, g.n - 3)
                            for j in range(QUAD):
                                ins = act.activation(rows_of(x1, g)[:, j, :], pS[g.slot % 2][:, j * F:(j + 1) * F], ACT.Copy,
                                                     scale=B["rs"][:, slot, NORM1, j:j + 1])
                            ins.then_inc(c_x1, 1)
                        g, (n, slot, _) = at(turn, k, OUT), batch(turn, k, 1)
                        if g.real:
                            need(act, s_out[g.slot // 2], 16 * g.turn)
                            tail_out(act, g, slot, B, rows_of(o_out, g))
                    steps(act, step)

                @block.vector
                def _(dve):
                    dve.wait_ge(c_zero, 1)

                    def step(turn, k):
                        b, a, c, f = at(turn, k, 1), at(turn, k, ADD), at(turn, k, SCALE), at(turn, k, OUT)
                        n, slot, real = batch(turn, k)
                        before, old, had = batch(turn, k, 1)

                        if real:
                            need(dve, b_half, 2 * n)
                        logits, before_e = k == 0 and turn_has_logits(turn), turn - 1
                        if a.real:
                            tail_add(dve, a, B, pV, c_V, a.n + 1, rows_of(x1, a))
                        if had:
                            need(dve, c_x1, min(before - 2, GROUPS) if isinstance(before, int) else before - 2)
                            need(dve, t_out, before - 7)
                            batch_inverse(dve, before, old, B)
                        if a.real:
                            dve.wait_ge(t_v, a.n + 1)
                            stats(dve, B["v"][:, a.slot % 2], B["st"][:, NORM2]).then_inc(b_st[NORM2], 1)
                        if f.real:
                            tail_shift(dve, f, before, old, B)
                        if logits:
                            dve.wait_ge(e_L, before_e + 1)
                            dve.tensor_scalar(l_low[:, :], pL[:, 0:QUAD * RH], SLOPE, None, ALU.mult).then_inc(e_low, 1)
                        if c.real:
                            tail_scale(dve, c, before, old, B, B["xb"][:, c.slot % 2], t_xb, c.n + 1)
                        if b.real:
                            dve.wait_ge(c_S, b.n + 1)
                            stats(dve, split(pS[b.slot % 2][:, :]), B["st"][:, NORM1]).then_inc(b_st[NORM1], 1)
                        if c.real:
                            dve.wait_ge(t_y, c.n + 1)
                            stats(dve, B["w"][:, c.slot], B["st"][:, NORM3]).then_inc(b_st[NORM3], 1)
                        if logits:
                            dve.wait_ge(e_low, before_e + 1)
                            dve.tensor_tensor(l_leaky[:, :], pL[:, 0:QUAD * RH], l_low[:, :], ALU.max).then_inc(e_lk, 1)
                        if real:
                            for norm, g in ((NORM1, b), (NORM2, a), (NORM3, c)):
                                if g.real:
                                    dve.wait_ge(b_st[norm], g.n + 1)
                            batch_means(dve, n, slot, B)
                        if logits:
                            dve.wait_ge(e_lk, before_e + 1)
                            dve.tensor_tensor(
                                logit[:, bass.ds(before_e * QUAD * RH, QUAD * RH)].rearrange("p (t h) -> p t h", h=H),
                                l_leaky[:, :].rearrange("p (t h) -> p t h", h=H),
                                off_rel[:, bass.ds(before_e * QUAD * R, QUAD * R)].unsqueeze(2).broadcast_to([P, QUAD * R, H]),
                                ALU.add).then_inc(e_log, 1)
                    steps(dve, step)

        weight = logit
        with ExitStack() as ctx:
            buf0 = sb("buf0", [P, BE], F32, ctx)
            buf1 = sb("buf1", [P, BE], F32, ctx)
            buf2 = sb("buf2", [P, BE], F32, ctx)
            buf3 = sb("buf3", [P, BE], F32, ctx)
            same_f = sb("same_f", [P, BE], BF16, ctx)
            apart = sb("apart", [P, BE], BF16, ctx)
            last_f = sb("last_f", [P, BE], BF16, ctx)
            more_f = sb("more_f", [P, BE], BF16, ctx)
            through = sb("through", [P, 3], F32, ctx)
            carry = sb("carry", [P, 5], F32, ctx)
            s_flag = [sem(f"s_flag{i}") for i in range(2)]
            s_pack, s_packed, s_vec, s_exp, s_back, s_backed, s_rc = (
                sem("s_pack"), sem("s_packed"), sem("s_vec"), sem("s_exp"), sem("s_back"), sem("s_backed"), sem("s_rc"))
            s_order = sem("s_order")
            s_pen_ready, s_alpha_ready, s_arg_ready, s_rc_ready = (
                sem("s_pen_ready"), sem("s_alpha_ready"), sem("s_arg_ready"), sem("s_rc_ready"))
            BANKS_USED = -(-BT // QUAD)

            def cols(q):
                return min(QUAD, BT - QUAD * q)

            with nc.Block() as block:
                @block.sync
                def _(sp):
                    for n, (flag, dest) in enumerate(((same_dram, buf2), (last_dram, buf3))):
                        for b in range(BLOCKS):
                            sp.dma_start(dest[b * RH:(b + 1) * RH, :],
                                         flag[b * BE:(b + 1) * BE].unsqueeze(0).broadcast_to([RH, BE])).then_inc(s_flag[n], 16)
                    sp.wait_ge(s_rc_ready, 1)
                    for b in range(BLOCKS):
                        sp.dma_start(rcnt_dram[b:b + 1, :], buf3[b * RH:b * RH + 1, :]).then_inc(s_rc, 16)
                    sp.wait_ge(s_rc, 16 * BLOCKS)

                @block.tensor
                def _(pe):
                    pe.wait_ge(s_order, 1)
                    for i in range(BT):
                        pe.transpose(bank[i // QUAD][:, (i % QUAD) * P:(i % QUAD + 1) * P], buf1[:, i * P:(i + 1) * P],
                                     ident[:, :]).then_inc(s_pack, 1)
                    for n, (ready, frm) in enumerate(((s_pen_ready, buf3), (s_alpha_ready, buf0))):
                        pe.wait_ge(ready, 1)
                        for i in range(BT):
                            if i % QUAD == 0:
                                if n == 0:
                                    pe.wait_ge(s_packed, i // QUAD + 1)
                                else:
                                    pe.wait_ge(s_backed, i // QUAD + 1)
                            pe.transpose(bank[i // QUAD][:, (i % QUAD) * P:(i % QUAD + 1) * P],
                                         frm[:, i * P:(i + 1) * P], ident[:, :]).then_inc(s_back, 1)

                @block.scalar
                def _(act):
                    act.copy(buf1[:, :].rearrange("p (i b c) -> p i b c", b=BLOCKS, c=RH),
                             logit[:, :].rearrange("p (b i c) -> p i b c", b=BLOCKS, c=RH)).then_inc(s_order, 1)
                    for q in range(BANKS_USED):
                        act.wait_ge(s_pack, QUAD * q + cols(q))
                        act.copy(buf0[:, q * GROUP:q * GROUP + cols(q) * P], bank[q][:, 0:cols(q) * P]).then_inc(s_packed, 1)
                    for q in range(BANKS_USED):
                        act.wait_ge(s_back, QUAD * q + cols(q))
                        frm = bank[q][:, 0:cols(q) * P].rearrange("p (i b r h) -> p i b r h", b=BLOCKS, r=R, h=H)
                        to = absent[:, :].rearrange("p (b i r) -> p i b r", b=BLOCKS, r=R)
                        act.copy(to[:, QUAD * q:QUAD * q + cols(q)], frm[:, :, :, :, 0]).then_inc(s_backed, 1)
                    act.wait_ge(s_arg_ready, 1)
                    act.activation(buf1[:, :], buf1[:, :], ACT.Exp, scale=-1.0).then_inc(s_exp, 1)
                    for q in range(BANKS_USED):
                        act.wait_ge(s_back, BT + QUAD * q + cols(q))
                        frm = bank[q][:, 0:cols(q) * P].rearrange("p (i b c) -> p i b c", b=BLOCKS, c=RH)
                        to = weight[:, :].rearrange("p (b i c) -> p i b c", b=BLOCKS, c=RH)
                        act.copy(to[:, QUAD * q:QUAD * q + cols(q)], frm).then_inc(s_backed, 1)

                @block.vector
                def _(dve):
                    chain = [0]

                    def link(ins):
                        chain[0] += 1
                        ins.then_inc(s_vec, 1)
                        dve.wait_ge(s_vec, chain[0])

                    def last_inc(ins, done):
                        ins.then_inc(done, 1)

                    def quarter(v, b):
                        return v[b * RH:(b + 1) * RH]

                    def run(outp, data0, data1, op0, op1, n, thr, start, forward):
                        order = slice(None, None, 1 if forward else -1)
                        edge = slice(BE - 1, BE) if forward else slice(0, 1)
                        link(dve.memset(carry[:, n:n + 1], start))
                        link(dve.tensor_tensor_scan(outp[:, order], data0[:, order], data1[:, order], start, op0, op1))
                        for b in range(BLOCKS - 1):
                            here, there = (b, b + 1) if forward else (BLOCKS - 1 - b, BLOCKS - 2 - b)
                            link(dve.scalar_tensor_tensor(
                                quarter(carry, there)[:, n:n + 1], quarter(carry, here)[:, n:n + 1],
                                quarter(through, here)[:, thr:thr + 1], quarter(outp, here)[:, edge], op0, op1))
                        link(dve.tensor_tensor_scan(outp[:, order], data0[:, order], data1[:, order],
                                                    carry[:, n:n + 1], op0, op1))

                    dve.wait_ge(s_flag[0], 16 * BLOCKS)
                    dve.wait_ge(s_flag[1], 16 * BLOCKS)
                    link(dve.tensor_copy(same_f[:, :], buf2[:, :]))
                    link(dve.tensor_scalar(apart[:, :], buf2[:, :], 1.0, -NEG, ALU.subtract, ALU.mult))
                    link(dve.tensor_copy(last_f[:, :], buf3[:, :]))
                    link(dve.tensor_scalar(more_f[:, :], buf3[:, :], -1.0, 1.0, ALU.mult, ALU.add))
                    for n, v in enumerate((apart, same_f, more_f)):
                        link(dve.tensor_reduce(through[:, n:n + 1], v[:, :], AX_X, ALU.min))
                    dve.wait_ge(s_packed, BANKS_USED)
                    run(buf1, apart, buf0, ALU.add, ALU.max, 0, 0, NEG, True)
                    link(dve.tensor_tensor(buf3[:, :], buf1[:, :], last_f[:, :], ALU.mult))
                    run(buf2, more_f, buf3, ALU.mult, ALU.add, 1, 2, 0.0, False)
                    last_inc(dve.tensor_scalar(buf3[:, :], buf2[:, :], 0.1 * NEG, NEG, ALU.is_lt, ALU.mult), s_pen_ready)
                    last_inc(dve.scalar_tensor_tensor(buf1[:, :], buf2[:, :], 0.1 * NEG, buf0[:, :], ALU.max, ALU.subtract),
                             s_arg_ready)
                    dve.wait_ge(s_exp, 1)
                    run(buf0, same_f, buf1, ALU.mult, ALU.add, 2, 1, 0.0, True)
                    link(dve.tensor_tensor(buf2[:, :], buf0[:, :], last_f[:, :], ALU.mult))
                    run(buf0, more_f, buf2, ALU.mult, ALU.add, 3, 2, 0.0, False)
                    link(dve.tensor_scalar(buf0[:, :], buf0[:, :], 1e-30, None, ALU.max))
                    link(dve.reciprocal(buf2[:, :], buf0[:, :]))
                    last_inc(dve.tensor_tensor(buf0[:, :], buf1[:, :], buf2[:, :], ALU.mult), s_alpha_ready)
                    dve.wait_ge(s_alpha_ready, 1)
                    link(dve.memset(buf1[:, :], 1.0))
                    run(buf2, more_f, buf1, ALU.mult, ALU.add, 4, 2, 0.0, False)
                    dve.wait_ge(s_back, BT)
                    dve.reciprocal(buf3[:, :], buf2[:, :]).then_inc(s_rc_ready, 1)

        with ExitStack() as ctx:
            same_g = sb("same_g", [P, 2, GROUP], F32, ctx)
            s_t = sb("s_t", [P, GROUP], F32, ctx)
            d_t = sb("d_t", [P, GROUP], F32, ctx)
            val = sb("val", [P, 2, R * F], F32, ctx)
            rel_t = sb("rel_t", [P, R, GROUP], F32, ctx)
            act_t = sb("act_t", [P, R, GROUP], F32, ctx)
            tails = sb("tails", [P, R], F32, ctx)
            ent = sb("ent", [P, 2, QUAD, 6 * EB], F32, ctx)
            lg = sb("lg", [P, QUAD * K5 * H], F32, ctx)
            lg2 = sb("lg2", [P, QUAD * K5 * H], F32, ctx)
            ex = sb("ex", [P, QUAD * K5 * H], F32, ctx)
            top = sb("top", [P, QUAD * H], F32, ctx)
            rsum = sb("rsum", [P, QUAD * H], F32, ctx)
            rinv = sb("rinv", [P, QUAD * H], F32, ctx)
            z_e = sb("z_e", [P, 2, QUAD, F], F32, ctx)
            x1_e = sb("x1_e", [P, 2, QUAD, F], F32, ctx)
            st_e = sb("st_e", [P, QUAD, 6], F32, ctx)
            mv_e = sb("mv_e", [P, QUAD, 2], F32, ctx)
            mid_e = sb("mid_e", [P, QUAD, 4], F32, ctx)
            sd_e = sb("sd_e", [P, QUAD], F32, ctx)
            rs_e = sb("rs_e", [P, QUAD], F32, ctx)
            rl_e = sb("rl_e", [P, QUAD], F32, ctx)
            put_ix = sb("put_ix", [P, 2, QUAD], I32, ctx)
            pXW, pM, pE = bank[0:2], bank[2:6], bank[6:8]
            f_hv, f_sp = sem("f_hv"), sem("f_sp")
            f_same = [sem(f"f_same{i}") for i in range(2)]
            f_put = [sem(f"f_put{i}") for i in range(2)]
            f_kept = [sem(f"f_kept{i}") for i in range(2)]
            f_rl = sem("f_rl")
            (f_s, f_d, f_XW, f_val, f_M, f_scan, f_tail, f_gelu, f_E0, f_E1, f_ent0, f_ent1, f_ls, f_ld, f_low, f_lg, f_top, f_arg,
             f_ex, f_sum, f_inv, f_al, f_wt, f_p1, f_p2, f_z, f_st, f_mv, f_sd, f_rs, f_x1, f_ix) = [sem("f_" + s) for s in (
                "s", "d", "XW", "val", "M", "scan", "tail", "gelu", "E0", "E1", "ent0", "ent1", "ls", "ld", "low", "lg", "top", "arg",
                "ex", "sum", "inv", "al", "wt", "p1", "p2", "z", "st", "mv", "sd", "rs", "x1", "ix")]

            def at(turn, k, offset):
                return behind(turn, k, 2, offset, EG)

            def steps(eng, step):
                for turn in (0, 1):
                    for k in range(2):
                        step(turn, k)
                with eng.Fori(2, EG // 2) as turn:
                    for k in range(2):
                        step(turn, k)
                for turn in range(EG // 2, EG // 2 + 3):
                    for k in range(2):
                        step(turn, k)

            def entry(s):
                return ent[:, s].rearrange("p j (k c) -> p j k c", k=6)

            with nc.Block() as block:
                @block.sync
                def _(sp):
                    def step(turn, k):
                        g = at(turn, k, 0)
                        if g.real:
                            need(sp, f_scan, R * (g.n - 1))
                            sp.dma_start(same_g[:, k, :], same_dram[bass.ds(g.n * GROUP, GROUP)].unsqueeze(0)
                                         .broadcast_to([P, GROUP])).then_inc(f_same[k], 16)
                        w = at(turn, k, 3)
                        if w.real:
                            sp.wait_ge(f_x1, w.n + 1)
                            sp.dma_start(reached_dram[bass.ds(w.n * GROUP, GROUP), :].rearrange("(j p) f -> p j f", p=P),
                                         x1_e[:, w.slot]).then_inc(f_kept[w.slot], 16)
                    steps(sp, step)
                    for slot in range(2):
                        sp.wait_ge(f_kept[slot], 16 * ((EG + 1 - slot) // 2))

                @block.tensor
                def _(pe):
                    def product(g, j):
                        need(pe, f_val, 4 * g.n + j - 1)
                        pe.matmul(pXW[j % 2][:, :], s_t[:, j * P:(j + 1) * P], w_rel[:, :], start=True, stop=True).then_inc(f_XW, 1)

                    def turn_over(g, j):
                        pe.wait_ge(f_val, 4 * g.n + j + 1)
                        for r in range(R):
                            if j == 0:
                                need(pe, f_scan, R * (g.n - 1) + r + 1)
                            ins = pe.transpose(pM[r][:, j * P:(j + 1) * P], val[:, j % 2, r * F:(r + 1) * F], ident[:, :])
                        ins.then_inc(f_M, 1)

                    def step(turn, k):
                        g, e = at(turn, k, 0), at(turn, k, 1)
                        if g.real:
                            pe.wait_ge(f_s, g.n + 1)
                            product(g, 0)
                            product(g, 1)
                            turn_over(g, 0)
                            product(g, 2)
                            turn_over(g, 1)
                            product(g, 3)
                            turn_over(g, 2)
                            turn_over(g, 3)
                        if e.real:
                            pe.wait_ge(f_gelu, R * (e.n + 1))
                            pe.wait_ge(f_d, e.n + 1)
                            for j in range(QUAD):
                                need(pe, f_ent0, 4 * e.n + j)
                                for r in range(3):
                                    ins = pe.matmul(pE[0][:, r * EB:(r + 1) * EB], act_t[:, r, j * P:(j + 1) * P],
                                                    w_cross[:, :], start=(r == 0), stop=(r == 2), skip_group_check=True)
                                ins.then_inc(f_E0, 1)
                                need(pe, f_ent1, 4 * e.n + j)
                                pe.matmul(pE[1][:, 0:EB], act_t[:, 3, j * P:(j + 1) * P], w_cross[:, :],
                                          start=True, stop=False, skip_group_check=True)
                                pe.matmul(pE[1][:, EB:3 * EB], d_t[:, j * P:(j + 1) * P], w_node[:, :],
                                          start=False, stop=False, skip_group_check=True)
                                pe.matmul(pE[1][:, 2 * EB:2 * EB + F], ones_b[:, :], lang3[:, :],
                                          start=False, stop=True, skip_group_check=True).then_inc(f_E1, 1)
                    steps(pe, step)

                @block.scalar
                def _(act):
                    def step(turn, k):
                        g, e, s, w = at(turn, k, 0), at(turn, k, 1), at(turn, k, 2), at(turn, k, 3)
                        if s.real:
                            act.wait_ge(f_arg, s.n + 1)
                            need(act, f_al, s.n)
                            act.activation(ex[:, :], lg[:, :], ACT.Exp).then_inc(f_ex, 1)
                        if e.real:
                            need(act, f_z, e.n - 1)
                            for j in range(QUAD):
                                act.wait_ge(f_E0, 4 * e.n + j + 1)
                                act.copy(ent[:, e.slot, j, 0:3 * EB], pE[0][:, 0:3 * EB]).then_inc(f_ent0, 1)
                                act.wait_ge(f_E1, 4 * e.n + j + 1)
                                act.copy(ent[:, e.slot, j, 3 * EB:6 * EB], pE[1][:, 0:3 * EB]).then_inc(f_ent1, 1)
                        if w.real:
                            act.wait_ge(f_mv, 2 * w.n + 2)
                            act.activation(sd_e[:, :], mv_e[:, :, 1], ACT.Sqrt, bias=eps_col[:, 0:1], scale=1.0 / F).then_inc(f_sd, 1)
                        if g.real:
                            need(act, f_E1, 4 * g.n)
                            for r in range(R):
                                act.wait_ge(f_scan, R * g.n + r + 1)
                                act.activation(act_t[:, r, :], rel_t[:, r, :], ACT.Gelu, bias=rel_bias[:, r:r + 1]).then_inc(f_gelu, 1)
                    steps(act, step)

                @block.vector
                def _(dve):
                    def messages(g, j):
                        dve.wait_ge(f_XW, 4 * g.n + j + 1)
                        need(dve, f_M, 4 * g.n + j - 1)
                        dve.tensor_tensor(
                            val[:, j % 2, :].rearrange("p (c d) -> p c d", d=D),
                            pXW[j % 2][:, :].rearrange("p (c d) -> p c d", d=D),
                            weight[:, bass.ds((g.n * QUAD + j) * RH, RH)].unsqueeze(2).broadcast_to([P, RH, D]),
                            ALU.mult).then_inc(f_val, 1)

                    def scale(s, j):
                        e4 = entry(s.slot)[:, j, 0:K5, 0:F].rearrange("p k (h d) -> p k h d", d=D)
                        al = lg2[:, :].rearrange("p (j k h) -> p j k h", j=QUAD, h=H)[:, j]
                        dve.tensor_tensor(e4, e4, al.unsqueeze(3).broadcast_to([P, K5, H, D]), ALU.mult).then_inc(f_wt, 1)

                    def step(turn, k):
                        g, e, s, w = at(turn, k, 0), at(turn, k, 1), at(turn, k, 2), at(turn, k, 3)
                        if g.real:
                            need(dve, f_XW, 4 * g.n)
                            dve.tensor_copy(s_t[:, :], src_t[:, bass.ds(g.n * GROUP, GROUP)]).then_inc(f_s, 1)
                        if e.real:
                            need(dve, f_E1, 4 * e.n)
                            dve.tensor_copy(d_t[:, :], dst_t[:, bass.ds(e.n * GROUP, GROUP)]).then_inc(f_d, 1)
                        lg4 = lg[:, :].rearrange("p (j k h) -> p j k h", j=QUAD, h=H)
                        low4 = lg2[:, :].rearrange("p (j k h) -> p j k h", j=QUAD, h=H)
                        if s.real:
                            dve.wait_ge(f_ent1, 4 * (s.n + 1))
                            dve.wait_ge(f_ent0, 4 * (s.n + 1))
                            en = entry(s.slot)
                            dve.tensor_tensor(lg4, en[:, :, 0:K5, F:EB],
                                              en[:, :, K5, F:EB].unsqueeze(2).broadcast_to([P, QUAD, K5, H]), ALU.add).then_inc(f_ls, 1)
                            dve.wait_ge(f_ls, s.n + 1)
                            dve.scalar_tensor_tensor(lg2[:, :], lg[:, :], SLOPE, lg[:, :], ALU.mult, ALU.max).then_inc(f_low, 1)
                            dve.wait_ge(f_low, s.n + 1)
                            dve.tensor_tensor(low4[:, :, 0:R, :], low4[:, :, 0:R, :],
                                              absent[:, bass.ds(s.n * QUAD * R, QUAD * R)].rearrange("p (j r) -> p j r", r=R)
                                              .unsqueeze(3).broadcast_to([P, QUAD, R, H]), ALU.add).then_inc(f_lg, 1)
                            dve.wait_ge(f_lg, s.n + 1)
                            top3 = top[:, :].rearrange("p (j h) -> p j h", h=H)
                            dve.tensor_reduce(top3, low4.rearrange("p j k h -> p j h k"), AX_X, ALU.max).then_inc(f_top, 1)
                            dve.wait_ge(f_top, s.n + 1)
                            dve.tensor_tensor(lg4, low4, top3.unsqueeze(2).broadcast_to([P, QUAD, K5, H]), ALU.subtract).then_inc(f_arg, 1)
                        if g.real:
                            messages(g, 0)
                            messages(g, 1)
                        if s.real:
                            dve.wait_ge(f_ex, s.n + 1)
                            ex4 = ex[:, :].rearrange("p (j k h) -> p j k h", j=QUAD, h=H)
                            sum3 = rsum[:, :].rearrange("p (j h) -> p j h", h=H)
                            dve.tensor_reduce(sum3, ex4.rearrange("p j k h -> p j h k"), AX_X, ALU.add).then_inc(f_sum, 1)
                            dve.wait_ge(f_sum, s.n + 1)
                            dve.reciprocal(rinv[:, :], rsum[:, :]).then_inc(f_inv, 1)
                            dve.wait_ge(f_inv, s.n + 1)
                            inv3 = rinv[:, :].rearrange("p (j h) -> p j h", h=H)
                            dve.tensor_tensor(low4, ex4, inv3.unsqueeze(2).broadcast_to([P, QUAD, K5, H]), ALU.mult).then_inc(f_al, 1)
                        if g.real:
                            messages(g, 2)
                        if s.real:
                            dve.wait_ge(f_al, s.n + 1)
                            scale(s, 0)
                        if g.real:
                            messages(g, 3)
                        if s.real:
                            for j in range(1, QUAD):
                                scale(s, j)
                        if w.real:
                            dve.wait_ge(f_z, w.n + 1)
                            stats(dve, z_e[:, w.slot], st_e).then_inc(f_st, 1)
                            dve.wait_ge(f_st, w.n + 1)
                            dve.tensor_tensor(mid_e[:, :, 0:2], st_e[:, :, 1:3], st_e[:, :, 4:6], ALU.add).then_inc(f_hv, 1)
                            dve.tensor_tensor(mid_e[:, :, 2], st_e[:, :, 1], st_e[:, :, 4], ALU.subtract).then_inc(f_hv, 1)
                            dve.wait_ge(f_hv, 2 * (w.n + 1))
                            dve.scalar_tensor_tensor(mid_e[:, :, 3], mid_e[:, :, 2], F / 4.0, mid_e[:, :, 2], ALU.mult, ALU.mult).then_inc(f_sp, 1)
                            dve.tensor_scalar(mv_e[:, :, 0], mid_e[:, :, 0], 0.5, None, ALU.mult).then_inc(f_mv, 1)
                            dve.wait_ge(f_sp, w.n + 1)
                            dve.tensor_tensor(mv_e[:, :, 1], mid_e[:, :, 3], mid_e[:, :, 1], ALU.add).then_inc(f_mv, 1)
                        if g.real:
                            dve.wait_ge(f_same[k], 16 * (g.turn + 1))
                            need(dve, f_tail, g.n)
                            for r in range(R):
                                dve.wait_ge(f_M, 4 * (g.n + 1))
                                need(dve, f_gelu, R * (g.n - 1) + r + 1)
                                start = tails[:, r:r + 1] if not isinstance(g.n, int) or g.n > 0 else 0.0
                                dve.tensor_tensor_scan(rel_t[:, r, :], same_g[:, k, :], pM[r][:, :], start,
                                                       ALU.mult, ALU.add).then_inc(f_scan, 1)
                            dve.wait_ge(f_scan, R * (g.n + 1))
                            dve.tensor_copy(tails[:, :], rel_t[:, :, GROUP - 1]).then_inc(f_tail, 1)
                        if w.real:
                            dve.wait_ge(f_sd, w.n + 1)
                            dve.reciprocal(rs_e[:, :], sd_e[:, :]).then_inc(f_rs, 1)
                            dve.wait_ge(f_rs, w.n + 1)
                            dve.tensor_tensor(rl_e[:, :], rs_e[:, :], last_e[:, bass.ds(w.n * QUAD, QUAD)], ALU.mult).then_inc(f_rl, 1)
                            dve.wait_ge(f_rl, w.n + 1)
                            need(dve, f_put[w.slot], 64 * w.turn)
                            need(dve, f_kept[w.slot], 16 * w.turn)
                            for j in range(QUAD):
                                ins = dve.tensor_scalar(x1_e[:, w.slot, j, :], z_e[:, w.slot, j, :], mv_e[:, j, 0:1],
                                                        rl_e[:, j:j + 1], ALU.subtract, ALU.mult)
                            ins.then_inc(f_x1, 1)
                    steps(dve, step)

                @block.gpsimd
                def _(pool):
                    def step(turn, k):
                        s, o = at(turn, k, 2), at(turn, k, 4)
                        if o.real:
                            need(pool, f_put[o.slot], 64 * o.turn)
                            pool.tensor_copy(put_ix[:, o.slot, :], idx_last[:, bass.ds(o.n * QUAD, QUAD)]).then_inc(f_ix, 1)
                            pool.wait_ge(f_ix, o.n + 1)
                            pool.wait_ge(f_x1, o.n + 1)
                        if s.real:
                            pool.wait_ge(f_wt, 4 * (s.n + 1))
                            en = entry(s.slot)

                            def plus(a, b, dest, done):
                                pool.tensor_tensor(dest, en[:, :, a, 0:F], en[:, :, b, 0:F], ALU.add).then_inc(done, 1)
                            plus(0, 1, en[:, :, 0, 0:F], f_p1)
                            plus(2, 3, en[:, :, 2, 0:F], f_p1)
                            plus(4, 5, en[:, :, 4, 0:F], f_p1)
                            pool.wait_ge(f_p1, 3 * (s.n + 1))
                            plus(0, 2, en[:, :, 0, 0:F], f_p2)
                            pool.wait_ge(f_p2, s.n + 1)
                            need(pool, f_x1, s.n - 1)
                            plus(0, 4, z_e[:, s.slot], f_z)
                        if o.real:
                            for j in range(QUAD):
                                pool.indirect_dma_start(
                                    x1_dram[:, :], bass.IndirectOffsetOnAxis(ap=put_ix[:, o.slot, j:j + 1], axis=0),
                                    x1_e[:, o.slot, j, :], None, bounds_check=N - 1, oob_is_err=False).then_inc(f_put[o.slot], 16)
                    steps(pool, step)
                    for slot in range(2):
                        pool.wait_ge(f_put[slot], 64 * ((EG + 1 - slot) // 2))
        edges_only.close()

        with ExitStack() as ctx:
            more_h = sb("more_h", [P, 4, GROUP], F32, ctx)
            rcnt_h = sb("rcnt_h", [P, 4, GROUP], F32, ctx)
            attr_h = sb("attr_h", [2, 4, GROUP], F32, ctx)
            xs_r = sb("xs_r", [P, 4, QUAD, F], F32, ctx)
            xl_r = sb("xl_r", [P, 4, QUAD, F], F32, ctx)
            xs_t = sb("xs_t", [P, 2, GROUP], F32, ctx)
            xd_t = sb("xd_t", [P, 4, GROUP], F32, ctx)
            msg_t = sb("msg_t", [P, 2, GROUP], F32, ctx)
            sum_t = sb("sum_t", [P, 2, GROUP], F32, ctx)
            mean_t = sb("mean_t", [P, 2, GROUP], F32, ctx)
            up_t = sb("up_t", [P, 2, GROUP], F32, ctx)
            o_e = sb("o_e", [P, 4, QUAD, F], F32, ctx)
            get_ix = sb("get_ix", [P, 4, QUAD], I32, ctx)
            out_ix = sb("out_ix", [P, 4, QUAD], I32, ctx)
            B2 = tail_buffers("e", ctx)
            qS, qD, qH, qU, qV, qR = bank[0], bank[1], bank[2], bank[3], bank[4], bank[5:7]
            TURN, HID, MEAN = 2, 3, 4
            PUT = OUT + 1
            h_row = [sem(f"h_row{i}") for i in range(4)]
            h_got = [sem(f"h_got{i}") for i in range(4)]
            h_put = [sem(f"h_put{i}") for i in range(4)]
            h_zero, h_ix, h_T, h_xs, h_xd, h_H, h_msg, h_sum, h_mean, h_U, h_up, h_V, h_R, h_oix = [sem("h_" + s) for s in (
                "zero", "ix", "T", "xs", "xd", "H", "msg", "sum", "mean", "U", "up", "V", "R", "oix")]

            def at(turn, k, offset):
                return behind(turn, k, 4, offset, EG)

            def late(g):
                return g._replace(n=g.n + GROUPS)

            def batch(turn, k, offset=0):
                n = 4 * turn + k - offset
                real = 0 <= n < EG + SCALE if isinstance(n, int) else True
                return n + BATCHES, (k - offset) % 2, real

            def steps(eng, step):
                for turn in (0, 1):
                    for k in range(4):
                        step(turn, k)
                with eng.Fori(2, EG // 4) as turn:
                    for k in range(4):
                        step(turn, k)
                for turn in range(EG // 4, EG // 4 + 3):
                    for k in range(4):
                        step(turn, k)

            def place(turn, k, offset=0):
                return turn * -4 + (EG - 1 - k + offset)

            with nc.Block() as block:
                @block.sync
                def _(sp):
                    def step(turn, k):
                        g = at(turn, k, 0)
                        if g.real:
                            cols = bass.ds(place(turn, k) * GROUP, GROUP)
                            need(sp, h_mean, g.n - 3)
                            need(sp, h_sum, g.n - 3)
                            need(sp, h_H, g.n - 3)
                            need(sp, h_T, g.n - 3)
                            sp.dma_start(more_h[:, k, :], more_dram[cols].unsqueeze(0).broadcast_to([P, GROUP])).then_inc(h_row[k], 16)
                            sp.dma_start(rcnt_h[:, k, :], rcnt_dram.rearrange("b e -> (b e)")[cols].unsqueeze(0)
                                         .broadcast_to([P, GROUP])).then_inc(h_row[k], 16)
                            sp.dma_start(attr_h[:, k, :], attr_dram[:, cols]).then_inc(h_row[k], 16)
                            sp.dma_start(xl_r[:, k], reached_dram[cols, :].rearrange("(j p) f -> p j f", p=P)).then_inc(h_row[k], 16)
                    steps(sp, step)

                @block.gpsimd
                def _(pool):
                    pool.memset(B2["st"][:, :, :, :], 0.0).then_inc(h_zero, 1)

                    def step(turn, k):
                        g, m, o = at(turn, k, 0), at(turn, k, MEAN), at(turn, k, PUT)
                        if g.real:
                            cols = bass.ds(place(turn, k) * QUAD, QUAD)
                            need(pool, h_T, g.n - 3)
                            pool.tensor_copy(get_ix[:, k, :], idx_src[:, cols]).then_inc(h_ix, 1)
                            pool.wait_ge(h_ix, g.n + 1)
                        if o.real:
                            cols = bass.ds(place(turn, k, PUT) * QUAD, QUAD)
                            need(pool, h_put[o.slot], 64 * o.turn)
                            pool.tensor_copy(out_ix[:, o.slot, :], idx_first[:, cols]).then_inc(h_oix, 1)
                            pool.wait_ge(h_oix, o.n + 1)
                            pool.wait_ge(t_out, late(o).n + 1)
                        if m.real:
                            pool.wait_ge(h_sum, m.n + 1)
                            need(pool, h_U, m.n - 1)
                            pool.tensor_tensor(mean_t[:, m.slot % 2, :], sum_t[:, m.slot % 2, :], rcnt_h[:, m.slot, :],
                                               ALU.mult).then_inc(h_mean, 1)
                        if g.real:
                            for j in range(QUAD):
                                pool.indirect_dma_start(
                                    xs_r[:, k, j, :], None, x1_dram[:, :],
                                    bass.IndirectOffsetOnAxis(ap=get_ix[:, k, j:j + 1], axis=0)).then_inc(h_got[k], 16)
                        if o.real:
                            for j in range(QUAD):
                                pool.indirect_dma_start(
                                    out[:, :], bass.IndirectOffsetOnAxis(ap=out_ix[:, o.slot, j:j + 1], axis=0),
                                    o_e[:, o.slot, j, :], None, bounds_check=N - 1, oob_is_err=False).then_inc(h_put[o.slot], 16)
                    steps(pool, step)
                    for slot in range(4):
                        pool.wait_ge(h_put[slot], 64 * ((EG + 3 - slot) // 4))

                @block.tensor
                def _(pe):
                    def step(turn, k):
                        g = at(turn, k, ADD)
                        if g.real:
                            x_of = xd_t[:, g.slot]
                            pe.wait_ge(h_up, g.n + 1)
                            pe.wait_ge(t_w, late(g).n)
                            pe.wait_ge(b_st[NORM2], late(g).n)
                            pe.matmul(qV[:, :], ones_b[:, :], along(u2b3), start=True, stop=False)
                            for j in range(QUAD):
                                pe.matmul(qV[:, j * F:(j + 1) * F], up_t[:, g.slot % 2, j * P:(j + 1) * P], w_u2[:, :],
                                          start=False, stop=False)
                                ins = pe.matmul(qV[:, j * F:(j + 1) * F], x_of[:, j * P:(j + 1) * P], ident[:, :],
                                                start=False, stop=(j == QUAD - 1))
                            ins.then_inc(h_V, 1)
                            need(pe, t_y, late(g).n - 1)
                            to = qR[g.slot % 2]
                            pe.matmul(to[:, :], ones_b[:, :], along(beta3), start=True, stop=False)
                            for j in range(QUAD):
                                ins = pe.matmul(to[:, j * F:(j + 1) * F], x_of[:, j * P:(j + 1) * P], ident[:, :],
                                                start=False, stop=(j == QUAD - 1))
                            ins.then_inc(h_R, 1)
                        g = at(turn, k, HID)
                        if g.real:
                            pe.wait_ge(h_xs, g.n + 1)
                            pe.wait_ge(h_xd, g.n + 1)
                            need(pe, h_msg, g.n)
                            pe.matmul(qH[:, :], w_m1s[:, :], xs_t[:, g.slot % 2, :], start=True, stop=False)
                            pe.matmul(qH[:, :], w_m1d[:, :], xd_t[:, g.slot, :], start=False, stop=False)
                            pe.matmul(qH[:, :], w_m1a[:, :], attr_h[:, g.slot, :], start=False, stop=True).then_inc(h_H, 1)
                        g = at(turn, k, TURN)
                        if g.real:
                            pe.wait_ge(h_row[g.slot], 64 * (g.turn + 1))
                            need(pe, h_xd, g.n)
                            for j in range(QUAD):
                                pe.transpose(qD[:, j * P:(j + 1) * P], xl_r[:, g.slot, j, :], ident[:, :])
                            pe.wait_ge(h_got[g.slot], 64 * (g.turn + 1))
                            need(pe, h_xs, g.n)
                            for j in range(QUAD):
                                ins = pe.transpose(qS[:, j * P:(j + 1) * P], xs_r[:, g.slot, j, :], ident[:, :])
                            ins.then_inc(h_T, 1)
                        g = at(turn, k, MEAN)
                        if g.real:
                            pe.wait_ge(h_mean, g.n + 1)
                            need(pe, h_up, g.n)
                            pe.matmul(qU[:, :], w_u1x[:, :], xd_t[:, g.slot, :], start=True, stop=False)
                            pe.matmul(qU[:, :], w_u1m[:, :], mean_t[:, g.slot % 2, :], start=False, stop=True).then_inc(h_U, 1)
                    steps(pe, step)

                @block.scalar
                def _(act):
                    def step(turn, k):
                        n, slot, real = batch(turn, k, 1)
                        if real:
                            batch_root(act, n, slot, B2)
                        g = at(turn, k, HID)
                        if g.real:
                            act.wait_ge(h_H, g.n + 1)
                            need(act, h_sum, g.n - 1)
                            act.activation(msg_t[:, g.slot % 2, :], qH[:, :], ACT.Relu, bias=m1_bias[:, 0:1]).then_inc(h_msg, 1)
                        g = at(turn, k, OUT)
                        if g.real:
                            need(act, h_put[g.slot], 64 * g.turn)
                            tail_out(act, late(g), slot, B2, o_e[:, g.slot])
                        g = at(turn, k, TURN)
                        if g.real:
                            act.wait_ge(h_T, g.n + 1)
                            need(act, h_H, g.n - 1)
                            act.copy(xs_t[:, g.slot % 2, :], qS[:, :]).then_inc(h_xs, 1)
                        g = at(turn, k, MEAN)
                        if g.real:
                            act.wait_ge(h_U, g.n + 1)
                            need(act, h_V, g.n - 1)
                            act.activation(up_t[:, g.slot % 2, :], qU[:, :], ACT.Relu, bias=u1m_bias[:, 0:1]).then_inc(h_up, 1)
                    steps(act, step)

                @block.vector
                def _(dve):
                    dve.wait_ge(h_zero, 1)

                    def spread(to, done, g, slots, factors, frm):
                        first = isinstance(g.n, int) and g.n == 0
                        if not first:
                            dve.wait_ge(done, g.n)
                        dve.tensor_tensor_scan(to[:, g.slot % slots, ::-1], factors[:, g.slot, ::-1], frm[:, ::-1],
                                               0.0 if first else to[:, (g.slot - 1) % slots, 0:1],
                                               ALU.mult, ALU.add).then_inc(done, 1)

                    def step(turn, k):
                        d, m, a, c, f = (at(turn, k, o) for o in (TURN, HID, ADD, SCALE, OUT))
                        n, slot, real = batch(turn, k)
                        before, old, had = batch(turn, k, 1)
                        if a.real:
                            a = late(a)
                            need(dve, t_out, a.n - 3)
                            dve.wait_ge(h_V, a.n - GROUPS + 1)
                            dve.tensor_tensor(B2["w"][:, a.slot], split(qV[:, :]), along(gamma_b), ALU.mult).then_inc(t_w, 1)
                        if had:
                            need(dve, t_out, before - BATCHES - 7 + GROUPS)
                            batch_inverse(dve, before, old, B2)
                        if a.real:
                            need(dve, b_half, 2 * n)
                            stats(dve, split(qV[:, :]), B2["st"][:, NORM2]).then_inc(b_st[NORM2], 1)
                        if f.real:
                            tail_shift(dve, late(f), before, old, B2)
                        if d.real:
                            dve.wait_ge(h_T, d.n + 1)
                            need(dve, h_V, d.n - 3)
                            need(dve, h_R, d.n - 3)
                            spread(xd_t, h_xd, d, 4, more_h, qD)
                        if c.real:
                            tail_scale(dve, late(c), before, old, B2, split(qR[c.slot % 2][:, :]), h_R, c.n + 1)
                        if m.real:
                            dve.wait_ge(h_msg, m.n + 1)
                            need(dve, h_mean, m.n - 1)
                            spread(sum_t, h_sum, m, 2, more_h, msg_t[:, m.slot % 2, :])
                        if c.real:
                            dve.wait_ge(t_y, late(c).n + 1)
                            need(dve, b_half, 2 * n)
                            stats(dve, B2["w"][:, c.slot], B2["st"][:, NORM3]).then_inc(b_st[NORM3], 1)
                        if real:
                            for norm, g in ((NORM2, a), (NORM3, c)):
                                if g.real:
                                    dve.wait_ge(b_st[norm], g.n + 1 + (GROUPS if g is c else 0))
                            batch_means(dve, n, slot, B2)
                    steps(dve, step)


_INS = ['x', 'src', 'dst', 'edge_attr_2', 'edge_type_4', 'L0_gnn_W_rel', 'L0_gnn_att_src_rel', 'L0_gnn_att_dst_rel',
        'L0_gnn_bias_rel', 'L0_gnn_W_self', 'L0_gnn_W_cross', 'L0_gnn_att_src_lang', 'L0_gnn_att_dst_lang',
        'L0_gnn_bias_lang', 'L1_gnn_mW1', 'L1_gnn_mb1', 'L1_gnn_mW2', 'L1_gnn_mb2', 'L1_gnn_uW1', 'L1_gnn_ub1',
        'L1_gnn_uW2', 'L1_gnn_ub2', 'L1_gnn_gamma', 'L1_gnn_beta']


def kernel(**inputs):
    import numpy as _np
    import concourse.bacc as _bacc
    from concourse import mybir as _mybir
    from concourse.bass_utils import run_bass_kernel_spmd as _run

    nc = _bacc.Bacc("TRN2", target_bir_lowering=False, num_devices=1)
    arrays, args = {}, []
    for name in _INS:
        a = _np.ascontiguousarray(inputs[name])
        arrays[f"in_{name}_dram"] = a
        args.append(nc.dram_tensor(f"in_{name}_dram", a.shape, _mybir.dt.from_np(a.dtype), kind="ExternalInput").ap())
    x = arrays["in_x_dram"]
    args.append(nc.dram_tensor("out_0_dram", x.shape, _mybir.dt.from_np(x.dtype), kind="ExternalOutput").ap())
    build(nc, *args)
    r = _run(nc, [arrays], core_ids=[0])
    return r.results[0]["out_0_dram"]
```

```python
from contextlib import ExitStack
from collections import namedtuple

import concourse.bass as bass
from concourse import mybir

P = 128
QUAD = 4
F32 = mybir.dt.float32
BF16 = mybir.dt.bfloat16
I32 = mybir.dt.int32
ALU = mybir.AluOpType
ACT = mybir.ActivationFunctionType
AX_X = mybir.AxisListType.X
LN_EPS = 1e-5
SLOPE = 0.2
NEG = -1e30

Group = namedtuple("Group", "n turn slot real")


def need(eng, sem, value):
    if not isinstance(value, int) or value > 0:
        eng.wait_ge(sem, value)


def behind(turn, k, unroll, offset, total, first=0):
    t, slot = turn + (k - offset) // unroll, (k - offset) % unroll
    n = unroll * t + slot + first
    real = 0 <= n < total if isinstance(n, int) else True
    return Group(n, t, slot, real)


def split(v):
    return v.rearrange("p (j f) -> p j f", j=QUAD)


def build(nc, x, src, dst, edge_attr, edge_type, W_rel, a_src_rel, a_dst_rel, b_rel, W_self, W_cross,
          a_src_lang, a_dst_lang, b_lang, mW1, mb1, mW2, mb2, uW1, ub1, uW2, ub2, gamma, beta, out):
    N, F = x.shape
    E = src.shape[0]
    R, H, D = a_src_rel.shape
    RH = R * H
    K5 = R + 1
    EB = F + H
    GROUP = QUAD * P
    SUPER = 2 * GROUP
    SUPERS = -(-N // SUPER)
    GROUPS = 2 * SUPERS
    TAIL = N - SUPER
    SKIP = ((SUPERS - 1) * SUPER - TAIL) // 8
    BLOCKS = P // RH
    BT = -(-E // (P * BLOCKS))
    TILES = BLOCKS * BT
    EP = TILES * P
    EG = TILES // QUAD
    BE = BT * P
    FULL = E // P
    REST = E - FULL * P
    assert F == P and H * D == F and RH * BLOCKS == P and TILES % QUAD == 0 and TILES <= P
    assert SUPERS == 2 * (EG - 1) + 1 and N < 2 ** 24 and ((SUPERS - 1) * SUPER - TAIL) % 8 == 0

    x1_dram = nc.dram_tensor("x1_rows", (N, F), F32, kind="Internal").ap()
    same_dram = nc.dram_tensor("same_run", (EP,), F32, kind="Internal").ap()
    more_dram = nc.dram_tensor("more_of_run", (EP,), F32, kind="Internal").ap()
    reached_dram = nc.dram_tensor("reached_rows", (EP, F), F32, kind="Internal").ap()
    attr_dram = nc.dram_tensor("attr_t", (2, EP), F32, kind="Internal").ap()
    scan_dram = nc.dram_tensor("scan_flags", (4, EP), BF16, kind="Internal").ap()
    count_dram = nc.dram_tensor("count", (BLOCKS, BE), F32, kind="Internal").ap()
    rcnt_dram = nc.dram_tensor("inverse_count", (EP,), F32, kind="Internal").ap()

    whole = ExitStack()
    with whole:
        def sb(name, shape, dt=F32, ctx=whole):
            return ctx.enter_context(nc.sbuf_tensor(name, shape, dt))

        def sem(name):
            return whole.enter_context(nc.semaphore(name))

        bank = [whole.enter_context(nc.psum_tensor(f"bank{i}", [P, 512], F32)) for i in range(8)]

        ident = sb("ident", [P, P])
        w_self_id = sb("w_self_id", [P, F])
        w_node = sb("w_node", [P, 2 * EB])
        w_rel = sb("w_rel", [P, R * F])
        w_log_s = sb("w_log_s", [P, RH])
        w_log_d = sb("w_log_d", [P, RH])
        w_cross = sb("w_cross", [P, EB])
        w_m1s = sb("w_m1s", [P, F])
        w_m1d = sb("w_m1d", [P, F])
        w_m1a = sb("w_m1a", [2, F])
        w_u1x = sb("w_u1x", [P, F])
        w_u1m = sb("w_u1m", [P, F])
        w_u2 = sb("w_u2", [P, F])
        rel_bias = sb("rel_bias", [P, R])
        m1_bias = sb("m1_bias", [P, 1])
        u1_bias = sb("u1_bias", [P, 1])
        u1m_bias = sb("u1m_bias", [P, 1])
        gamma_b = sb("gamma_b", [P, F])
        beta_b = sb("beta_b", [P, F])
        eps_col = sb("eps_col", [P, 1])
        power = sb("power", [P, 1])
        ones_b = sb("ones_b", [P, P], BF16)
        select = sb("select", [P, BLOCKS * H])
        lang3 = sb("lang3", [P, F], BF16)
        lang3c = sb("lang3c", [P, F], BF16)
        u2b3 = sb("u2b3", [P, F], BF16)
        beta3 = sb("beta3", [P, F], BF16)
        idx_src = sb("idx_src", [P, TILES], I32)
        idx_dst = sb("idx_dst", [P, TILES], I32)
        idx_last = sb("idx_last", [P, TILES], I32)
        idx_first = sb("idx_first", [P, TILES], I32)
        last_e = sb("last_e", [P, TILES])
        off_rel = sb("off_rel", [P, TILES * R])
        logit = sb("logit", [P, TILES * RH])
        absent = sb("absent", [P, TILES * R])
        edges_only = whole.enter_context(ExitStack())
        src_t = sb("src_t", [P, EP], F32, edges_only)
        dst_t = sb("dst_t", [P, EP], F32, edges_only)

        with ExitStack() as ctx:
            w_self = sb("w_self", [P, F], F32, ctx)
            w_m2 = sb("w_m2", [P, F], F32, ctx)
            w_m2t = sb("w_m2t", [P, F], F32, ctx)
            w_u1b = sb("w_u1b", [P, F], F32, ctx)
            mb2_col = sb("mb2_col", [P, 1], F32, ctx)
            a_s = sb("a_s", [P, R * F], F32, ctx)
            a_d = sb("a_d", [P, R * F], F32, ctx)
            al_s = sb("al_s", [P, F], F32, ctx)
            al_d = sb("al_d", [P, F], F32, ctx)
            bias2 = sb("bias2", [P, 4, F], F32, ctx)
            part = sb("part", [P, 3, 4, F], BF16, ctx)
            left = sb("left", [P, 2, 4, F], F32, ctx)
            w_u2_raw = sb("w_u2_raw", [P, F], F32, ctx)
            w_sum = sb("w_sum", [P, F], F32, ctx)
            means4 = sb("means4", [P, 4], F32, ctx)
            prod = sb("prod", [P, 5, R * F], F32, ctx)
            rows_i = sb("rows_i", [P, 5, P], I32, ctx)
            rows = sb("rows", [P, 5, P], F32, ctx)
            flags = sb("flags", [P, 6, P], F32, ctx)
            scan_flags = sb("scan_flags_rows", [P, 4, P], BF16, ctx)
            attr = sb("attr", [P, 2 * P], F32, ctx)
            attr2 = sb("attr2", [P, 2, P], F32, ctx)
            type_e = sb("type_e", [P, TILES], F32, ctx)
            s_weights, s_weights_p = sem("s_weights"), sem("s_weights_p")

            def wait_weights(eng):
                eng.wait_ge(s_weights, 16 * (len(loads) - len(loads) // 3))
                eng.wait_ge(s_weights_p, 16 * (len(loads) // 3))
            s_ident0 = sem("s_ident0")
            s_ident = sem("s_ident")
            s_pads = sem("s_pads")
            s_rows = sem("s_rows")
            s_const = sem("s_const")
            s_centre = sem("s_centre")
            s_bias = sem("s_bias")
            s_split = sem("s_split")
            s_prod = sem("s_prod")
            s_rowsf = sem("s_rowsf")
            s_flags = sem("s_flags")
            s_scan = sem("s_scan")
            s_scratch = sem("s_scratch")
            s_tabs = sem("s_tabs")
            s_taken = sem("s_taken")
            s_type = sem("s_type")
            s_m2t = sem("s_m2t")
            s_m2ts = sem("s_m2ts")
            s_fold = sem("s_fold")
            s_done = sem("s_done")

            def row_of(v):
                return v.unsqueeze(0)

            loads = [
                (w_self[:, :], W_self), (w_rel[:, :].rearrange("i (r o) -> i r o", r=R), W_rel.rearrange("r i o -> i r o")),
                (w_cross[:, 0:F], W_cross), (w_m1s[:, :], mW1[0:F, :]), (w_m1d[:, :], mW1[F:2 * F, :]),
                (w_m1a[:, :], mW1[2 * F:2 * F + 2, :]), (w_m2[:, :], mW2), (w_u1x[:, :], uW1[0:F, :]),
                (w_u1b[:, :], uW1[F:2 * F, :]), (w_u2_raw[:, :], uW2),
                (m1_bias[:, :], mb1.unsqueeze(1)), (u1_bias[:, :], ub1.unsqueeze(1)), (mb2_col[:, :], mb2.unsqueeze(1)),
                (gamma_b[:, :], row_of(gamma).broadcast_to([P, F])), (beta_b[:, :], row_of(beta).broadcast_to([P, F])),
                (al_s[:, :], row_of(a_src_lang.rearrange("h d -> (h d)")).broadcast_to([P, F])),
                (al_d[:, :], row_of(a_dst_lang.rearrange("h d -> (h d)")).broadcast_to([P, F])),
                (a_s[:, :], row_of(a_src_rel.rearrange("r h d -> (r h d)")).broadcast_to([P, R * F])),
                (a_d[:, :], row_of(a_dst_rel.rearrange("r h d -> (r h d)")).broadcast_to([P, R * F])),
                (bias2[:, 0, :], row_of(b_lang).broadcast_to([P, F])), (bias2[:, 1, :], row_of(ub2).broadcast_to([P, F])),
            ] + [(rel_bias[:, r:r + 1], b_rel[r, :].unsqueeze(1)) for r in range(R)]

            def tiled(v, start, count):
                return v[start:start + count * P].rearrange("(t p) -> t p", p=P)

            with nc.Block() as block:
                @block.sync
                def _(sp):
                    for n, (dest, source) in enumerate(loads):
                        if n % 3 < 2:
                            sp.dma_start(dest, source).then_inc(s_weights, 16)

                @block.scalar
                def _(act):
                    act.wait_ge(s_pads, 6)
                    for kind, v in ((0, src), (1, edge_type), (2, dst)):
                        act.dma_start(rows_i[0:FULL, kind, :], tiled(v, 0, FULL)).then_inc(s_rows, 16)
                        act.dma_start(rows_i[FULL:FULL + 1, kind, 0:REST], row_of(v[FULL * P:E])).then_inc(s_rows, 16)
                    act.dma_start(rows_i[0:1, 3, 1:P], row_of(dst[0:P - 1])).then_inc(s_rows, 16)
                    act.dma_start(rows_i[1:FULL, 3, :], tiled(dst, P - 1, FULL - 1)).then_inc(s_rows, 16)
                    act.dma_start(rows_i[FULL:FULL + 1, 3, 0:REST + 1], row_of(dst[FULL * P - 1:E])).then_inc(s_rows, 16)
                    act.dma_start(rows_i[0:FULL, 4, :], tiled(dst, 1, FULL)).then_inc(s_rows, 16)
                    act.dma_start(rows_i[FULL:FULL + 1, 4, 0:REST - 1], row_of(dst[FULL * P + 1:E])).then_inc(s_rows, 16)
                    act.dma_start(attr[0:FULL, :], edge_attr[0:FULL * P, :].rearrange("(t p) c -> t (p c)", p=P)).then_inc(s_rows, 16)
                    act.dma_start(attr[FULL:FULL + 1, 0:2 * REST],
                                  row_of(edge_attr[FULL * P:E, :].rearrange("p c -> (p c)"))).then_inc(s_rows, 16)

                @block.gpsimd
                def _(pool):
                    for kind, value in ((0, 0), (1, 0), (2, N), (3, N), (4, N + 1)):
                        pool.memset(rows_i[:, kind, :], value).then_inc(s_pads, 1)
                    pool.memset(attr[:, :], 0.0).then_inc(s_pads, 1)
                    pool.memset(ident[:, :], 0.0).then_inc(s_ident0, 1)
                    pool.wait_ge(s_ident0, 1)
                    pool.affine_select(out=ident[:, :], in_=ident[:, :], compare_op=ALU.not_equal, fill=1.0, base=0,
                                       pattern=[[-1, P]], channel_multiplier=1).then_inc(s_ident, 1)
                    pool.memset(ones_b[:, :], 1.0).then_inc(s_const, 1)
                    pool.memset(eps_col[:, :], LN_EPS).then_inc(s_const, 1)
                    pool.memset(power[:, :], -0.5).then_inc(s_const, 1)
                    pool.memset(lang3[:, :], 0.0).then_inc(s_const, 1)
                    pool.memset(lang3c[:, :], 0.0).then_inc(s_const, 1)
                    pool.memset(u2b3[:, :], 0.0).then_inc(s_const, 1)
                    pool.memset(beta3[:, :], 0.0).then_inc(s_const, 1)
                    for n, (dest, source) in enumerate(loads):
                        if n % 3 == 2:
                            pool.dma_start(dest, source).then_inc(s_weights_p, 16)

            ROW_LOADS = 13
            with nc.Block() as block:
                @block.vector
                def _(dve):
                    dve.wait_ge(s_rows, 16 * ROW_LOADS)
                    dve.tensor_copy(rows[:, :, :], rows_i[:, :, :]).then_inc(s_rowsf, 1)
                    dve.tensor_copy(attr2[:, :, :], attr[:, :].rearrange("t (p c) -> t c p", c=2)).then_inc(s_rowsf, 1)
                    dve.wait_ge(s_rowsf, 2)
                    dve.tensor_tensor(flags[:, 0, :], rows[:, 2, :], rows[:, 3, :], ALU.is_equal).then_inc(s_flags, 1)
                    dve.tensor_tensor(flags[:, 1, :], rows[:, 2, :], rows[:, 4, :], ALU.not_equal).then_inc(s_flags, 1)
                    dve.tensor_scalar(flags[:, 2, :], rows[:, 2, :], float(N - 1), None, ALU.min).then_inc(s_flags, 1)
                    dve.wait_ge(s_flags, 3)
                    dve.scalar_tensor_tensor(flags[:, 3, :], rows[:, 2, :], float(N), flags[:, 1, :],
                                             ALU.subtract, ALU.mult).then_inc(s_flags, 1)
                    dve.tensor_scalar(flags[:, 4, :], flags[:, 0, :], -1.0, 1.0, ALU.mult, ALU.add).then_inc(s_flags, 1)
                    dve.tensor_scalar(flags[:, 5, :], flags[:, 1, :], -1.0, 1.0, ALU.mult, ALU.add).then_inc(s_flags, 1)
                    dve.wait_ge(s_flags, 6)
                    for k, flag in ((0, 0), (2, 5)):
                        dve.tensor_copy(scan_flags[:, k, :], flags[:, flag, :]).then_inc(s_scan, 1)
                        dve.tensor_scalar(scan_flags[:, k + 1, :], flags[:, flag, :], 1.0, -NEG, ALU.subtract, ALU.mult).then_inc(s_scan, 1)
                    dve.scalar_tensor_tensor(flags[:, 4, :], rows[:, 2, :], float(N), flags[:, 4, :],
                                             ALU.subtract, ALU.mult).then_inc(s_flags, 1)
                    dve.wait_ge(s_flags, 7)
                    dve.tensor_scalar(flags[:, 3:5, :], flags[:, 3:5, :], float(N), None, ALU.add).then_inc(s_flags, 1)
                    wait_weights(dve)
                    dve.wait_ge(s_ident, 1)
                    dve.tensor_tensor(w_sum[:, :], w_self[:, :], ident[:, :], ALU.add).then_inc(s_centre, 1)
                    dve.tensor_copy(bias2[:, 2, :], bias2[:, 0, :]).then_inc(s_bias, 1)
                    dve.tensor_copy(bias2[:, 3, :], beta_b[:, :]).then_inc(s_bias, 1)
                    dve.wait_ge(s_centre, 1)
                    dve.wait_ge(s_bias, 2)
                    centred = [(w_sum[:, :], w_self_id[:, :]), (w_u2_raw[:, :], w_u2[:, :]),
                               (bias2[:, 1, :], bias2[:, 1, :]), (bias2[:, 2, :], bias2[:, 2, :])]
                    for n, (v, _) in enumerate(centred):
                        dve.tensor_reduce(means4[:, n:n + 1], v, AX_X, ALU.add).then_inc(s_centre, 1)
                    dve.wait_ge(s_centre, 5)
                    dve.tensor_scalar(means4[:, :], means4[:, :], 1.0 / F, None, ALU.mult).then_inc(s_centre, 1)
                    dve.wait_ge(s_centre, 6)
                    for n, (v, dest) in enumerate(centred):
                        dve.tensor_scalar(dest, v, means4[:, n:n + 1], None, ALU.subtract).then_inc(s_centre, 1)
                    dve.wait_ge(s_centre, 10)
                    dve.tensor_copy(part[:, 0], bias2[:, :, :]).then_inc(s_split, 1)
                    dve.wait_ge(s_split, 1)
                    dve.tensor_tensor(left[:, 0], bias2[:, :, :], part[:, 0], ALU.subtract).then_inc(s_split, 1)
                    dve.wait_ge(s_split, 2)
                    dve.tensor_copy(part[:, 1], left[:, 0]).then_inc(s_split, 1)
                    dve.wait_ge(s_split, 3)
                    dve.tensor_tensor(left[:, 1], left[:, 0], part[:, 1], ALU.subtract).then_inc(s_split, 1)
                    dve.wait_ge(s_split, 4)
                    dve.tensor_copy(part[:, 2], left[:, 1]).then_inc(s_split, 1)
                    dve.wait_ge(s_split, 5)
                    dve.wait_ge(s_const, 7)
                    for k in range(3):
                        for b, dest in ((0, lang3), (1, u2b3), (2, lang3c), (3, beta3)):
                            dve.tensor_copy(dest[32 * k:32 * k + 1, :], part[32 * k:32 * k + 1, k, b, :]).then_inc(s_done, 1)
                    pairs = [(w_rel[:, :], a_s[:, :], w_log_s[:, :], R * F), (w_rel[:, :], a_d[:, :], w_log_d[:, :], R * F),
                             (w_cross[:, 0:F], al_s[:, :], w_cross[:, F:EB], F),
                             (w_self[:, :], al_s[:, :], w_node[:, F:EB], F),
                             (w_self[:, :], al_d[:, :], w_node[:, EB + F:2 * EB], F)]
                    for n, (w, a, _, size) in enumerate(pairs):
                        dve.tensor_tensor(prod[:, n, 0:size], w, a, ALU.mult).then_inc(s_prod, 1)
                    for n, (_, _, dest, size) in enumerate(pairs):
                        dve.wait_ge(s_prod, n + 1)
                        dve.tensor_reduce(dest, prod[:, n, 0:size].rearrange("p (h d) -> p h d", d=D), AX_X, ALU.add).then_inc(s_done, 1)
                    dve.tensor_copy(w_node[:, 0:F], w_self[:, :]).then_inc(s_done, 1)
                    dve.tensor_copy(w_node[:, EB:EB + F], ident[:, :]).then_inc(s_done, 1)
                    dve.tensor_reduce(select[:, :], ident[:, :].rearrange("p (b r h) -> p b h r", b=BLOCKS, r=R),
                                      AX_X, ALU.add).then_inc(s_done, 1)
                    dve.wait_ge(s_tabs, 6)
                    for k, dest in enumerate((idx_src, idx_dst, idx_last, idx_first, type_e, last_e)):
                        dve.tensor_copy(dest[:, :], bank[4 * (k // 4)][:, (k % 4) * P:(k % 4) * P + TILES]).then_inc(s_type, 1)
                    dve.wait_ge(s_type, 6)
                    for r in range(R):
                        dve.tensor_scalar(off_rel[:, r::R], type_e[:, :], float(r), NEG, ALU.not_equal, ALU.mult).then_inc(s_done, 1)
                    dve.wait_ge(s_m2t, 1)
                    dve.tensor_copy(w_m2t[:, :], bank[1][:, 0:F]).then_inc(s_m2ts, 1)
                    dve.wait_ge(s_fold, 2)
                    dve.tensor_copy(w_u1m[:, :], bank[2][:, 0:F]).then_inc(s_done, 1)
                    dve.tensor_tensor(u1m_bias[:, :], bank[3][:, 0:1], u1_bias[:, :], ALU.add).then_inc(s_done, 1)

                @block.tensor
                def _(pe):
                    pe.wait_ge(s_ident, 1)
                    pe.wait_ge(s_flags, 8)
                    for k, table in enumerate((rows[:, 0, :], flags[:, 2, :], flags[:, 3, :], flags[:, 4, :],
                                               rows[:, 1, :], flags[:, 1, :])):
                        pe.transpose(bank[4 * (k // 4)][:, (k % 4) * P:(k % 4 + 1) * P], table, ident[:, :]).then_inc(s_tabs, 1)
                    wait_weights(pe)
                    pe.transpose(bank[1][:, 0:F], w_m2[:, :], ident[:, :]).then_inc(s_m2t, 1)
                    pe.wait_ge(s_m2ts, 1)
                    pe.matmul(bank[2][:, 0:F], w_m2t[:, :], w_u1b[:, :], start=True, stop=True).then_inc(s_fold, 1)
                    pe.matmul(bank[3][:, 0:1], w_u1b[:, :], mb2_col[:, :], start=True, stop=True).then_inc(s_fold, 1)

                @block.sync
                def _(sp):
                    sp.wait_ge(s_flags, 6)
                    sp.dma_start(same_dram.rearrange("(t p) -> t p", p=P), flags[0:TILES, 0, :]).then_inc(s_scratch, 16)
                    sp.wait_ge(s_scan, 4)
                    sp.dma_start(scan_dram.rearrange("k (t p) -> t k p", p=P), scan_flags[0:TILES]).then_inc(s_scratch, 16)
                    sp.dma_start(more_dram.rearrange("(t p) -> t p", p=P), flags[0:TILES, 5, :]).then_inc(s_scratch, 16)
                    for c in range(2):
                        sp.dma_start(attr_dram[c].rearrange("(t p) -> t p", p=P), attr2[0:TILES, c, :]).then_inc(s_scratch, 16)
                    sp.wait_ge(s_scratch, 80)

        ADD, SCALE, OUT = 5, 6, 7
        NORM1, NORM2, NORM3 = 0, 1, 2
        t_v, t_w, t_xb, t_y, t_nm, t_out = [sem("t_" + s) for s in ("sum", "gamma", "residual", "scaled", "shift", "out")]
        b_st = [sem(f"b_stats{i + 1}") for i in range(3)]
        b_half, b_spread, b_mv, b_sd, b_rs = [sem("b_" + s) for s in ("halves", "spread", "means", "deviation", "inverse")]
        BATCHES = GROUPS + SCALE

        def tail_buffers(tag, ctx):
            return {
                "v": sb(f"{tag}_v", [P, 2, QUAD, F], F32, ctx), "w": sb(f"{tag}_w", [P, 4, QUAD, F], F32, ctx),
                "xb": sb(f"{tag}_xb", [P, 2, QUAD, F], F32, ctx), "st": sb(f"{tag}_st", [P, 2, 3, QUAD, 6], F32, ctx),
                "mid": sb(f"{tag}_mid", [P, 3, QUAD, 2], F32, ctx), "mv": sb(f"{tag}_mv", [P, 2, 3, QUAD, 2], F32, ctx),
                "sd": sb(f"{tag}_sd", [P, 3, QUAD], F32, ctx), "rs": sb(f"{tag}_rs", [P, 2, 3, QUAD], F32, ctx),
                "nm": sb(f"{tag}_nm", [P, 2, QUAD], F32, ctx)}

        def stats(dve, rows_in, st, rows=range(QUAD)):
            for j in rows:
                ins = dve.bn_stats(st[:, j, :], rows_in[:, j, :])
            return ins

        def batch_halves(dve, n, slot, B):
            st, mid, mv = B["st"][:, slot], B["mid"], B["mv"][:, slot]
            dve.tensor_tensor(mv[:, :, :, 0:2], st[:, :, :, 1:3], st[:, :, :, 4:6], ALU.add).then_inc(b_half, 1)
            dve.tensor_tensor(mid[:, :, :, 0], st[:, :, :, 1], st[:, :, :, 4], ALU.subtract).then_inc(b_half, 1)

        def batch_spread(dve, n, slot, B):
            mid = B["mid"]
            dve.wait_ge(b_half, 2 * (n + 1))
            dve.scalar_tensor_tensor(mid[:, :, :, 1], mid[:, :, :, 0], F / 4.0, mid[:, :, :, 0], ALU.mult, ALU.mult).then_inc(b_spread, 1)

        def batch_variance(dve, n, slot, B):
            mid, mv = B["mid"], B["mv"][:, slot]
            dve.wait_ge(b_spread, n + 1)
            dve.tensor_tensor(mv[:, :, :, 1], mv[:, :, :, 1], mid[:, :, :, 1], ALU.add).then_inc(b_mv, 1)

        def batch_root(act, n, slot, B):
            need(act, b_rs, n)
            act.wait_ge(b_mv, n + 1)
            act.activation(B["sd"][:, :, :], B["mv"][:, slot, :, :, 1], ACT.Sqrt, bias=eps_col[:, 0:1],
                           scale=1.0 / F).then_inc(b_sd, 1)

        def batch_inverse(dve, n, slot, B):
            dve.wait_ge(b_sd, n + 1)
            dve.reciprocal(B["rs"][:, slot], B["sd"][:, :, :]).then_inc(b_rs, 1)

        def tail_add(dve, g, B, pV, c_V, count, x1_rows):
            need(dve, t_w, g.n - 1)
            dve.wait_ge(c_V, count)
            dve.tensor_tensor(B["v"][:, g.slot % 2], split(pV[:, :]), x1_rows, ALU.add).then_inc(t_v, 1)

        def tail_shift(dve, g, n, slot, B):
            need(dve, t_out, g.n - 1)
            dve.wait_ge(b_rs, n + 1)
            dve.scalar_tensor_tensor(B["nm"][:, g.slot % 2, :], B["mv"][:, slot, NORM3, :, 0], -0.5, B["rs"][:, slot, NORM3, :],
                                     ALU.mult, ALU.mult).then_inc(t_nm, 1)

        def tail_scale(dve, g, n, slot, B, xb_rows, c_xb, count):
            dve.wait_ge(b_rs, n + 1)
            dve.wait_ge(t_w, g.n + 1)
            dve.wait_ge(c_xb, count)
            for j in range(QUAD):
                w = B["w"][:, g.slot, j, :]
                ins = dve.scalar_tensor_tensor(w, w, B["rs"][:, slot, NORM2, j:j + 1], xb_rows[:, j, :],
                                               ALU.mult, ALU.add)
            ins.then_inc(t_y, 1)

        def along(v):
            return v[:, :].unsqueeze(1).broadcast_to([P, QUAD, F])

        def tail_residual(pool, g, B, x1_rows):
            need(pool, t_y, g.n - 1)
            pool.tensor_tensor(B["xb"][:, g.slot % 2], x1_rows, along(beta_b), ALU.add).then_inc(t_xb, 1)

        def tail_gamma(pool, g, B):
            need(pool, t_out, g.n - 3)
            pool.wait_ge(t_v, g.n + 1)
            pool.tensor_tensor(B["w"][:, g.slot], B["v"][:, g.slot % 2], along(gamma_b), ALU.mult).then_inc(t_w, 1)

        def tail_out(act, g, slot, B, out_rows):
            act.wait_ge(t_nm, g.n + 1)
            for j in range(QUAD):
                ins = act.activation(out_rows[:, j, :], B["w"][:, g.slot, j, :], ACT.Identity,
                                     bias=B["nm"][:, g.slot % 2, j:j + 1], scale=B["rs"][:, slot, NORM3, j:j + 1])
            ins.then_inc(t_out, 1)

        scans_only = whole.enter_context(ExitStack())
        least = sb("least", [P, 4], F32, scans_only)
        same_f, more_f = [sb(n, [P, BE], BF16, scans_only) for n in ("same_f", "more_f")]
        SAME, APART_F, MORE, APART_L = range(4)
        s_flag = [sem(f"s_flag{i}") for i in range(4)]

        def load_flags(sp, kind, dest):
            for b in range(BLOCKS):
                sp.dma_start(dest[b * RH:(b + 1) * RH, :],
                             scan_dram[kind:kind + 1, b * BE:(b + 1) * BE].broadcast_to([RH, BE])).then_inc(s_flag[kind], 16)

        with ExitStack() as ctx:
            x_in = sb("x_in", [P, 2, 8 * F], F32, ctx)
            x_t = sb("x_t", [P, 2, GROUP], F32, ctx)
            x1 = sb("x1", [P, 2, 8, F], F32, ctx)
            x1_t = sb("x1_t", [P, 2, GROUP], F32, ctx)
            hid_t = sb("hid_t", [P, 2, GROUP], F32, ctx)
            o_out = sb("o_out", [P, 2, 8, F], F32, ctx)
            B = tail_buffers("n", ctx)
            e_rows = sb("e_rows", [P, 2 * QUAD, F], F32, ctx)
            e_idx = sb("e_idx", [P, 2 * QUAD], I32, ctx)
            e_t = sb("e_t", [P, 2, GROUP], F32, ctx)
            l_low = sb("l_low", [P, QUAD * RH], F32, ctx)
            l_leaky = sb("l_leaky", [P, QUAD * RH], F32, ctx)
            pT, pS, pX, pU, pV, pE, pL = bank[0], bank[1:3], bank[3], bank[4], bank[5], bank[6], bank[7]

            s_x = [sem(f"s_x{i}") for i in range(2)]
            s_x1 = [sem(f"s_x1out{i}") for i in range(2)]
            s_out = [sem(f"s_out{i}") for i in range(2)]
            c_zero, c_T, c_xt, c_S, c_x1, c_X, c_x1t, c_U, c_hid, c_V = [sem("c_" + s) for s in (
                "zero", "T", "xt", "S", "x1", "X", "x1t", "U", "hid", "V")]
            e_got = [sem(f"e_got{i}") for i in range(2)]
            e_ix, e_T, e_ts, e_kept, e_L, e_low, e_lk, e_log = [sem("e_" + s) for s in (
                "ix", "T", "ts", "kept", "L", "low", "lk", "log")]

            def wait_stored(eng):
                for q in range(2):
                    count = 16 * (EG - 1) + (32 if q == 0 else 0)
                    eng.wait_ge(s_x1[q], count)
                    eng.wait_ge(s_out[q], count)

            def rows_of(buf, g):
                return buf[:, g.slot // 2, 4 * (g.slot % 2):4 * (g.slot % 2) + 4, :]

            def steps(eng, step):
                for turn in range(3):
                    for k in range(4):
                        step(turn, k)
                with eng.Fori(3, EG - 1) as turn:
                    for k in range(4):
                        step(turn, k)
                for turn in (EG - 1, EG, EG + 1):
                    for k in range(4):
                        step(turn, k)

            def at(turn, k, offset):
                return behind(turn, k, 4, offset, GROUPS)

            def batch(turn, k, offset=0):
                n = 4 * turn + k - offset
                real = 0 <= n < BATCHES if isinstance(n, int) else True
                return n, (k - offset) % 2, real

            def turn_has_logits(turn):
                return not isinstance(turn, int) or 1 <= turn <= EG

            def has_edges(turn):
                return not isinstance(turn, int) or turn < EG

            with nc.Block() as block:
                @block.sync
                def _(sp):
                    def view(dram, turn, q):
                        s = 2 * turn + q
                        base = TAIL if isinstance(s, int) and s == SUPERS - 1 else s * SUPER
                        return dram[bass.ds(base, SUPER), :].rearrange("(p j) f -> p (j f)", p=P)

                    def load(turn, q):
                        if isinstance(turn, int) and 2 * turn + q >= SUPERS:
                            return
                        need(sp, c_T, 4 * turn + 2 * q - 2)
                        sp.dma_start(x_in[:, q, :], view(x, turn, q)).then_inc(s_x[q], 16)

                    def store(turn, q, buf, dram, ready, done):
                        if isinstance(turn, int) and not 0 <= 2 * turn + q < SUPERS:
                            return
                        sp.wait_ge(ready, 4 * turn + 2 * q + 2)
                        flat = buf[:, q].rearrange("p j f -> p (j f)")
                        to = view(dram, turn, q)
                        if isinstance(turn, int) and 2 * turn + q == SUPERS - 1:
                            for lo, hi in ((SKIP, 32), (32, P)):
                                sp.dma_start(to[lo:hi, :], flat[lo:hi, :]).then_inc(done[q], 16)
                        else:
                            sp.dma_start(to, flat).then_inc(done[q], 16)

                    def turn_of(turn):
                        load(turn + 1, 0)
                        store(turn, 0, x1, x1_dram, c_x1, s_x1)
                        store(turn - 1, 0, o_out, out, t_out, s_out)
                        load(turn + 1, 1)
                        store(turn, 1, x1, x1_dram, c_x1, s_x1)
                        store(turn - 1, 1, o_out, out, t_out, s_out)
                    load(0, 0)
                    load(0, 1)
                    load_flags(sp, MORE, more_f)
                    load_flags(sp, SAME, same_f)
                    turn_of(0)
                    turn_of(1)
                    with sp.Fori(2, EG - 2) as turn:
                        turn_of(turn)
                    for turn in range(EG - 2, EG + 1):
                        turn_of(turn)
                    for kind in (MORE, SAME):
                        sp.wait_ge(s_flag[kind], 16 * BLOCKS)

                @block.gpsimd
                def _(pool):
                    def indices(e, half):
                        need(pool, e_T, 2 * e + half - 1)
                        pool.tensor_copy(e_idx[:, 4 * half:4 * half + 4],
                                         (idx_src, idx_dst)[half][:, bass.ds(e * QUAD, QUAD)]).then_inc(e_ix, 1)
                        pool.wait_ge(e_ix, 2 * e + half + 1)

                    def gather(half):
                        for j in range(4 * half, 4 * half + 4):
                            pool.indirect_dma_start(e_rows[:, j, :], None, x[:, :],
                                                    bass.IndirectOffsetOnAxis(ap=e_idx[:, j:j + 1], axis=0)).then_inc(e_got[half], 16)

                    pool.memset(B["st"][:, :, :, :, :], 0.0).then_inc(c_zero, 1)

                    for half in range(2):
                        indices(0, half)
                        gather(half)

                    def step(turn, k):
                        ahead = has_edges(turn + 1) and k >= 2
                        if ahead:
                            indices(turn + 1, k - 2)
                        g = at(turn, k, ADD)
                        if g.real:
                            pool.wait_ge(c_x1, g.n + 1)
                            tail_residual(pool, g, B, rows_of(x1, g))
                        if ahead:
                            gather(k - 2)
                        if g.real:
                            tail_gamma(pool, g, B)
                    steps(pool, step)

                @block.tensor
                def _(pe):
                    def step(turn, k):
                        g = at(turn, k, ADD)
                        if g.real:
                            pe.wait_ge(c_hid, g.n + 1)
                            need(pe, t_v, g.n)
                            pe.matmul(pV[:, :], ones_b[:, :], along(u2b3), start=True, stop=False)
                            for j in range(QUAD):
                                ins = pe.matmul(pV[:, j * F:(j + 1) * F], hid_t[:, g.slot % 2, j * P:(j + 1) * P],
                                                w_u2[:, :], start=False, stop=(j == QUAD - 1))
                            ins.then_inc(c_V, 1)
                        g = at(turn, k, 4)
                        if g.real:
                            pe.wait_ge(c_x1t, g.n + 1)
                            need(pe, c_hid, g.n)
                            pe.matmul(pU[:, :], w_u1x[:, :], x1_t[:, g.slot % 2, :], start=True, stop=True).then_inc(c_U, 1)
                        g = at(turn, k, 1)
                        if g.real:
                            pe.wait_ge(c_xt, g.n + 1)
                            need(pe, c_x1, g.n - 1)
                            to = pS[g.slot % 2]
                            pe.matmul(to[:, :], ones_b[:, :], along(lang3c), start=True, stop=False)
                            for j in range(QUAD):
                                ins = pe.matmul(to[:, j * F:(j + 1) * F], x_t[:, g.slot % 2, j * P:(j + 1) * P],
                                                w_self_id[:, :], start=False, stop=(j == QUAD - 1))
                            ins.then_inc(c_S, 1)
                        g = at(turn, k, 0)
                        if g.real:
                            pe.wait_ge(s_x[g.slot // 2], 16 * (g.turn + 1))
                            need(pe, c_xt, g.n)
                            for j in range(QUAD):
                                r = 4 * (g.slot % 2) + j
                                ins = pe.transpose(pT[:, j * P:(j + 1) * P], x_in[:, g.slot // 2, r * F:(r + 1) * F], ident[:, :])
                            ins.then_inc(c_T, 1)
                        g = at(turn, k, 3)
                        if g.real:
                            pe.wait_ge(c_x1, g.n + 1)
                            need(pe, c_x1t, g.n)
                            for j in range(QUAD):
                                ins = pe.transpose(pX[:, j * P:(j + 1) * P], rows_of(x1, g)[:, j, :], ident[:, :])
                            ins.then_inc(c_X, 1)
                        if has_edges(turn) and k in (1, 2):
                            pe.wait_ge(e_got[k - 1], 64 * (turn + 1))
                            need(pe, e_ts, 2 * turn + k - 1)
                            need(pe, e_kept, 2 * turn + k - 1)
                            for j in range(QUAD):
                                ins = pe.transpose(pE[:, j * P:(j + 1) * P], e_rows[:, QUAD * (k - 1) + j, :], ident[:, :])
                            ins.then_inc(e_T, 1)
                        if has_edges(turn) and k == 3:
                            pe.wait_ge(e_ts, 2 * turn + 2)
                            need(pe, e_low, turn)
                            need(pe, e_lk, turn)
                            for j in range(QUAD):
                                pe.matmul(pL[:, j * RH:(j + 1) * RH], e_t[:, 0, j * P:(j + 1) * P], w_log_s[:, :],
                                          start=True, stop=False)
                                ins = pe.matmul(pL[:, j * RH:(j + 1) * RH], e_t[:, 1, j * P:(j + 1) * P], w_log_d[:, :],
                                                start=False, stop=True)
                            ins.then_inc(e_L, 1)
                    steps(pe, step)

                @block.scalar
                def _(act):
                    def step(turn, k):
                        g = at(turn, k, 4)
                        if g.real:
                            act.wait_ge(c_U, g.n + 1)
                            need(act, c_V, g.n - 1)
                            act.activation(hid_t[:, g.slot % 2, :], pU[:, :], ACT.Relu, bias=u1_bias[:, 0:1]).then_inc(c_hid, 1)
                        n, slot, real = batch(turn, k, 1)
                        if real:
                            batch_root(act, n, slot, B)
                        g = at(turn, k, 0)
                        if g.real:
                            act.wait_ge(c_T, g.n + 1)
                            need(act, c_S, g.n - 1)
                            act.copy(x_t[:, g.slot % 2, :], pT[:, :]).then_inc(c_xt, 1)
                        g = at(turn, k, 3)
                        if g.real:
                            act.wait_ge(c_X, g.n + 1)
                            need(act, c_U, g.n - 1)
                            act.copy(x1_t[:, g.slot % 2, :], pX[:, :]).then_inc(c_x1t, 1)
                        g, (n, slot, _) = at(turn, k, 2), batch(turn, k, 1)
                        if g.real:
                            act.wait_ge(b_rs, n + 1)
                            need(act, s_x1[g.slot // 2], 16 * g.turn)
                            need(act, t_xb, g.n - 3)
                            need(act, t_v, g.n - 3)
                            for j in range(QUAD):
                                ins = act.activation(rows_of(x1, g)[:, j, :], pS[g.slot % 2][:, j * F:(j + 1) * F], ACT.Copy,
                                                     scale=B["rs"][:, slot, NORM1, j:j + 1])
                            ins.then_inc(c_x1, 1)
                        if has_edges(turn) and k in (1, 2):
                            c = k - 1
                            act.wait_ge(e_T, 2 * turn + c + 1)
                            need(act, e_L, turn)
                            act.copy(e_t[:, c, :], pE[:, :]).then_inc(e_ts, 1)
                            act.copy((src_t, dst_t)[c][:, bass.ds(turn * GROUP, GROUP)], pE[:, :]).then_inc(e_kept, 1)
                        g, (n, slot, _) = at(turn, k, OUT), batch(turn, k, 1)
                        if g.real:
                            need(act, s_out[g.slot // 2], 16 * g.turn)
                            tail_out(act, g, slot, B, rows_of(o_out, g))
                    steps(act, step)

                @block.vector
                def _(dve):
                    dve.wait_ge(c_zero, 1)

                    def step(turn, k):
                        b, a, c, f = at(turn, k, 1), at(turn, k, ADD), at(turn, k, SCALE), at(turn, k, OUT)
                        n, slot, real = batch(turn, k)
                        before, old, had = batch(turn, k, 1)

                        logits, before_e = k == 0 and turn_has_logits(turn), turn - 1
                        if real:
                            need(dve, b_half, 2 * (n - 1))
                        if a.real:
                            tail_add(dve, a, B, pV, c_V, a.n + 1, rows_of(x1, a))
                        if had:
                            for norm, offset in ((NORM1, 2), (NORM2, ADD + 1), (NORM3, SCALE + 1)):
                                g = at(turn, k, offset)
                                if g.real:
                                    dve.wait_ge(b_st[norm], g.n + 1)
                            batch_halves(dve, before, old, B)
                        if a.real:
                            dve.wait_ge(t_v, a.n + 1)
                            stats(dve, B["v"][:, a.slot % 2], B["st"][:, slot, NORM2], (0,))
                        if had:
                            batch_spread(dve, before, old, B)
                        if a.real:
                            stats(dve, B["v"][:, a.slot % 2], B["st"][:, slot, NORM2], (1,))
                        if had:
                            batch_variance(dve, before, old, B)
                        if a.real:
                            stats(dve, B["v"][:, a.slot % 2], B["st"][:, slot, NORM2], (2, 3)).then_inc(b_st[NORM2], 1)
                        if b.real:
                            dve.wait_ge(c_S, b.n + 1)
                            stats(dve, split(pS[b.slot % 2][:, :]), B["st"][:, slot, NORM1], (0, 1, 2))
                        if logits:
                            dve.wait_ge(e_L, before_e + 1)
                            dve.tensor_scalar(l_low[:, :], pL[:, 0:QUAD * RH], SLOPE, None, ALU.mult).then_inc(e_low, 1)
                        if had:
                            need(dve, c_x1, min(before - 2, GROUPS) if isinstance(before, int) else before - 2)
                            need(dve, t_out, before - 7)
                            batch_inverse(dve, before, old, B)
                        if logits:
                            dve.wait_ge(e_low, before_e + 1)
                            dve.tensor_tensor(l_leaky[:, :], pL[:, 0:QUAD * RH], l_low[:, :], ALU.max).then_inc(e_lk, 1)
                        if c.real:
                            tail_scale(dve, c, before, old, B, B["xb"][:, c.slot % 2], t_xb, c.n + 1)
                        if f.real:
                            tail_shift(dve, f, before, old, B)
                        if b.real:
                            stats(dve, split(pS[b.slot % 2][:, :]), B["st"][:, slot, NORM1], (3,)).then_inc(b_st[NORM1], 1)
                        if c.real:
                            dve.wait_ge(t_y, c.n + 1)
                            stats(dve, B["w"][:, c.slot], B["st"][:, slot, NORM3]).then_inc(b_st[NORM3], 1)
                        if logits:
                            dve.wait_ge(e_lk, before_e + 1)
                            dve.tensor_tensor(
                                logit[:, bass.ds(before_e * QUAD * RH, QUAD * RH)].rearrange("p (t h) -> p t h", h=H),
                                l_leaky[:, :].rearrange("p (t h) -> p t h", h=H),
                                off_rel[:, bass.ds(before_e * QUAD * R, QUAD * R)].unsqueeze(2).broadcast_to([P, QUAD * R, H]),
                                ALU.add).then_inc(e_log, 1)
                    steps(dve, step)

        weight = logit
        with ExitStack() as ctx:
            buf0 = sb("buf0", [P, BE], F32, ctx)
            buf1 = sb("buf1", [P, BE], F32, ctx)
            buf2 = sb("buf2", [P, BE], F32, ctx)
            buf3 = sb("buf3", [P, BE], F32, ctx)
            apart_f, apart_l = [sb(n, [P, BE], BF16, ctx) for n in ("apart_f", "apart_l")]
            carry = sb("carry", [P, 5], F32, ctx)
            DEN = BT * BLOCKS * H
            den, den_inv = buf0[:, 0:DEN], buf0[:, DEN:2 * DEN]
            counts = sb("counts", [TILES, P], F32, ctx)
            rcounts = sb("rcounts", [TILES, P], F32, ctx)
            s_pack, s_packed, s_vec, s_exp, s_back, s_backed, s_den = (
                sem("s_pack"), sem("s_packed"), sem("s_vec"), sem("s_exp"), sem("s_back"), sem("s_backed"), sem("s_den"))
            s_order = sem("s_order")
            s_pen_ready, s_arg_ready, s_den_ready, s_count_ready, s_count, s_counted, s_rc_ready, s_rc = [sem("s_" + n) for n in (
                "pen_ready", "arg_ready", "den_ready", "count_ready", "count", "counted", "rc_ready", "rc")]
            s_weight = sem("s_weight")
            BANKS_USED = -(-BT // QUAD)
            BH = BLOCKS * H
            DEN_BANKS = (bank[7], bank[0])
            PER = 512 // BH
            assert BT <= 2 * PER and BANKS_USED <= 7

            def cols(q):
                return min(QUAD, BT - QUAD * q)

            with nc.Block() as block:
                @block.sync
                def _(sp):
                    wait_stored(sp)
                    load_flags(sp, APART_F, apart_f)
                    load_flags(sp, APART_L, apart_l)
                    sp.wait_ge(s_count_ready, 1)
                    for b in range(BLOCKS):
                        sp.dma_start(count_dram[b:b + 1, :], buf2[b * RH:b * RH + 1, :]).then_inc(s_count, 16)
                    sp.wait_ge(s_count, 16 * BLOCKS)
                    sp.dma_start(counts[:, :], count_dram.rearrange("b (i p) -> (b i) p", p=P)).then_inc(s_counted, 16)
                    sp.wait_ge(s_rc_ready, 1)
                    sp.dma_start(rcnt_dram.rearrange("(t p) -> t p", p=P), rcounts[:, :]).then_inc(s_rc, 16)
                    sp.wait_ge(s_rc, 16)

                @block.tensor
                def _(pe):
                    def to_bank(i):
                        return bank[i // QUAD][:, (i % QUAD) * P:(i % QUAD + 1) * P]

                    pe.wait_ge(s_order, 1)
                    for i in range(BT):
                        pe.transpose(to_bank(i), buf1[:, i * P:(i + 1) * P], ident[:, :]).then_inc(s_pack, 1)
                    pe.wait_ge(s_pen_ready, 1)
                    for i in range(BT):
                        if i % QUAD == 0:
                            pe.wait_ge(s_packed, i // QUAD + 1)
                        pe.transpose(to_bank(i), buf3[:, i * P:(i + 1) * P], ident[:, :]).then_inc(s_back, 1)
                    pe.wait_ge(s_exp, 1)
                    for i in range(BT):
                        if i % QUAD == 0:
                            pe.wait_ge(s_backed, i // QUAD + 1)
                        pe.transpose(to_bank(i), buf1[:, i * P:(i + 1) * P], ident[:, :]).then_inc(s_back, 1)
                    pe.wait_ge(s_backed, 2 * BANKS_USED)
                    for i in range(BT):
                        if i % PER == 0:
                            pe.wait_ge(s_den_ready, i // PER + 1)
                        pe.matmul(DEN_BANKS[i // PER][:, (i % PER) * BH:(i % PER + 1) * BH], buf2[:, i * P:(i + 1) * P],
                                  select[:, :], start=True, stop=True).then_inc(s_den, 1)

                @block.scalar
                def _(act):
                    wait_stored(act)
                    act.copy(buf1[:, :].rearrange("p (i b c) -> p i b c", b=BLOCKS, c=RH),
                             logit[:, :].rearrange("p (b i c) -> p i b c", b=BLOCKS, c=RH)).then_inc(s_order, 1)
                    for q in range(BANKS_USED):
                        act.wait_ge(s_pack, QUAD * q + cols(q))
                        act.copy(buf0[:, q * GROUP:q * GROUP + cols(q) * P], bank[q][:, 0:cols(q) * P]).then_inc(s_packed, 1)
                    act.wait_ge(s_arg_ready, 1)
                    act.activation(buf1[:, :], buf1[:, :], ACT.Exp, scale=-1.0).then_inc(s_exp, 1)
                    for q in range(BANKS_USED):
                        act.wait_ge(s_back, QUAD * q + cols(q))
                        frm = bank[q][:, 0:cols(q) * P].rearrange("p (i b r h) -> p i b r h", b=BLOCKS, r=R, h=H)
                        to = absent[:, :].rearrange("p (b i r) -> p i b r", b=BLOCKS, r=R)
                        act.copy(to[:, QUAD * q:QUAD * q + cols(q)], frm[:, :, :, :, 0]).then_inc(s_backed, 1)
                    for q in range(BANKS_USED):
                        act.wait_ge(s_back, BT + QUAD * q + cols(q))
                        frm = bank[q][:, 0:cols(q) * P].rearrange("p (i b c) -> p i b c", b=BLOCKS, c=RH)
                        to = weight[:, :].rearrange("p (b i c) -> p i b c", b=BLOCKS, c=RH)
                        act.copy(to[:, QUAD * q:QUAD * q + cols(q)], frm).then_inc(s_backed, 1)

                @block.vector
                def _(dve):
                    chain = [0]

                    def link(ins):
                        chain[0] += 1
                        ins.then_inc(s_vec, 1)
                        dve.wait_ge(s_vec, chain[0])

                    def quarter(v, b):
                        return v[b * RH:(b + 1) * RH]

                    def run(outp, data0, data1, op0, op1, n, thr, start, forward, done=None):
                        order = slice(None, None, 1 if forward else -1)
                        edge = slice(BE - 1, BE) if forward else slice(0, 1)
                        link(dve.memset(carry[:, n:n + 1], start))
                        link(dve.tensor_tensor_scan(outp[:, order], data0[:, order], data1[:, order], start, op0, op1))
                        for b in range(BLOCKS - 1):
                            here, there = (b, b + 1) if forward else (BLOCKS - 1 - b, BLOCKS - 2 - b)
                            link(dve.scalar_tensor_tensor(
                                quarter(carry, there)[:, n:n + 1], quarter(carry, here)[:, n:n + 1],
                                quarter(least, here)[:, thr:thr + 1], quarter(outp, here)[:, edge], op0, op1))
                        ins = dve.tensor_tensor_scan(outp[:, order], data0[:, order], data1[:, order],
                                                     carry[:, n:n + 1], op0, op1)
                        if done is None:
                            link(ins)
                        else:
                            ins.then_inc(done, 1)

                    for k, v in ((MORE, more_f), (SAME, same_f)):
                        dve.wait_ge(s_flag[k], 16 * BLOCKS)
                        link(dve.tensor_reduce(least[:, k:k + 1], v[:, :], AX_X, ALU.min))
                        link(dve.tensor_scalar(least[:, k + 1:k + 2], least[:, k:k + 1], 1.0, -NEG, ALU.subtract, ALU.mult))
                        if k == MORE:
                            wait_stored(dve)
                            run(buf2, more_f, ones_b[:, 0:1].broadcast_to([P, BE]), ALU.mult, ALU.add, 2, MORE, 0.0, False,
                                s_count_ready)
                    dve.wait_ge(s_flag[APART_F], 16 * BLOCKS)
                    dve.wait_ge(s_flag[APART_L], 16 * BLOCKS)
                    dve.wait_ge(s_packed, BANKS_USED)
                    run(buf3, apart_f, buf0, ALU.add, ALU.max, 0, APART_F, NEG, True)
                    dve.wait_ge(s_count, 16 * BLOCKS)
                    run(buf2, apart_l, buf3, ALU.add, ALU.max, 1, APART_L, NEG, False)
                    dve.scalar_tensor_tensor(buf1[:, :], buf2[:, :], 0.1 * NEG, buf0[:, :], ALU.max, ALU.subtract).then_inc(s_arg_ready, 1)
                    dve.tensor_scalar(buf3[:, :], buf2[:, :], 0.1 * NEG, NEG, ALU.is_lt, ALU.mult).then_inc(s_pen_ready, 1)
                    dve.wait_ge(s_counted, 16)
                    dve.reciprocal(rcounts[:, :], counts[:, :]).then_inc(s_rc_ready, 1)
                    dve.wait_ge(s_exp, 1)
                    run(buf0, same_f, buf1, ALU.mult, ALU.add, 3, SAME, 0.0, True)
                    dve.wait_ge(s_back, BT)
                    run(buf3, more_f, buf0, ALU.mult, ALU.max, 4, MORE, 0.0, False)
                    for i in range(0, BT, PER):
                        part_of = slice(i * P, min(BT, i + PER) * P)
                        dve.scalar_tensor_tensor(buf2[:, part_of], buf1[:, part_of], 0.0, buf3[:, part_of],
                                                 ALU.is_gt, ALU.mult).then_inc(s_den_ready, 1)
                    for i in range(0, BT, PER):
                        part_of = slice(i * BH, min(BT, i + PER) * BH)
                        dve.wait_ge(s_den, min(BT, i + PER))
                        link(dve.tensor_scalar(den[:, part_of], DEN_BANKS[i // PER][:, 0:min(PER, BT - i) * BH], 1e-30, None, ALU.max))
                        link(dve.reciprocal(den_inv[:, part_of], den[:, part_of]))
                    dve.wait_ge(s_backed, 2 * BANKS_USED)
                    for b in range(BLOCKS):
                        w = weight[:, b * BT * RH:(b + 1) * BT * RH].rearrange("p (i r h) -> p i r h", r=R, h=H)
                        by = den_inv.rearrange("p (i b h) -> p i b h", b=BLOCKS, h=H)[:, :, b, :]
                        dve.tensor_tensor(w, w, by.unsqueeze(2).broadcast_to([P, BT, R, H]), ALU.mult).then_inc(s_weight, 1)

        scans_only.close()

        with ExitStack() as ctx:
            same_g = sb("same_g", [P, 2, GROUP], F32, ctx)
            s_t = sb("s_t", [P, 2, GROUP], F32, ctx)
            d_t = sb("d_t", [P, 2, GROUP], F32, ctx)
            val = sb("val", [P, 2, R * F], F32, ctx)
            rel_t = sb("rel_t", [P, R, GROUP], F32, ctx)
            act_t = sb("act_t", [P, R, GROUP], F32, ctx)
            tails = sb("tails", [P, R], F32, ctx)
            ent = sb("ent", [P, 2, QUAD, 6 * EB], F32, ctx)
            lg = sb("lg", [P, QUAD * K5 * H], F32, ctx)
            lg2 = sb("lg2", [P, QUAD * K5 * H], F32, ctx)
            ex = sb("ex", [P, QUAD * K5 * H], F32, ctx)
            top = sb("top", [P, QUAD * H], F32, ctx)
            rsum = sb("rsum", [P, QUAD * H], F32, ctx)
            rinv = sb("rinv", [P, QUAD * H], F32, ctx)
            z_e = sb("z_e", [P, 2, QUAD, F], F32, ctx)
            x1_e = sb("x1_e", [P, 2, QUAD, F], F32, ctx)
            st_e = sb("st_e", [P, QUAD, 6], F32, ctx)
            mv_e = sb("mv_e", [P, QUAD, 2], F32, ctx)
            mid_e = sb("mid_e", [P, QUAD, 4], F32, ctx)
            rs_e = sb("rs_e", [P, QUAD], F32, ctx)
            rl_e = sb("rl_e", [P, QUAD], F32, ctx)
            put_ix = sb("put_ix", [P, 2, QUAD], I32, ctx)
            pXW, pM, pE = bank[0:2], bank[2:6], bank[6:8]
            f_hv, f_sp = sem("f_halves"), sem("f_spread")
            f_same = [sem(f"f_same{i}") for i in range(2)]
            f_put = [sem(f"f_put{i}") for i in range(2)]
            f_kept = [sem(f"f_kept{i}") for i in range(2)]
            f_rl = sem("f_rl")
            (f_s, f_d, f_XW, f_val, f_M, f_scan, f_tail, f_gelu, f_E0, f_E1, f_ent0, f_ent1, f_ls, f_ld, f_low, f_lg, f_top, f_arg,
             f_ex, f_sum, f_inv, f_al, f_wt, f_p1, f_p2, f_z, f_st, f_mv, f_rs, f_x1, f_ix) = [sem("f_" + s) for s in (
                "s", "d", "XW", "val", "M", "scan", "tail", "gelu", "E0", "E1", "ent0", "ent1", "ls", "ld", "low", "lg", "top", "arg",
                "ex", "sum", "inv", "al", "wt", "p1", "p2", "z", "st", "mv", "rs", "x1", "ix")]

            def at(turn, k, offset):
                g = behind(turn, k, 4, offset, EG)
                return g._replace(turn=g.turn * 2 + g.slot // 2, slot=g.slot % 2)

            def steps(eng, step):
                for turn in (0, 1):
                    for k in range(4):
                        step(turn, k)
                with eng.Fori(2, EG // 4) as turn:
                    for k in range(4):
                        step(turn, k)
                for turn in (EG // 4, EG // 4 + 1):
                    for k in range(4):
                        step(turn, k)

            def columns(eng, g, to, frm, done):
                eng.tensor_copy(to[:, g.slot, :], frm[:, bass.ds(g.n * GROUP, GROUP)]).then_inc(done, 1)

            def entry(s):
                return ent[:, s].rearrange("p j (k c) -> p j k c", k=6)

            with nc.Block() as block:
                @block.sync
                def _(sp):
                    def step(turn, k):
                        g = at(turn, k, 0)
                        if g.real:
                            need(sp, f_scan, R * (g.n - 1))
                            sp.dma_start(same_g[:, g.slot, :], same_dram[bass.ds(g.n * GROUP, GROUP)].unsqueeze(0)
                                         .broadcast_to([P, GROUP])).then_inc(f_same[g.slot], 16)
                        w = at(turn, k, 4)
                        if w.real:
                            sp.wait_ge(f_x1, w.n + 1)
                            sp.dma_start(reached_dram[bass.ds(w.n * GROUP, GROUP), :].rearrange("(j p) f -> p j f", p=P),
                                         x1_e[:, w.slot]).then_inc(f_kept[w.slot], 16)
                    steps(sp, step)
                    for slot in range(2):
                        sp.wait_ge(f_kept[slot], 16 * ((EG + 1 - slot) // 2))

                @block.tensor
                def _(pe):
                    def product(g, j):
                        need(pe, f_val, 4 * g.n + j - 1)
                        pe.matmul(pXW[j % 2][:, :], s_t[:, g.slot, j * P:(j + 1) * P], w_rel[:, :], start=True, stop=True).then_inc(f_XW, 1)

                    def turn_over(g, j):
                        pe.wait_ge(f_val, 4 * g.n + j + 1)
                        for r in range(R):
                            if j == 0:
                                need(pe, f_scan, R * (g.n - 1) + r + 1)
                            ins = pe.transpose(pM[r][:, j * P:(j + 1) * P], val[:, j % 2, r * F:(r + 1) * F], ident[:, :])
                        ins.then_inc(f_M, 1)

                    def step(turn, k):
                        g, e = at(turn, k, 0), at(turn, k, 1)
                        if g.real:
                            pe.wait_ge(f_s, g.n + 1)
                            product(g, 0)
                            product(g, 1)
                            product(g, 2)
                            turn_over(g, 0)
                            product(g, 3)
                            turn_over(g, 1)
                            turn_over(g, 2)
                            turn_over(g, 3)
                        if e.real:
                            pe.wait_ge(f_gelu, R * (e.n + 1))
                            pe.wait_ge(f_d, e.n + 1)
                            for j in range(QUAD):
                                need(pe, f_ent0, 4 * e.n + j)
                                for r in range(3):
                                    ins = pe.matmul(pE[0][:, r * EB:(r + 1) * EB], act_t[:, r, j * P:(j + 1) * P],
                                                    w_cross[:, :], start=(r == 0), stop=(r == 2), skip_group_check=True)
                                ins.then_inc(f_E0, 1)
                                need(pe, f_ent1, 4 * e.n + j)
                                pe.matmul(pE[1][:, 0:EB], act_t[:, 3, j * P:(j + 1) * P], w_cross[:, :],
                                          start=True, stop=False, skip_group_check=True)
                                pe.matmul(pE[1][:, EB:3 * EB], d_t[:, e.slot, j * P:(j + 1) * P], w_node[:, :],
                                          start=False, stop=False, skip_group_check=True)
                                pe.matmul(pE[1][:, 2 * EB:2 * EB + F], ones_b[:, :], lang3[:, :],
                                          start=False, stop=True, skip_group_check=True).then_inc(f_E1, 1)
                    steps(pe, step)

                @block.scalar
                def _(act):
                    def step(turn, k):
                        g, e, s = at(turn, k, 0), at(turn, k, 1), at(turn, k, 2)
                        if s.real:
                            act.wait_ge(f_arg, s.n + 1)
                            need(act, f_al, s.n)
                            act.activation(ex[:, :], lg[:, :], ACT.Exp).then_inc(f_ex, 1)
                        if e.real:
                            need(act, f_z, e.n - 1)
                            for j in range(QUAD):
                                act.wait_ge(f_E0, 4 * e.n + j + 1)
                                act.copy(ent[:, e.slot, j, 0:3 * EB], pE[0][:, 0:3 * EB]).then_inc(f_ent0, 1)
                                act.wait_ge(f_E1, 4 * e.n + j + 1)
                                act.copy(ent[:, e.slot, j, 3 * EB:6 * EB], pE[1][:, 0:3 * EB]).then_inc(f_ent1, 1)
                        if g.real:
                            need(act, f_E1, 4 * g.n)
                            for r in range(R):
                                act.wait_ge(f_scan, R * g.n + r + 1)
                                act.activation(act_t[:, r, :], rel_t[:, r, :], ACT.Gelu, bias=rel_bias[:, r:r + 1]).then_inc(f_gelu, 1)
                    steps(act, step)

                @block.vector
                def _(dve):
                    def messages(g, j):
                        dve.wait_ge(f_XW, 4 * g.n + j + 1)
                        need(dve, f_M, 4 * g.n + j - 1)
                        dve.tensor_tensor(
                            val[:, j % 2, :].rearrange("p (c d) -> p c d", d=D),
                            pXW[j % 2][:, :].rearrange("p (c d) -> p c d", d=D),
                            weight[:, bass.ds((g.n * QUAD + j) * RH, RH)].unsqueeze(2).broadcast_to([P, RH, D]),
                            ALU.mult).then_inc(f_val, 1)

                    def scale(s, j):
                        e4 = entry(s.slot)[:, j, 0:K5, 0:F].rearrange("p k (h d) -> p k h d", d=D)
                        al = lg2[:, :].rearrange("p (j k h) -> p j k h", j=QUAD, h=H)[:, j]
                        dve.tensor_tensor(e4, e4, al.unsqueeze(3).broadcast_to([P, K5, H, D]), ALU.mult).then_inc(f_wt, 1)

                    columns(dve, at(0, 0, 0), s_t, src_t, f_s)

                    def step(turn, k):
                        ahead, g, s, w, v = (at(turn, k, o) for o in (-1, 0, 2, 3, 4))
                        if g.real:
                            messages(g, 0)
                            messages(g, 1)
                        lg4 = lg[:, :].rearrange("p (j k h) -> p j k h", j=QUAD, h=H)
                        low4 = lg2[:, :].rearrange("p (j k h) -> p j k h", j=QUAD, h=H)
                        if s.real:
                            dve.wait_ge(f_ent1, 4 * (s.n + 1))
                            dve.wait_ge(f_ent0, 4 * (s.n + 1))
                            en = entry(s.slot)
                            dve.tensor_tensor(lg4, en[:, :, 0:K5, F:EB],
                                              en[:, :, K5, F:EB].unsqueeze(2).broadcast_to([P, QUAD, K5, H]), ALU.add).then_inc(f_ls, 1)
                        if v.real:
                            dve.wait_ge(f_rs, v.n + 1)
                            dve.tensor_tensor(rl_e[:, :], rs_e[:, :], last_e[:, bass.ds(v.n * QUAD, QUAD)], ALU.mult).then_inc(f_rl, 1)
                        if s.real:
                            dve.wait_ge(f_ls, s.n + 1)
                            dve.scalar_tensor_tensor(lg2[:, :], lg[:, :], SLOPE, lg[:, :], ALU.mult, ALU.max).then_inc(f_low, 1)
                        if ahead.real:
                            need(dve, f_XW, 4 * (ahead.n - 1))
                            columns(dve, ahead, s_t, src_t, f_s)
                        if s.real:
                            dve.wait_ge(f_low, s.n + 1)
                            dve.tensor_tensor(low4[:, :, 0:R, :], low4[:, :, 0:R, :],
                                              absent[:, bass.ds(s.n * QUAD * R, QUAD * R)].rearrange("p (j r) -> p j r", r=R)
                                              .unsqueeze(3).broadcast_to([P, QUAD, R, H]), ALU.add).then_inc(f_lg, 1)
                            dve.wait_ge(f_lg, s.n + 1)
                            top3 = top[:, :].rearrange("p (j h) -> p j h", h=H)
                            dve.tensor_reduce(top3, low4.rearrange("p j k h -> p j h k"), AX_X, ALU.max).then_inc(f_top, 1)
                            dve.wait_ge(f_top, s.n + 1)
                            dve.tensor_tensor(lg4, low4, top3.unsqueeze(2).broadcast_to([P, QUAD, K5, H]), ALU.subtract).then_inc(f_arg, 1)
                        if v.real:
                            dve.wait_ge(f_rl, v.n + 1)
                            need(dve, f_put[v.slot], 64 * v.turn)
                            need(dve, f_kept[v.slot], 16 * v.turn)
                            for j in range(QUAD):
                                ins = dve.tensor_scalar(x1_e[:, v.slot, j, :], z_e[:, v.slot, j, :], mv_e[:, j, 0:1],
                                                        rl_e[:, j:j + 1], ALU.subtract, ALU.mult)
                            ins.then_inc(f_x1, 1)
                        if g.real:
                            messages(g, 2)
                            messages(g, 3)
                        if s.real:
                            dve.wait_ge(f_ex, s.n + 1)
                            ex4 = ex[:, :].rearrange("p (j k h) -> p j k h", j=QUAD, h=H)
                            sum3 = rsum[:, :].rearrange("p (j h) -> p j h", h=H)
                            dve.tensor_reduce(sum3, ex4.rearrange("p j k h -> p j h k"), AX_X, ALU.add).then_inc(f_sum, 1)
                        if w.real:
                            dve.wait_ge(f_z, w.n + 1)
                            stats(dve, z_e[:, w.slot], st_e).then_inc(f_st, 1)
                        if w.real:
                            dve.wait_ge(f_st, w.n + 1)
                            dve.tensor_tensor(mid_e[:, :, 0:2], st_e[:, :, 1:3], st_e[:, :, 4:6], ALU.add).then_inc(f_hv, 1)
                            dve.tensor_tensor(mid_e[:, :, 2], st_e[:, :, 1], st_e[:, :, 4], ALU.subtract).then_inc(f_hv, 1)
                        if s.real:
                            dve.wait_ge(f_sum, s.n + 1)
                            dve.reciprocal(rinv[:, :], rsum[:, :]).then_inc(f_inv, 1)
                        if w.real:
                            dve.wait_ge(f_hv, 2 * (w.n + 1))
                            dve.scalar_tensor_tensor(mid_e[:, :, 3], mid_e[:, :, 2], 0.25, mid_e[:, :, 2], ALU.mult, ALU.mult).then_inc(f_sp, 1)
                            dve.tensor_scalar(mid_e[:, :, 1], mid_e[:, :, 1], 1.0 / F, LN_EPS, ALU.mult, ALU.add).then_inc(f_sp, 1)
                            dve.tensor_scalar(mv_e[:, :, 0], mid_e[:, :, 0], 0.5, None, ALU.mult).then_inc(f_mv, 1)
                        if s.real:
                            dve.wait_ge(f_inv, s.n + 1)
                            inv3 = rinv[:, :].rearrange("p (j h) -> p j h", h=H)
                            dve.tensor_tensor(low4, ex4, inv3.unsqueeze(2).broadcast_to([P, QUAD, K5, H]), ALU.mult).then_inc(f_al, 1)
                        if w.real:
                            dve.wait_ge(f_sp, 2 * (w.n + 1))
                            dve.tensor_tensor(mv_e[:, :, 1], mid_e[:, :, 1], mid_e[:, :, 3], ALU.add).then_inc(f_mv, 1)
                        if s.real:
                            dve.wait_ge(f_al, s.n + 1)
                            for j in range(QUAD):
                                scale(s, j)
                        if g.real:
                            dve.wait_ge(f_same[g.slot], 16 * (g.turn + 1))
                            need(dve, f_tail, g.n)
                            for r in range(R):
                                dve.wait_ge(f_M, 4 * (g.n + 1))
                                need(dve, f_gelu, R * (g.n - 1) + r + 1)
                                start = tails[:, r:r + 1] if not isinstance(g.n, int) or g.n > 0 else 0.0
                                dve.tensor_tensor_scan(rel_t[:, r, :], same_g[:, g.slot, :], pM[r][:, :], start,
                                                       ALU.mult, ALU.add).then_inc(f_scan, 1)
                            dve.wait_ge(f_scan, R * (g.n + 1))
                            dve.tensor_copy(tails[:, :], rel_t[:, :, GROUP - 1]).then_inc(f_tail, 1)
                    steps(dve, step)

                @block.gpsimd
                def _(pool):
                    def step(turn, k):
                        g, w, v = at(turn, k, 0), at(turn, k, 3), at(turn, k, 4)
                        if v.real:
                            need(pool, f_put[v.slot], 64 * v.turn)
                            pool.tensor_copy(put_ix[:, v.slot, :], idx_last[:, bass.ds(v.n * QUAD, QUAD)]).then_inc(f_ix, 1)
                            pool.wait_ge(f_mv, 2 * (v.n + 1))
                            need(pool, f_rl, v.n)
                            pool.tensor_tensor(rs_e[:, :], mv_e[:, :, 1], power[:, 0:1].broadcast_to([P, QUAD]), ALU.pow).then_inc(f_rs, 1)
                        if w.real:
                            pool.wait_ge(f_wt, 4 * (w.n + 1))
                            en = entry(w.slot)

                            def plus(a, b, dest, done):
                                pool.tensor_tensor(dest, en[:, :, a, 0:F], en[:, :, b, 0:F], ALU.add).then_inc(done, 1)
                            plus(0, 1, en[:, :, 0, 0:F], f_p1)
                            plus(2, 3, en[:, :, 2, 0:F], f_p1)
                            plus(4, 5, en[:, :, 4, 0:F], f_p1)
                            pool.wait_ge(f_p1, 3 * (w.n + 1))
                            plus(0, 2, en[:, :, 0, 0:F], f_p2)
                            pool.wait_ge(f_p2, w.n + 1)
                        if g.real:
                            need(pool, f_E1, 4 * (g.n - 1))
                            columns(pool, g, d_t, dst_t, f_d)
                        if v.real:
                            pool.wait_ge(f_ix, v.n + 1)
                            pool.wait_ge(f_x1, v.n + 1)
                        if w.real:
                            plus(0, 4, z_e[:, w.slot], f_z)
                        if v.real:
                            for j in range(QUAD):
                                pool.indirect_dma_start(
                                    x1_dram[:, :], bass.IndirectOffsetOnAxis(ap=put_ix[:, v.slot, j:j + 1], axis=0),
                                    x1_e[:, v.slot, j, :], None, bounds_check=N - 1, oob_is_err=False).then_inc(f_put[v.slot], 16)
                    steps(pool, step)
                    for slot in range(2):
                        pool.wait_ge(f_put[slot], 64 * ((EG + 1 - slot) // 2))
        edges_only.close()

        with ExitStack() as ctx:
            more_h = sb("more_h", [P, 4, GROUP], F32, ctx)
            rcnt_h = sb("rcnt_h", [P, 4, GROUP], F32, ctx)
            attr_h = sb("attr_h", [2, 4, GROUP], F32, ctx)
            xs_r = sb("xs_r", [P, 4, QUAD, F], F32, ctx)
            xl_r = sb("xl_r", [P, 4, QUAD, F], F32, ctx)
            xs_t = sb("xs_t", [P, 2, GROUP], F32, ctx)
            xd_t = sb("xd_t", [P, 4, GROUP], F32, ctx)
            msg_t = sb("msg_t", [P, 2, GROUP], F32, ctx)
            sum_t = sb("sum_t", [P, 2, GROUP], F32, ctx)
            mean_t = sb("mean_t", [P, 2, GROUP], F32, ctx)
            up_t = sb("up_t", [P, 2, GROUP], F32, ctx)
            o_e = sb("o_e", [P, 4, QUAD, F], F32, ctx)
            get_ix = sb("get_ix", [P, 4, QUAD], I32, ctx)
            out_ix = sb("out_ix", [P, 4, QUAD], I32, ctx)
            no_ix = sb("no_ix", [P, QUAD], I32, ctx)
            B2 = tail_buffers("e", ctx)
            qS, qD, qH, qU, qV, qR = bank[0], bank[1], bank[2], bank[3], bank[4], bank[5:7]
            TURN, HID, MEAN, ADDED, SCALED, WRITTEN, PUT = range(2, 9)
            h_row = [sem(f"h_row{i}") for i in range(4)]
            h_got = [sem(f"h_got{i}") for i in range(4)]
            h_put = [sem(f"h_put{i}") for i in range(4)]
            h_zero, h_ix, h_T, h_xs, h_xd, h_H, h_msg, h_sum, h_mean, h_U, h_up, h_V, h_R, h_oix = [sem("h_" + s) for s in (
                "zero", "ix", "T", "xs", "xd", "H", "msg", "sum", "mean", "U", "up", "V", "R", "oix")]

            def at(turn, k, offset):
                return behind(turn, k, 4, offset, EG)

            def late(g):
                return g._replace(n=g.n + GROUPS)

            def batch(turn, k, offset=0):
                n = 4 * turn + k - offset
                real = 0 <= n < EG + SCALED if isinstance(n, int) else True
                return n + BATCHES, (k - offset) % 2, real

            def steps(eng, step):
                for turn in range(3):
                    for k in range(4):
                        step(turn, k)
                with eng.Fori(3, EG // 4) as turn:
                    for k in range(4):
                        step(turn, k)
                for turn in range(EG // 4, EG // 4 + 3):
                    for k in range(4):
                        step(turn, k)

            def place(turn, k, offset=0):
                return turn * -4 + (EG - 1 - k + offset)

            with nc.Block() as block:
                @block.sync
                def _(sp):
                    def step(turn, k):
                        g = at(turn, k, 0)
                        if g.real:
                            cols = bass.ds(place(turn, k) * GROUP, GROUP)
                            need(sp, h_mean, g.n - 3)
                            need(sp, h_sum, g.n - 3)
                            need(sp, h_H, g.n - 3)
                            need(sp, h_T, g.n - 3)
                            sp.dma_start(more_h[:, k, :], more_dram[cols].unsqueeze(0).broadcast_to([P, GROUP])).then_inc(h_row[k], 16)
                            sp.dma_start(rcnt_h[:, k, :], rcnt_dram[cols].unsqueeze(0)
                                         .broadcast_to([P, GROUP])).then_inc(h_row[k], 16)
                            sp.dma_start(attr_h[:, k, :], attr_dram[:, cols]).then_inc(h_row[k], 16)
                            sp.dma_start(xl_r[:, k], reached_dram[cols, :].rearrange("(j p) f -> p j f", p=P)).then_inc(h_row[k], 16)
                    steps(sp, step)

                @block.gpsimd
                def _(pool):
                    pool.memset(B2["st"][:, :, :, :, :], 0.0).then_inc(h_zero, 1)

                    pool.memset(no_ix[:, :], 0).then_inc(h_zero, 1)
                    pool.wait_ge(h_zero, 2)
                    pool.tensor_copy(get_ix[:, 0, :], idx_src[:, (EG - 1) * QUAD:EG * QUAD]).then_inc(h_ix, 1)

                    def step(turn, k):
                        g, o, next_g, next_o = (at(turn, k, n) for n in (0, PUT, -1, PUT - 1))
                        if next_o.real:
                            cols = bass.ds(place(turn, k, PUT - 1) * QUAD, QUAD)
                            need(pool, h_put[next_o.slot], 64 * next_o.turn)
                            pool.tensor_copy(out_ix[:, next_o.slot, :], idx_first[:, cols]).then_inc(h_oix, 1)
                        if next_g.real:
                            cols = bass.ds(place(turn, k, -1) * QUAD, QUAD)
                        if g.real:
                            pool.wait_ge(h_ix, g.n + 1)
                            need(pool, h_T, g.n - 2)
                        if o.real:
                            pool.wait_ge(h_oix, o.n + 1)
                            pool.wait_ge(t_out, late(o).n + 1)
                        if next_g.real:
                            pool.tensor_tensor(get_ix[:, next_g.slot, :], idx_src[:, cols], no_ix[:, :], ALU.add).then_inc(h_ix, 1)
                        if g.real:
                            for j in range(QUAD):
                                pool.indirect_dma_start(
                                    xs_r[:, k, j, :], None, x1_dram[:, :],
                                    bass.IndirectOffsetOnAxis(ap=get_ix[:, k, j:j + 1], axis=0)).then_inc(h_got[k], 16)
                        if o.real:
                            for j in range(QUAD):
                                pool.indirect_dma_start(
                                    out[:, :], bass.IndirectOffsetOnAxis(ap=out_ix[:, o.slot, j:j + 1], axis=0),
                                    o_e[:, o.slot, j, :], None, bounds_check=N - 1, oob_is_err=False).then_inc(h_put[o.slot], 16)
                    steps(pool, step)
                    for slot in range(4):
                        pool.wait_ge(h_put[slot], 64 * ((EG + 3 - slot) // 4))

                @block.tensor
                def _(pe):
                    def step(turn, k):
                        g = at(turn, k, HID)
                        if g.real:
                            pe.wait_ge(h_xs, g.n + 1)
                            pe.wait_ge(h_xd, g.n + 1)
                            need(pe, h_msg, g.n)
                            pe.matmul(qH[:, :], w_m1s[:, :], xs_t[:, g.slot % 2, :], start=True, stop=False)
                            pe.matmul(qH[:, :], w_m1d[:, :], xd_t[:, g.slot, :], start=False, stop=False)
                            pe.matmul(qH[:, :], w_m1a[:, :], attr_h[:, g.slot, :], start=False, stop=True).then_inc(h_H, 1)
                        g = at(turn, k, ADDED)
                        if g.real:
                            x_of = xd_t[:, g.slot]
                            pe.wait_ge(h_up, g.n + 1)
                            pe.wait_ge(t_w, late(g).n)
                            pe.wait_ge(b_st[NORM2], late(g).n)
                            pe.matmul(qV[:, :], ones_b[:, :], along(u2b3), start=True, stop=False)
                            for j in range(QUAD):
                                pe.matmul(qV[:, j * F:(j + 1) * F], up_t[:, g.slot % 2, j * P:(j + 1) * P], w_u2[:, :],
                                          start=False, stop=False)
                                ins = pe.matmul(qV[:, j * F:(j + 1) * F], x_of[:, j * P:(j + 1) * P], ident[:, :],
                                                start=False, stop=(j == QUAD - 1))
                            ins.then_inc(h_V, 1)
                            need(pe, t_y, late(g).n - 1)
                            to = qR[g.slot % 2]
                            pe.matmul(to[:, :], ones_b[:, :], along(beta3), start=True, stop=False)
                            for j in range(QUAD):
                                ins = pe.matmul(to[:, j * F:(j + 1) * F], x_of[:, j * P:(j + 1) * P], ident[:, :],
                                                start=False, stop=(j == QUAD - 1))
                            ins.then_inc(h_R, 1)
                        g = at(turn, k, TURN)
                        if g.real:
                            pe.wait_ge(h_row[g.slot], 64 * (g.turn + 1))
                            need(pe, h_xd, g.n)
                            for j in range(QUAD):
                                pe.transpose(qD[:, j * P:(j + 1) * P], xl_r[:, g.slot, j, :], ident[:, :])
                            pe.wait_ge(h_got[g.slot], 64 * (g.turn + 1))
                            need(pe, h_xs, g.n)
                            for j in range(QUAD):
                                ins = pe.transpose(qS[:, j * P:(j + 1) * P], xs_r[:, g.slot, j, :], ident[:, :])
                            ins.then_inc(h_T, 1)
                        g = at(turn, k, MEAN)
                        if g.real:
                            pe.wait_ge(h_mean, g.n + 1)
                            need(pe, h_up, g.n)
                            pe.matmul(qU[:, :], w_u1x[:, :], xd_t[:, g.slot, :], start=True, stop=False)
                            pe.matmul(qU[:, :], w_u1m[:, :], mean_t[:, g.slot % 2, :], start=False, stop=True).then_inc(h_U, 1)
                    steps(pe, step)

                @block.scalar
                def _(act):
                    def step(turn, k):
                        n, slot, real = batch(turn, k, 1)
                        if real:
                            batch_root(act, n, slot, B2)
                        g = at(turn, k, HID)
                        if g.real:
                            act.wait_ge(h_H, g.n + 1)
                            need(act, h_sum, g.n - 1)
                            act.activation(msg_t[:, g.slot % 2, :], qH[:, :], ACT.Relu, bias=m1_bias[:, 0:1]).then_inc(h_msg, 1)
                        g = at(turn, k, WRITTEN)
                        if g.real:
                            need(act, h_put[g.slot], 64 * g.turn)
                            tail_out(act, late(g), slot, B2, o_e[:, g.slot])
                        g = at(turn, k, TURN)
                        if g.real:
                            act.wait_ge(h_T, g.n + 1)
                            need(act, h_H, g.n - 1)
                            act.copy(xs_t[:, g.slot % 2, :], qS[:, :]).then_inc(h_xs, 1)
                        g = at(turn, k, MEAN)
                        if g.real:
                            act.wait_ge(h_U, g.n + 1)
                            need(act, h_V, g.n - 1)
                            act.activation(up_t[:, g.slot % 2, :], qU[:, :], ACT.Relu, bias=u1m_bias[:, 0:1]).then_inc(h_up, 1)
                    steps(act, step)

                @block.vector
                def _(dve):
                    dve.wait_ge(h_zero, 1)

                    def spread(to, done, g, slots, factors, frm):
                        first = isinstance(g.n, int) and g.n == 0
                        if not first:
                            dve.wait_ge(done, g.n)
                        dve.tensor_tensor_scan(to[:, g.slot % slots, ::-1], factors[:, g.slot, ::-1], frm[:, ::-1],
                                               0.0 if first else to[:, (g.slot - 1) % slots, 0:1],
                                               ALU.mult, ALU.add).then_inc(done, 1)

                    def step(turn, k):
                        d, m, q, a, c, f = (at(turn, k, o) for o in (TURN, HID, MEAN, ADDED, SCALED, WRITTEN))
                        n, slot, real = batch(turn, k)
                        before, old, had = batch(turn, k, 1)
                        if q.real:
                            dve.wait_ge(h_sum, q.n + 1)
                            need(dve, h_U, q.n - 1)
                            dve.tensor_tensor(mean_t[:, q.slot % 2, :], sum_t[:, q.slot % 2, :], rcnt_h[:, q.slot, :],
                                              ALU.mult).then_inc(h_mean, 1)
                        if a.real:
                            a = late(a)
                            need(dve, t_out, a.n - 3)
                            dve.wait_ge(h_V, a.n - GROUPS + 1)
                            dve.tensor_tensor(B2["w"][:, a.slot], split(qV[:, :]), along(gamma_b), ALU.mult).then_inc(t_w, 1)
                        if had:
                            need(dve, t_out, before - BATCHES - 7 + GROUPS)
                            batch_inverse(dve, before, old, B2)
                        if a.real:
                            need(dve, b_half, 2 * n)
                            stats(dve, split(qV[:, :]), B2["st"][:, slot, NORM2]).then_inc(b_st[NORM2], 1)
                        if f.real:
                            tail_shift(dve, late(f), before, old, B2)
                        if d.real:
                            dve.wait_ge(h_T, d.n + 1)
                            need(dve, h_V, d.n - 3)
                            need(dve, h_R, d.n - 3)
                            spread(xd_t, h_xd, d, 4, more_h, qD)
                        if c.real:
                            tail_scale(dve, late(c), before, old, B2, split(qR[c.slot % 2][:, :]), h_R, c.n + 1)
                        if m.real:
                            dve.wait_ge(h_msg, m.n + 1)
                            need(dve, h_mean, m.n - 1)
                            spread(sum_t, h_sum, m, 2, more_h, msg_t[:, m.slot % 2, :])
                        if c.real:
                            dve.wait_ge(t_y, late(c).n + 1)
                            need(dve, b_half, 2 * n)
                            stats(dve, B2["w"][:, c.slot], B2["st"][:, slot, NORM3]).then_inc(b_st[NORM3], 1)
                        if real:
                            for norm, g in ((NORM2, a), (NORM3, c)):
                                if g.real:
                                    dve.wait_ge(b_st[norm], g.n + 1 + (GROUPS if g is c else 0))
                            batch_halves(dve, n, slot, B2)
                            batch_spread(dve, n, slot, B2)
                            batch_variance(dve, n, slot, B2)
                    steps(dve, step)


_INS = ['x', 'src', 'dst', 'edge_attr_2', 'edge_type_4', 'L0_gnn_W_rel', 'L0_gnn_att_src_rel', 'L0_gnn_att_dst_rel',
        'L0_gnn_bias_rel', 'L0_gnn_W_self', 'L0_gnn_W_cross', 'L0_gnn_att_src_lang', 'L0_gnn_att_dst_lang',
        'L0_gnn_bias_lang', 'L1_gnn_mW1', 'L1_gnn_mb1', 'L1_gnn_mW2', 'L1_gnn_mb2', 'L1_gnn_uW1', 'L1_gnn_ub1',
        'L1_gnn_uW2', 'L1_gnn_ub2', 'L1_gnn_gamma', 'L1_gnn_beta']


def kernel(**inputs):
    import numpy as _np
    import concourse.bacc as _bacc
    from concourse import mybir as _mybir
    from concourse.bass_utils import run_bass_kernel_spmd as _run

    nc = _bacc.Bacc("TRN2", target_bir_lowering=False, num_devices=1)
    arrays, args = {}, []
    for name in _INS:
        a = _np.ascontiguousarray(inputs[name])
        arrays[f"in_{name}_dram"] = a
        args.append(nc.dram_tensor(f"in_{name}_dram", a.shape, _mybir.dt.from_np(a.dtype), kind="ExternalInput").ap())
    x = arrays["in_x_dram"]
    args.append(nc.dram_tensor("out_0_dram", x.shape, _mybir.dt.from_np(x.dtype), kind="ExternalOutput").ap())
    build(nc, *args)
    r = _run(nc, [arrays], core_ids=[0])
    return r.results[0]["out_0_dram"]
```
